# Optimizing a Trainium2 kernel written in Bass

```python
import numpy as np
import jax
import jax.numpy as jnp

def _softmax(x, axis=-1):
    return jax.nn.softmax(x, axis=axis)

def _gelu(x):
    return jax.nn.gelu(x, approximate=True)

def _silu(x):
    return jax.nn.silu(x)

def _sigmoid(x):
    return jax.nn.sigmoid(x)

def _layernorm(x, axis=-1, eps=1e-05):
    m = jnp.mean(x, axis=axis, keepdims=True)
    v = jnp.var(x, axis=axis, keepdims=True)
    return (x - m) / jnp.sqrt(v + eps)

def _scatter_add(tgt, idx, src, axis=0):
    return tgt.at[idx].add(src)

def _segment_sum(src, seg, n):
    return jax.ops.segment_sum(src, seg, n)
kernel_name = 'mk_hybrid_d1_jaxref_r8_2bd4e3'

def setup_inputs(seed: int=0):
    np.random.seed(seed)
    _w = jnp.asarray

    def _L0_attn_a_setup():
        import jax, jax.numpy as jnp
        import numpy as np
        D = 256
        H = 32
        DH = D // H
        M = 4
        S = 64
        EPS = 1e-09
        ROPE_BASE = 10000.0

        def _rope(x, cos, sin):
            xp = x.reshape(x.shape[:-1] + (DH // 2, 2))
            xe, xo = (xp[..., 0], xp[..., 1])
            oe = xe * cos - xo * sin
            oo = xe * sin + xo * cos
            return jnp.stack((oe, oo), axis=-1).reshape(x.shape)

        def _masked_softmax(scores, valid):
            s = jnp.where(valid, scores, -jnp.inf)
            mx = jnp.max(s, axis=-1, keepdims=True)
            mx = jnp.where(jnp.isfinite(mx), mx, 0.0)
            e = jnp.exp(s - mx) * valid
            return e / jnp.maximum(jnp.sum(e, axis=-1, keepdims=True), EPS)

        def _split_heads(t):
            B, L, _ = t.shape
            return t.reshape(B, L, H, DH).transpose(0, 2, 1, 3)

        def _forward(x, w_qkv, b_qkv, pool_q, w_lm_qkv, b_lm_qkv, w_lm_out, b_lm_out, w_l2t_q, b_l2t_q, w_l2t_out, b_l2t_out, w_lm_kv, b_lm_kv, w_out, b_out, w_gate, b_gate):
            B, L, _ = x.shape
            Nb = L // S
            scale = DH ** (-0.5)
            q, k, v = jnp.split(x @ w_qkv + b_qkv, 3, axis=-1)
            q, k, v = map(_split_heads, (q, k, v))
            inv = 1.0 / ROPE_BASE ** (jnp.arange(0, DH, 2, dtype=jnp.float32) / DH)
            fr = jnp.arange(L, dtype=jnp.float32)[:, None] * inv[None, :]
            cos, sin = (jnp.cos(fr), jnp.sin(fr))
            q = _rope(q, cos, sin)
            k = _rope(k, cos, sin)
            qb = q.reshape(B, H, Nb, S, DH)
            kb = k.reshape(B, H, Nb, S, DH)
            vb = v.reshape(B, H, Nb, S, DH)
            sc = jnp.einsum('bhnqd,bhnkd->bhnqk', qb, kb) * scale
            causal = jnp.tril(jnp.ones((S, S), dtype=bool))
            out_local = jnp.einsum('bhnqk,bhnkd->bhnqd', _masked_softmax(sc, causal), vb)
            out_local = out_local.reshape(B, H, L, DH)
            pq = pool_q.reshape(M, H, DH).transpose(1, 0, 2)
            pa = jax.nn.softmax(jnp.einsum('hmd,bhnsd->bhnms', pq, kb) * scale, axis=-1)
            lm_h = jnp.einsum('bhnms,bhnsd->bhnmd', pa, vb)
            lmf = lm_h.transpose(0, 2, 3, 1, 4).reshape(B, Nb * M, D)
            NL = Nb * M
            lq, lk, lv = jnp.split(lmf @ w_lm_qkv + b_lm_qkv, 3, axis=-1)
            lq, lk, lv = map(_split_heads, (lq, lk, lv))
            blk = jnp.repeat(jnp.arange(Nb), M)
            lm_mask = blk[:, None] >= blk[None, :]
            la = _masked_softmax(jnp.einsum('bhqd,bhkd->bhqk', lq, lk) * scale, lm_mask)
            lo = jnp.einsum('bhqk,bhkd->bhqd', la, lv).transpose(0, 2, 1, 3).reshape(B, NL, D)
            lmf = lmf + lo @ w_lm_out + b_lm_out
            l2q = _split_heads(lmf @ w_l2t_q + b_l2t_q).reshape(B, H, Nb, M, DH)
            ra = jax.nn.softmax(jnp.einsum('bhnmd,bhnsd->bhnms', l2q, kb) * scale, axis=-1)
            ro = jnp.einsum('bhnms,bhnsd->bhnmd', ra, vb)
            ro = ro.transpose(0, 2, 3, 1, 4).reshape(B, NL, D)
            lmf = lmf + ro @ w_l2t_out + b_l2t_out
            gk, gv = jnp.split(lmf @ w_lm_kv + b_lm_kv, 2, axis=-1)
            gk, gv = map(_split_heads, (gk, gv))
            tok_blk = jnp.repeat(jnp.arange(Nb), S)
            g_mask = tok_blk[:, None] > blk[None, :]
            ga = _masked_softmax(jnp.einsum('bhqd,bhkd->bhqk', q, gk) * scale, g_mask)
            out_global = jnp.einsum('bhqk,bhkd->bhqd', ga, gv)
            gate = jax.nn.sigmoid(x @ w_gate + b_gate)
            gate = gate.transpose(0, 2, 1)[..., None]
            out = (1.0 - gate) * out_local + gate * out_global
            out = out.transpose(0, 2, 1, 3).reshape(B, L, D)
            return out @ w_out + b_out
        key = jax.random.key(seed)
        ks = jax.random.split(key, 12)
        s = D ** (-0.5)
        w = lambda k, shp: jax.random.normal(k, shp, jnp.float32) * s
        return {'x': jax.random.normal(ks[0], (2, 512, D), jnp.float32), 'w_qkv': w(ks[1], (D, 3 * D)), 'b_qkv': jnp.zeros((3 * D,), jnp.float32), 'pool_q': w(ks[2], (M, D)), 'w_lm_qkv': w(ks[3], (D, 3 * D)), 'b_lm_qkv': jnp.zeros((3 * D,), jnp.float32), 'w_lm_out': w(ks[4], (D, D)), 'b_lm_out': jnp.zeros((D,), jnp.float32), 'w_l2t_q': w(ks[5], (D, D)), 'b_l2t_q': jnp.zeros((D,), jnp.float32), 'w_l2t_out': w(ks[6], (D, D)), 'b_l2t_out': jnp.zeros((D,), jnp.float32), 'w_lm_kv': w(ks[7], (D, 2 * D)), 'b_lm_kv': jnp.zeros((2 * D,), jnp.float32), 'w_out': w(ks[8], (D, D)), 'b_out': jnp.zeros((D,), jnp.float32), 'w_gate': w(ks[9], (D, H)), 'b_gate': jnp.zeros((H,), jnp.float32)}
    _L0_attn_a_in = _L0_attn_a_setup()

    def _L0_attn_b_setup():
        import jax, jax.numpy as jnp
        import numpy as np
        HIDDEN = 256
        NUM_HEADS = 16
        NUM_KV_HEADS = 4
        HEAD_DIM = HIDDEN // NUM_HEADS
        Q_PER_KV = NUM_HEADS // NUM_KV_HEADS
        GROUP_SIZE = (Q_PER_KV + 2) * HEAD_DIM
        TOTAL_PROJ = NUM_KV_HEADS * GROUP_SIZE
        SEQ, BATCH = (256, 2)
        key = jax.random.key(seed)
        k1, k2, k3 = jax.random.split(key, 3)
        x = jax.random.normal(k1, (SEQ, BATCH, HIDDEN), dtype=jnp.float32)
        weight_qkv = jax.random.normal(k2, (TOTAL_PROJ, HIDDEN), dtype=jnp.float32) * 0.02
        weight_proj = jax.random.normal(k3, (HIDDEN, NUM_HEADS * HEAD_DIM), dtype=jnp.float32) * 0.02
        return {'x': x, 'weight_qkv': weight_qkv, 'weight_proj': weight_proj}
    _L0_attn_b_in = _L0_attn_b_setup()

    def _L0_ffn_setup():
        import jax, jax.numpy as jnp
        import numpy as np
        NUM_EXPERTS = 8
        TOP_K = 2
        HID = 256
        FF = 512
        B, S = (2, 128)
        SCALE = 0.02

        def _gated_mlp(x, w_gate, w_up, w_down):
            h = jax.nn.silu(x @ w_gate.T) * (x @ w_up.T)
            return h @ w_down.T
        key = jax.random.key(seed)
        ks = jax.random.split(key, 8)
        return {'hidden_states': jax.random.normal(ks[0], (B, S, HID), dtype=jnp.float32), 'wg': jax.random.normal(ks[1], (NUM_EXPERTS, HID), dtype=jnp.float32) * SCALE, 'sh_gate': jax.random.normal(ks[2], (FF, HID), dtype=jnp.float32) * SCALE, 'sh_up': jax.random.normal(ks[3], (FF, HID), dtype=jnp.float32) * SCALE, 'sh_down': jax.random.normal(ks[4], (HID, FF), dtype=jnp.float32) * SCALE, 'ex_gate': jax.random.normal(ks[5], (NUM_EXPERTS, FF, HID), dtype=jnp.float32) * SCALE, 'ex_up': jax.random.normal(ks[6], (NUM_EXPERTS, FF, HID), dtype=jnp.float32) * SCALE, 'ex_down': jax.random.normal(ks[7], (NUM_EXPERTS, HID, FF), dtype=jnp.float32) * SCALE}
    _L0_ffn_in = _L0_ffn_setup()
    _d = {'L0_attn_a_x': _L0_attn_a_in['x'], 'L0_attn_a_w_qkv': _L0_attn_a_in['w_qkv'], 'L0_attn_a_b_qkv': _L0_attn_a_in['b_qkv'], 'L0_attn_a_pool_q': _L0_attn_a_in['pool_q'], 'L0_attn_a_w_lm_qkv': _L0_attn_a_in['w_lm_qkv'], 'L0_attn_a_b_lm_qkv': _L0_attn_a_in['b_lm_qkv'], 'L0_attn_a_w_lm_out': _L0_attn_a_in['w_lm_out'], 'L0_attn_a_b_lm_out': _L0_attn_a_in['b_lm_out'], 'L0_attn_a_w_l2t_q': _L0_attn_a_in['w_l2t_q'], 'L0_attn_a_b_l2t_q': _L0_attn_a_in['b_l2t_q'], 'L0_attn_a_w_l2t_out': _L0_attn_a_in['w_l2t_out'], 'L0_attn_a_b_l2t_out': _L0_attn_a_in['b_l2t_out'], 'L0_attn_a_w_lm_kv': _L0_attn_a_in['w_lm_kv'], 'L0_attn_a_b_lm_kv': _L0_attn_a_in['b_lm_kv'], 'L0_attn_a_w_out': _L0_attn_a_in['w_out'], 'L0_attn_a_b_out': _L0_attn_a_in['b_out'], 'L0_attn_a_w_gate': _L0_attn_a_in['w_gate'], 'L0_attn_a_b_gate': _L0_attn_a_in['b_gate'], 'L0_attn_b_weight_qkv': _L0_attn_b_in['weight_qkv'], 'L0_attn_b_weight_proj': _L0_attn_b_in['weight_proj'], 'L0_ffn_wg': _L0_ffn_in['wg'], 'L0_ffn_sh_gate': _L0_ffn_in['sh_gate'], 'L0_ffn_sh_up': _L0_ffn_in['sh_up'], 'L0_ffn_sh_down': _L0_ffn_in['sh_down'], 'L0_ffn_ex_gate': _L0_ffn_in['ex_gate'], 'L0_ffn_ex_up': _L0_ffn_in['ex_up'], 'L0_ffn_ex_down': _L0_ffn_in['ex_down']}
    _x0 = _d['L0_attn_a_x']
    _d['L0_attn_a_x'] = jax.random.normal(jax.random.fold_in(jax.random.key(seed), 1), (4, 512, 256), dtype=_x0.dtype)
    del _x0
    return _d

def reference(L0_attn_a_x, L0_attn_a_w_qkv, L0_attn_a_b_qkv, L0_attn_a_pool_q, L0_attn_a_w_lm_qkv, L0_attn_a_b_lm_qkv, L0_attn_a_w_lm_out, L0_attn_a_b_lm_out, L0_attn_a_w_l2t_q, L0_attn_a_b_l2t_q, L0_attn_a_w_l2t_out, L0_attn_a_b_l2t_out, L0_attn_a_w_lm_kv, L0_attn_a_b_lm_kv, L0_attn_a_w_out, L0_attn_a_b_out, L0_attn_a_w_gate, L0_attn_a_b_gate, L0_attn_b_weight_qkv, L0_attn_b_weight_proj, L0_ffn_wg, L0_ffn_sh_gate, L0_ffn_sh_up, L0_ffn_sh_down, L0_ffn_ex_gate, L0_ffn_ex_up, L0_ffn_ex_down):

    def _L0_attn_a_ref(x, w_qkv, b_qkv, pool_q, w_lm_qkv, b_lm_qkv, w_lm_out, b_lm_out, w_l2t_q, b_l2t_q, w_l2t_out, b_l2t_out, w_lm_kv, b_lm_kv, w_out, b_out, w_gate, b_gate):
        import jax, jax.numpy as jnp
        import numpy as np
        D = 256
        H = 32
        DH = D // H
        M = 4
        S = 64
        EPS = 1e-09
        ROPE_BASE = 10000.0

        def _rope(x, cos, sin):
            xp = x.reshape(x.shape[:-1] + (DH // 2, 2))
            xe, xo = (xp[..., 0], xp[..., 1])
            oe = xe * cos - xo * sin
            oo = xe * sin + xo * cos
            return jnp.stack((oe, oo), axis=-1).reshape(x.shape)

        def _masked_softmax(scores, valid):
            s = jnp.where(valid, scores, -jnp.inf)
            mx = jnp.max(s, axis=-1, keepdims=True)
            mx = jnp.where(jnp.isfinite(mx), mx, 0.0)
            e = jnp.exp(s - mx) * valid
            return e / jnp.maximum(jnp.sum(e, axis=-1, keepdims=True), EPS)

        def _split_heads(t):
            B, L, _ = t.shape
            return t.reshape(B, L, H, DH).transpose(0, 2, 1, 3)

        def _forward(x, w_qkv, b_qkv, pool_q, w_lm_qkv, b_lm_qkv, w_lm_out, b_lm_out, w_l2t_q, b_l2t_q, w_l2t_out, b_l2t_out, w_lm_kv, b_lm_kv, w_out, b_out, w_gate, b_gate):
            B, L, _ = x.shape
            Nb = L // S
            scale = DH ** (-0.5)
            q, k, v = jnp.split(x @ w_qkv + b_qkv, 3, axis=-1)
            q, k, v = map(_split_heads, (q, k, v))
            inv = 1.0 / ROPE_BASE ** (jnp.arange(0, DH, 2, dtype=jnp.float32) / DH)
            fr = jnp.arange(L, dtype=jnp.float32)[:, None] * inv[None, :]
            cos, sin = (jnp.cos(fr), jnp.sin(fr))
            q = _rope(q, cos, sin)
            k = _rope(k, cos, sin)
            qb = q.reshape(B, H, Nb, S, DH)
            kb = k.reshape(B, H, Nb, S, DH)
            vb = v.reshape(B, H, Nb, S, DH)
            sc = jnp.einsum('bhnqd,bhnkd->bhnqk', qb, kb) * scale
            causal = jnp.tril(jnp.ones((S, S), dtype=bool))
            out_local = jnp.einsum('bhnqk,bhnkd->bhnqd', _masked_softmax(sc, causal), vb)
            out_local = out_local.reshape(B, H, L, DH)
            pq = pool_q.reshape(M, H, DH).transpose(1, 0, 2)
            pa = jax.nn.softmax(jnp.einsum('hmd,bhnsd->bhnms', pq, kb) * scale, axis=-1)
            lm_h = jnp.einsum('bhnms,bhnsd->bhnmd', pa, vb)
            lmf = lm_h.transpose(0, 2, 3, 1, 4).reshape(B, Nb * M, D)
            NL = Nb * M
            lq, lk, lv = jnp.split(lmf @ w_lm_qkv + b_lm_qkv, 3, axis=-1)
            lq, lk, lv = map(_split_heads, (lq, lk, lv))
            blk = jnp.repeat(jnp.arange(Nb), M)
            lm_mask = blk[:, None] >= blk[None, :]
            la = _masked_softmax(jnp.einsum('bhqd,bhkd->bhqk', lq, lk) * scale, lm_mask)
            lo = jnp.einsum('bhqk,bhkd->bhqd', la, lv).transpose(0, 2, 1, 3).reshape(B, NL, D)
            lmf = lmf + lo @ w_lm_out + b_lm_out
            l2q = _split_heads(lmf @ w_l2t_q + b_l2t_q).reshape(B, H, Nb, M, DH)
            ra = jax.nn.softmax(jnp.einsum('bhnmd,bhnsd->bhnms', l2q, kb) * scale, axis=-1)
            ro = jnp.einsum('bhnms,bhnsd->bhnmd', ra, vb)
            ro = ro.transpose(0, 2, 3, 1, 4).reshape(B, NL, D)
            lmf = lmf + ro @ w_l2t_out + b_l2t_out
            gk, gv = jnp.split(lmf @ w_lm_kv + b_lm_kv, 2, axis=-1)
            gk, gv = map(_split_heads, (gk, gv))
            tok_blk = jnp.repeat(jnp.arange(Nb), S)
            g_mask = tok_blk[:, None] > blk[None, :]
            ga = _masked_softmax(jnp.einsum('bhqd,bhkd->bhqk', q, gk) * scale, g_mask)
            out_global = jnp.einsum('bhqk,bhkd->bhqd', ga, gv)
            gate = jax.nn.sigmoid(x @ w_gate + b_gate)
            gate = gate.transpose(0, 2, 1)[..., None]
            out = (1.0 - gate) * out_local + gate * out_global
            out = out.transpose(0, 2, 1, 3).reshape(B, L, D)
            return out @ w_out + b_out
        return _forward(x, w_qkv, b_qkv, pool_q, w_lm_qkv, b_lm_qkv, w_lm_out, b_lm_out, w_l2t_q, b_l2t_q, w_l2t_out, b_l2t_out, w_lm_kv, b_lm_kv, w_out, b_out, w_gate, b_gate)

    def _L0_attn_b_ref(x, weight_qkv, weight_proj):
        import jax, jax.numpy as jnp
        import numpy as np
        HIDDEN = 256
        NUM_HEADS = 16
        NUM_KV_HEADS = 4
        HEAD_DIM = HIDDEN // NUM_HEADS
        Q_PER_KV = NUM_HEADS // NUM_KV_HEADS
        GROUP_SIZE = (Q_PER_KV + 2) * HEAD_DIM
        TOTAL_PROJ = NUM_KV_HEADS * GROUP_SIZE
        SEQ, BATCH = (256, 2)
        seq, batch, hidden = x.shape
        q_size = Q_PER_KV * HEAD_DIM
        qkv = x.reshape(-1, hidden) @ weight_qkv.T
        qkv = qkv.reshape(-1, NUM_KV_HEADS, GROUP_SIZE)
        q = qkv[:, :, :q_size].reshape(seq, batch, NUM_HEADS, HEAD_DIM)
        k = qkv[:, :, q_size:q_size + HEAD_DIM].reshape(seq, batch, NUM_KV_HEADS, HEAD_DIM)
        v = qkv[:, :, q_size + HEAD_DIM:].reshape(seq, batch, NUM_KV_HEADS, HEAD_DIM)
        k = jnp.repeat(k, Q_PER_KV, axis=2)
        v = jnp.repeat(v, Q_PER_KV, axis=2)
        q = q.transpose(1, 2, 0, 3)
        k = k.transpose(1, 2, 0, 3)
        v = v.transpose(1, 2, 0, 3)
        scale = 1.0 / np.sqrt(HEAD_DIM)
        scores = jnp.einsum('bhqd,bhkd->bhqk', q, k) * scale
        causal = jnp.tril(jnp.ones((seq, seq), dtype=bool))
        scores = jnp.where(causal, scores, jnp.float32(-jnp.inf))
        probs = jax.nn.softmax(scores, axis=-1)
        attn = jnp.einsum('bhqk,bhkd->bhqd', probs, v)
        attn = attn.transpose(2, 0, 1, 3).reshape(seq * batch, NUM_HEADS * HEAD_DIM)
        out = attn @ weight_proj.T
        return out.reshape(seq, batch, hidden)

    def _L0_ffn_ref(hidden_states, wg, sh_gate, sh_up, sh_down, ex_gate, ex_up, ex_down):
        import jax, jax.numpy as jnp
        import numpy as np
        NUM_EXPERTS = 8
        TOP_K = 2
        HID = 256
        FF = 512
        B, S = (2, 128)
        SCALE = 0.02

        def _gated_mlp(x, w_gate, w_up, w_down):
            h = jax.nn.silu(x @ w_gate.T) * (x @ w_up.T)
            return h @ w_down.T
        bsz, seq, dim = hidden_states.shape
        x = hidden_states.reshape(-1, dim)
        shared_out = _gated_mlp(x, sh_gate, sh_up, sh_down)
        logits = x.astype(jnp.float32) @ wg.T
        probs = jax.nn.softmax(logits, axis=-1)
        top_w, top_idx = jax.lax.top_k(probs, TOP_K)
        top_w = top_w / jnp.sum(top_w, axis=-1, keepdims=True)
        top_w = top_w.astype(hidden_states.dtype)
        comb = jnp.sum(jax.nn.one_hot(top_idx, NUM_EXPERTS, dtype=top_w.dtype) * top_w[..., None], axis=1)
        out = jnp.zeros_like(x)
        for e in range(NUM_EXPERTS):
            h = jax.nn.silu(x @ ex_gate[e].T) * (x @ ex_up[e].T)
            out = out + h @ ex_down[e].T * comb[:, e:e + 1]
        return (out + shared_out).reshape(bsz, seq, dim)
    x = L0_attn_a_x
    x = x + _L0_attn_a_ref(_layernorm(x, axis=-1), L0_attn_a_w_qkv, L0_attn_a_b_qkv, L0_attn_a_pool_q, L0_attn_a_w_lm_qkv, L0_attn_a_b_lm_qkv, L0_attn_a_w_lm_out, L0_attn_a_b_lm_out, L0_attn_a_w_l2t_q, L0_attn_a_b_l2t_q, L0_attn_a_w_l2t_out, L0_attn_a_b_l2t_out, L0_attn_a_w_lm_kv, L0_attn_a_b_lm_kv, L0_attn_a_w_out, L0_attn_a_b_out, L0_attn_a_w_gate, L0_attn_a_b_gate)
    x = x + _L0_ffn_ref(_layernorm(x, axis=-1), L0_ffn_wg, L0_ffn_sh_gate, L0_ffn_sh_up, L0_ffn_sh_down, L0_ffn_ex_gate, L0_ffn_ex_up, L0_ffn_ex_down)
    x = x + _L0_attn_b_ref(_layernorm(x, axis=-1), L0_attn_b_weight_qkv, L0_attn_b_weight_proj)
    x = x + _L0_ffn_ref(_layernorm(x, axis=-1), L0_ffn_wg, L0_ffn_sh_gate, L0_ffn_sh_up, L0_ffn_sh_down, L0_ffn_ex_gate, L0_ffn_ex_up, L0_ffn_ex_down)
    return x

_drawn_inputs = setup_inputs


def setup_inputs(seed=0):
    import zlib

    import numpy as np

    out = dict(_drawn_inputs(seed))
    spreads = {'L0_attn_a_b_qkv': (0.0, 0.1),
     'L0_attn_a_b_lm_qkv': (0.0, 0.1),
     'L0_attn_a_b_lm_out': (0.0, 0.1),
     'L0_attn_a_b_l2t_q': (0.0, 0.8),
     'L0_attn_a_b_l2t_out': (0.0, 0.1),
     'L0_attn_a_b_lm_kv': (0.0, 0.1),
     'L0_attn_a_b_out': (0.0, 0.1),
     'L0_attn_a_b_gate': (0.0, 0.742)}
    factors = {'L0_attn_a_pool_q': 8.0, 'L0_attn_a_w_l2t_q': 4.969}
    for name, (base, spread) in spreads.items():
        noise = np.random.default_rng([zlib.crc32(name.encode()), seed]).standard_normal(out[name].shape)
        drawn = base * np.exp(spread * noise) if base else spread * noise
        out[name] = jnp.asarray(drawn.astype(out[name].dtype))
    for name, factor in factors.items():
        out[name] = (out[name] * factor).astype(out[name].dtype)
    return out
```

```python
from contextlib import ExitStack

import numpy as np

import concourse.bass as bass
from concourse import mybir

F32 = mybir.dt.float32
BF16 = mybir.dt.bfloat16
I32 = mybir.dt.int32
U32 = mybir.dt.uint32
ALU = mybir.AluOpType
ACT = mybir.ActivationFunctionType
AX = mybir.AxisListType

P = 128
B, L, D = 4, 512, 256
T = L // P
NT = B * T
KC = D // P
LN_EPS = 1e-5

H, DH = 32, 8
S = 64
NB = L // S
M = 4
NL = NB * M
HC = P // DH
HQ = 4
C8 = H // HQ
SCALE = DH ** -0.5
NEG = -1e30
SUM_EPS = 1e-9
PARTS = 3 * HQ * DH
ROWS = PARTS + 2 * HQ

SEQ, BATCH = B, L
NH, NKV, HD = 16, 4, 16
GROUP = (NH // NKV + 2) * HD
QKVB = NKV * GROUP
SCALE_B = float(np.float32(1.0 / np.sqrt(HD)))

E, TOPK, FF = 8, 2, 512
NW = E + 1
FC = FF // P
ROUTED = (NT * P * TOPK - E) // P + E
TILES = NT + ROUTED
SLOTS = TILES * P
WCOL = KC * FF


def constants():
    p = np.arange(P)
    f = np.float32
    inv = (f(1.0) / f(10000.0) ** (np.arange(0, DH, 2, dtype=f) / f(DH))).astype(f)
    angle = np.arange(L, dtype=f)[None, :] * inv[(p % DH) // 2][:, None]
    sign = np.where(p % 2 == 0, f(-1), f(1))[:, None]
    tab = {"ident": np.eye(P), "cos": np.cos(angle), "sin": np.sin(angle) * sign}
    r = np.arange(PARTS)
    part, feat = r // (HQ * DH), r % (HQ * DH)
    for name, hi_parts in (("selk", (0, 1)), ("selq", (0, 2))):
        sel = np.zeros((P, 4, 2, PARTS))
        for a in range(4):
            is_hi = np.isin(part, hi_parts)
            sel[HQ * DH * a + feat, a, np.where(is_hi, 0, 1), r] = 1.0
        tab[name] = sel.reshape(P, -1)
    tab["headmask"] = np.where(p[:, None] < PARTS, (p[:, None] % (HQ * DH)) // DH == np.arange(HQ),
                               (p[:, None] - PARTS) // 2 == np.arange(HQ)) * 1.0
    k = np.arange(S)
    tab["causal"] = np.where(k[None, :] > (p % S)[:, None], NEG, 0.0)
    tab["causalT"] = np.where((p % S)[:, None] > k[None, :], NEG, 0.0)
    tab["bd16"] = (p[:, None] // DH == np.arange(HC)) * 1.0
    lm = np.arange(NL)
    la = np.zeros((P, NL))
    la[:NL] = np.where((lm // M)[:, None] < (lm // M)[None, :], NEG, 0.0)
    tab["lamask"] = la
    selg = np.zeros((P, C8, HQ, NL))
    for h in range(H):
        selg[h, h // HQ, h % HQ] = 1.0
        selg[H + h, h // HQ, h % HQ] = 1.0
    below = np.where(np.arange(NB)[:, None] > (lm // M)[None, :], 0.0, NEG)
    selg[2 * H:2 * H + NB] = below[:, None, None, :]
    tab["selg"] = selg.reshape(P, -1)
    oh = np.zeros((P, L))
    oh[2 * H:2 * H + NB] = np.arange(L)[None, :] // S == np.arange(NB)[:, None]
    oh[0:NB] = oh[2 * H:2 * H + NB]
    tab["onehot"] = oh
    gm = np.zeros((P, NL))
    gm[0:NB] = below
    tab["gmask"] = gm
    tab["valid"] = (p[:, None] >= S) * 1.0
    tab["tri"] = (p[:, None] < p[None, :]) * 1.0
    tab["ones"] = np.ones((P, P))
    tab["iota8"] = np.broadcast_to(np.arange(E), (P, E))
    e = np.arange(E)
    tab["tri8"] = np.broadcast_to((e[None, :] < e[:, None]).reshape(1, E * E) * 1.0, (P, E * E))
    tab["tilestart"] = np.broadcast_to(np.arange(ROUTED) * float(P), (P, ROUTED))
    def pack(names):
        at, off = {}, 0
        for name in names:
            at[name] = (off, tab[name].shape[1])
            off += tab[name].shape[1]
        return np.ascontiguousarray(np.concatenate([tab[n] for n in names], 1, dtype=np.float64).astype(f)), at

    return pack([n for n in tab if n not in CAST]), pack(CAST)


CAST = ("selk", "selq", "causal", "causalT", "selg", "onehot", "gmask")
(CONST, CONST_AT), (TABLE, TABLE_AT) = constants()

W_COLS = {"k": (0, 256), "ks": (256, 256), "q": (512, 256), "qs": (768, 256), "v": (1024, 256),
          "gate": (1280, 32), "lm": (1312, 768), "lm_out": (2080, 256), "l2t_q": (2336, 256),
          "l2t_out": (2592, 256), "lm_kv": (2848, 512), "out": (3360, 256)}
W_TOTAL = 3616
B_COLS = {"k": 0, "ks": 2, "q": 4, "qs": 6, "lq": 8, "lk": 10, "lm_out": 12, "l2t_q": 14, "l2t_out": 16, "gk": 18}
B_TOTAL = 20
R_COLS = {"v": (0, 256), "gate": (256, 32), "lv": (288, 256), "gv": (544, 256), "out": (800, 256)}
R_TOTAL = 1056


def build(nc, x_d, const_d, table_d, wa_d, pq_d, ba_d, ra_d, wb_d, pb_d, wg_d, we_d, out_d):
    with ExitStack() as ctx:
        x = ctx.enter_context(nc.sbuf_tensor("x", [P, NT, D], F32))
        cst = ctx.enter_context(nc.sbuf_tensor("cst", [P, CONST.shape[1]], F32))
        mean = ctx.enter_context(nc.sbuf_tensor("mean", [P, NT], F32))
        rstd = ctx.enter_context(nc.sbuf_tensor("rstd", [P, NT], F32))
        slots_x = nc.dram_tensor("slots_x", (SLOTS, D), F32, kind="Internal").ap()
        slots_y = nc.dram_tensor("slots_y", (SLOTS, D), F32, kind="Internal").ap()
        banks = [ctx.enter_context(nc.psum_tensor(f"bank{i}", [P, 512], F32)) for i in range(8)]
        attention_a(nc, x, cst, mean, rstd, banks, x_d, const_d, table_d, wa_d, pq_d, ba_d, ra_d, slots_x)
        experts_and_attention_b(nc, x, cst, mean, rstd, banks, wb_d, pb_d, wg_d, we_d, slots_x, slots_y, out_d)


def const(cst, name, rows=slice(0, P)):
    off, n = CONST_AT[name]
    return cst[rows, off:off + n]


def table(stage, name, rows=slice(0, P)):
    off, n = TABLE_AT[name]
    return stage[rows, off:off + n]


def attention_a(nc, x, cst, mean, rstd, bank, x_d, const_d, table_d, wa_d, pq_d, ba_d, ra_d, slots_x):
    with ExitStack() as ctx:
        def sb(name, shape, dt=F32):
            return ctx.enter_context(nc.sbuf_tensor(name, shape, dt))

        def sem(name):
            return ctx.enter_context(nc.semaphore(name))

        w = sb("wa", [P, KC, W_TOTAL])
        pq = sb("pq", [P, KC, HC * M])
        ba = sb("ba", [P, B_TOTAL])
        rb = sb("ra", [P, R_TOTAL])
        identb = sb("identb", [P, P], BF16)
        selk = sb("selk", [P, 4, 2, PARTS], BF16)
        selq = sb("selq", [P, 4, 2, PARTS], BF16)
        causal = sb("causal", [P, 8, S], BF16)
        causal_t = sb("causal_t", [P, 8, S], BF16)
        selg = sb("selg", [P, C8, P], BF16)
        onehot = sb("onehot", [NB, L], BF16)
        gmask = sb("gmask", [NB, HC, NL], BF16)
        zero = sb("zero", [P, D])
        st6 = sb("st6", [P, NT, 6])
        mv = sb("mv", [P, NT, 2])
        newton = sb("newton", [P, 2, NT])

        xn = sb("xn", [P, T, D])
        xnT = sb("xnT", [P, KC, L])
        rope_ab = sb("rope_ab", [P, 4, L])
        rope_a, rope_b = rope_ab[:, 0:2, :], rope_ab[:, 2:4, :]
        kqT = sb("kqT", [P, 4, L])
        hi = sb("hi", [P, 4, L], BF16)
        lo = sb("lo", [P, 4, L], BF16)
        ks = sb("ks", [P, C8, L], BF16)
        qs = sb("qs", [P, C8, L], BF16)
        kd = sb("kd", [P, 2, C8, HQ, P], BF16)
        qd = sb("qd", [P, C8, HQ, P], BF16)
        v = sb("v", [P, T, D])
        vd = sb("vd", [P, T, H, 32])
        gate = sb("gate", [P, 3, T * H])
        nm = sb("nm", [P, 2, H])
        nmh = sb("nmh", [P, 2, H, 2], BF16)
        pt = sb("pt", [P, 2, 8, S])
        r_sb = sb("r_sb", [P, C8, S])
        rec = sb("rec", [S, 2, 16])
        ol = sb("ol", [P, T, D])
        a_s = sb("a_s", [P, L])
        a_stat = sb("a_stat", [P, 4, NB])
        a_pt = sb("a_pt", [P, T, 2, P])
        a_m = sb("a_m", [P, NL, HC])
        lmT = sb("lmT", [P, 8, KC, NL])
        lmf, lq, lk, lo_T, lmf2, l2q, roT, lmf3 = range(8)
        gkT = sb("gkT", [P, KC, NL])
        lv = sb("lv", [NL, D])
        gv = sb("gv", [NL, D])
        lkbd = sb("lkbd", [P, KC, HC, NL])
        lvd = sb("lvd", [P, C8, 32])
        le = sb("le", [NL, H, NL])
        lstat = sb("lstat", [NL, 3, H])
        lpt = sb("lpt", [P, C8, NL])
        l2qbd = lkbd[:, :, :, :].rearrange("p c h k -> p c (h k)").rearrange("p c (n j) -> p c n j", n=NB)
        gkbd = lkbd
        gvd = sb("gvd", [P, C8, 64])
        gnm = sb("gnm", [P, T, H])
        mm_ = sb("mm_", [P, L], BF16)
        pg = pt
        rg = rope_ab
        grec = sb("grec", [P, 2, H])
        og = xn
        oT = sb("oT", [P, 2, KC, P])

        stage = kd[:, :, :, :, :].rearrange("p a b c d -> p (a b c d)").bitcast(F32)
        d_w, d_x, x_in = sem("d_w"), [sem(f"d_x{i}") for i in range(B)], sem("x_in")
        c_ones, c_cast, c_stats, c_var, c_std = sem("c_ones"), sem("c_cast"), sem("c_stats"), sem("c_var"), sem("c_std")
        c_zero = sem("c_zero")
        c_rstd, batch_open = sem("c_rstd"), sem("batch_open")
        (xn_ready, xn_t, xnT_ready, proj, rope_mul, rope, hi_ready, lo_ready, v_ps, v_ready, vd_ready, gate_ps,
         gate_z, gate_e, gate_ready, stack_ps, stack, xb) = [sem(n) for n in (
             "xn_ready xn_t xnT_ready proj rope_mul rope hi_ready lo_ready v_ps v_ready vd_ready gate_ps "
             "gate_z gate_e gate_ready stack_ps stack xb").split()]
        (kd_ready, s_ps, smax, nmh_ready, nm_t, nm_row, qd_ready, st_ps, exps, pv, r_ready, r_t, rec_ready,
         ol_ready) = [sem(n) for n in (
             "kd_ready s_ps smax nmh_ready nm_t nm_row qd_ready st_ps exps pv r_ready r_t rec_ready "
             "ol_ready").split()]
        (at_s, at_sub, at_e, at_p, at_t, at_pt, at_o, at_red, lm_ps, lkbd_ready, lvd_ready, la_s, la_sub, la_e,
         la_p, la_t, la_pt, la_o, lo_ready_, lin_ps, lin_ready, gkbd_ready, gvd_ready) = [sem(n) for n in (
             "at_s at_sub at_e at_p at_t at_pt at_o at_red lm_ps lkbd_ready lvd_ready la_s la_sub la_e "
             "la_p la_t la_pt la_o lo_T_ready lin_ps lin_ready gkbd_ready gvd_ready").split()]
        (sg, gmax, gm_t, mm_hi, mm_lo, sgt, gexp, gpv, rg_ready, rg_t, og_ready, o_ready, o_t, oT_ready, y_ps,
         x_new) = [sem(n) for n in (
             "sg gmax gm_t mm_hi mm_lo sgt gexp gpv rg_ready rg_t og_ready o_ready o_t oT_ready y_ps "
             "x_new").split()]
        dve_step, pool_step = sem("dve_step"), sem("pool_step")

        ident = const(cst, "ident")
        bank5b = bank[5][:, :].bitcast(BF16)
        block = ctx.enter_context(nc.Block())

        def wcol(name, k, lo_=0, n=None):
            off, full = W_COLS[name]
            return w[:, k, off + lo_:off + lo_ + (full if n is None else n)]

        def bcol(name, c):
            return ba[:, B_COLS[name] + c:B_COLS[name] + c + 1]

        def row(name, rows=slice(0, P)):
            off, n = R_COLS[name]
            return rb[rows, off:off + n]

        @block.sync
        def _(sp):
            xv = x_d.rearrange("b (t p) d -> b p t d", p=P)
            for b in range(B):
                sp.dma_start(x[:, b * T:(b + 1) * T, :], xv[b]).then_inc(d_x[b], 16)
                if b == 0:
                    sp.dma_start(cst[:, :], const_d).then_inc(d_w, 16)
                    sp.dma_start(stage[:, 0:TABLE.shape[1]], table_d).then_inc(d_w, 16)
                    sp.dma_start(rb[:, :], ra_d).then_inc(d_w, 16)
                    sp.dma_start(ba[:, :], ba_d).then_inc(d_w, 16)
                    sp.dma_start(pq[:, :, :], pq_d).then_inc(d_w, 16)
                    sp.dma_start(w[:, :, :], wa_d).then_inc(d_w, 16)
            sp.wait_ge(c_zero, 1)
            sp.dma_start(slots_x[NT * P:SLOTS, :].rearrange("(j p) d -> p j d", p=P),
                         zero[:, :].unsqueeze(1).broadcast_to([P, ROUTED, D])).then_inc(x_in, 16)
            sp.wait_ge(x_in, 16)

        @block.gpsimd
        def _(pool):
            pool.memset(zero[:, :], 0.0).then_inc(c_zero, 1)
            n = 0
            for buf in (vd[:, :, :, :], a_pt[:, :, :, :], lvd[:, :, :], gvd[:, :, :]):
                pool.memset(buf, 0.0).then_inc(c_ones, 1)
                n += 1
            pool.wait_ge(d_w, 96)
            with pool.Fori(0, B) as b:
                pool.wait_ge(batch_open, b + 1)
                for t in range(T):
                    pool.wait_ge(xn_ready, b * T + t + 1)
                    pool.tensor_tensor(x[:, b * T + t, :], x[:, b * T + t, :], row("out"), ALU.add).then_inc(xb, 1)
                for r in range(4):
                    pool.wait_ge(rope_mul, b * 8 + 2 * r + 2)
                    pool.tensor_tensor(kqT[:, r, :], rope_a[:, r % 2, :], rope_b[:, r % 2, :],
                                       ALU.add).then_inc(rope, 1)
                for r in range(4):
                    pool.wait_ge(hi_ready, b * 4 + r + 1)
                    pool.tensor_tensor(lo[:, r, :], kqT[:, r, :], hi[:, r, :], ALU.subtract).then_inc(lo_ready, 1)
                pool.wait_ge(gate_ready, b + 1)
                for t in range(T):
                    pool.wait_ge(og_ready, b * T + t + 1)
                    pool.wait_ge(ol_ready, b * 16 + 4 * t + 4)
                    pool.tensor_tensor(og[:, t, :], og[:, t, :], ol[:, t, :], ALU.subtract).then_inc(pool_step, 1)
                    pool.wait_ge(pool_step, b * 2 * T + 2 * t + 1)
                    ogv = og[:, t, :].rearrange("p (h d) -> p h d", d=DH)
                    g = gate[:, 2, t * H:(t + 1) * H].unsqueeze(2).broadcast_to([P, H, DH])
                    pool.tensor_tensor(ogv, ogv, g, ALU.mult).then_inc(pool_step, 1)
                    pool.wait_ge(pool_step, b * 2 * T + 2 * t + 2)
                    pool.tensor_tensor(ol[:, t, :], ol[:, t, :], og[:, t, :], ALU.add).then_inc(o_ready, 1)

        @block.scalar
        def _(act):
            act.wait_ge(d_w, 96)
            act.activation(identb[:, :], ident, ACT.Copy).then_inc(c_cast, 1)
            for dst, name in ((selk, "selk"), (selq, "selq")):
                act.activation(dst[:, :, :, :].rearrange("p a b c -> p (a b c)"), table(stage, name),
                               ACT.Copy).then_inc(c_cast, 1)
            for dst, name in ((causal, "causal"), (causal_t, "causalT")):
                act.activation(dst[:, :, :], table(stage, name).unsqueeze(1).broadcast_to([P, 8, S]),
                               ACT.Copy).then_inc(c_cast, 1)
            act.activation(selg[:, :, :].rearrange("p a b -> p (a b)"), table(stage, "selg"), ACT.Copy).then_inc(c_cast, 1)
            act.activation(onehot[:, :], table(stage, "onehot", slice(0, NB)), ACT.Copy).then_inc(c_cast, 1)
            act.activation(gmask[:, :, :], table(stage, "gmask", slice(0, NB)).unsqueeze(1).broadcast_to([NB, HC, NL]),
                           ACT.Copy).then_inc(c_cast, 1)
            act.activation(mm_[2 * H:2 * H + NB, :], table(stage, "onehot", slice(2 * H, 2 * H + NB)),
                           ACT.Copy).then_inc(c_cast, 1)
            act.wait_ge(c_var, 1)
            act.activation(newton[:, 0, :], newton[:, 0, :], ACT.Sqrt).then_inc(c_std, 1)
            with act.Fori(0, B) as b:
                act.wait_ge(batch_open, b + 1)
                for p in range(2):
                    act.wait_ge(xn_t, b * T + 2 * p + 2)
                    act.activation(xnT[:, :, 2 * p * P:(2 * p + 2) * P].rearrange("p k (t c) -> p t k c", t=2),
                                   bank[5 + p][:, :].rearrange("p (t k c) -> p t k c", t=2, k=KC),
                                   ACT.Copy).then_inc(xnT_ready, 1)
                for r in range(4):
                    act.wait_ge(rope, b * 4 + r + 1)
                    act.activation(hi[:, r, :], kqT[:, r, :], ACT.Copy).then_inc(hi_ready, 1)
                for t in range(T):
                    act.wait_ge(v_ready, b * T + t + 1)
                    vv = v[:, t, :].rearrange("p (h d) -> p h d", d=DH)
                    for blk in range(2):
                        rows = slice(S * blk, S * blk + S)
                        act.activation(vd[rows, t, :, 16 * blk:16 * blk + DH], vv[rows], ACT.Copy).then_inc(vd_ready, 1)
                act.wait_ge(gate_z, b + 1)
                act.activation(gate[:, 1, :], gate[:, 0, :], ACT.Exp, scale=-1.0).then_inc(gate_e, 1)
                for s in range(16):
                    act.wait_ge(stack_ps, b * 16 + s + 1)
                    dst = ks if s < 8 else qs
                    act.activation(dst[0:PARTS, s % 8, :], bank[s % 4][0:PARTS, :], ACT.Copy).then_inc(stack, 1)

                def attend_exp(a):
                    act.wait_ge(at_sub, b * 2 + a + 1)
                    act.activation(a_s[:, :], a_s[:, :], ACT.Exp, scale=SCALE).then_inc(at_e, 1)

                def attend_turned(a):
                    act.wait_ge(at_t, b * 2 + a + 1)
                    for blk in range(2):
                        rows = slice(S * blk, S * blk + S)
                        act.activation(a_pt[rows, :, blk, :],
                                       bank[7][rows, :].rearrange("p (t c) -> p t c", t=T),
                                       ACT.Copy).then_inc(at_pt, 1)

                def la_exp():
                    act.wait_ge(la_sub, b * 2 + 2)
                    act.activation(le[:, :, :], le[:, :, :], ACT.Exp, scale=SCALE).then_inc(la_e, 1)

                def la_turned():
                    act.wait_ge(la_t, b + 1)
                    act.activation(lpt[:, :, :].rearrange("p c q -> p (c q)"), bank[7][:, 0:C8 * NL],
                                   ACT.Copy).then_inc(la_pt, 1)

                def la_out():
                    act.wait_ge(la_o, b + 1)
                    act.activation(lmT[:, lo_T, :, :].rearrange("p c q -> p (c q)"), bank[7][:, 0:KC * NL],
                                   ACT.Copy).then_inc(lo_ready_, 1)

                def exp_unit(t, g):
                    u = 4 * t + g
                    act.wait_ge(st_ps, b * 16 + u + 1)
                    if u >= 2:
                        act.wait_ge(pv, b * 16 + u - 1)
                    act.activation(pt[:, g % 2, :, :].rearrange("p h q -> p (h q)"), bank[2 + g % 2][:, :],
                                   ACT.Exp, scale=SCALE).then_inc(exps, 1)

                def weighted_out(t):
                    act.wait_ge(pv, b * 16 + 4 * t + 4)
                    if t >= 1:
                        act.wait_ge(r_t, b * 8 + 2 * t)
                    act.activation(r_sb[:, :, :].rearrange("p c q -> p (c q)"), bank[4][:, :],
                                   ACT.Copy).then_inc(r_ready, 1)

                landmarks = {1: lambda: attend_turned(0), 6: la_exp, 8: la_turned, 9: la_out,
                             12: lambda: attend_exp(1), 14: lambda: attend_turned(1)}
                attend_exp(0)
                for t in range(T):
                    act.wait_ge(nm_t, b * T + t + 1)
                    act.activation(qs[PARTS:ROWS, :, t * P:(t + 1) * P],
                                   bank5b[0:2 * HQ, :].rearrange("p (c q) -> p c q", c=C8),
                                   ACT.Copy).then_inc(nm_row, 1)
                    if t >= 1:
                        weighted_out(t - 1)
                    for g in range(4):
                        exp_unit(t, g)
                        if 4 * t + g in landmarks:
                            landmarks[4 * t + g]()
                weighted_out(T - 1)
                act.wait_ge(gm_t, b + 1)
                act.activation(mm_[0:H, :], bank[4][0:H, :], ACT.Copy).then_inc(mm_hi, 1)
                for c in range(C8):
                    act.wait_ge(sgt, b * C8 + c + 1)
                    if c >= 2:
                        act.wait_ge(gpv, b * C8 + c - 1)
                    act.activation(pg[:, c % 2, :, :].rearrange("p h q -> p (h q)"), bank[c % 4][:, :],
                                   ACT.Exp, scale=SCALE).then_inc(gexp, 1)
                for j in range(4):
                    act.wait_ge(gpv, b * C8 + 2 * j + 2)
                    act.activation(rg[:, j, :], bank[4 + j][:, :], ACT.Copy).then_inc(rg_ready, 1)
                for t in range(T):
                    act.wait_ge(o_t, b * T + t + 1)
                    if t >= 2:
                        act.wait_ge(y_ps, b * T + t - 1)
                    act.activation(oT[:, t % 2, :, :].rearrange("p k c -> p (k c)"), bank[4 + t][:, 0:KC * P],
                                   ACT.Copy).then_inc(oT_ready, 1)

        @block.vector
        def _(dve):
            def link(ins, b, per, n):
                ins.then_inc(dve_step, 1)
                dve.wait_ge(dve_step, b * per + n)

            dve.wait_ge(c_ones, 4)
            dve.memset(vd[0:S, :, :, 8:9], 1.0).then_inc(c_ones, 1)
            dve.memset(vd[S:P, :, :, 24:25], 1.0).then_inc(c_ones, 1)
            for i in range(HQ):
                dve.memset(gvd[32 * i:32 * i + 32, :, 32 + i:33 + i], 1.0).then_inc(c_ones, 1)
            dve.memset(ks[PARTS:P, :, :], 1.0).then_inc(c_ones, 1)
            for b in range(B):
                dve.wait_ge(d_x[b], 16)
                for t in range(b * T, (b + 1) * T):
                    dve.bn_stats(st6[:, t, :], x[:, t, :]).then_inc(c_stats, 1)
            for t in range(NT):
                dve.wait_ge(c_stats, t + 1)
                dve.bn_aggr(mv[:, t, :], st6[:, t, :]).then_inc(c_stats, 1)
            dve.wait_ge(c_stats, 2 * NT)
            dve.tensor_copy(mean[:, :], mv[:, :, 0]).then_inc(c_rstd, 1)
            dve.tensor_scalar(newton[:, 0, :], mv[:, :, 1], LN_EPS, None, ALU.add).then_inc(c_var, 1)
            dve.wait_ge(c_std, 1)
            dve.reciprocal(rstd[:, :], newton[:, 0, :]).then_inc(c_rstd, 1)
            dve.wait_ge(c_rstd, 2)
            dve.wait_ge(c_ones, 11)
            dve.wait_ge(c_cast, 9)
            dve.memset(newton[:, 1, 0:1], 0.0).then_inc(batch_open, 1)
            with dve.Fori(0, B) as b:
                count = [0]
                PER = DVE_LINKS_A

                def step(ins):
                    count[0] += 1
                    link(ins, b, PER, count[0])

                dve.wait_ge(batch_open, b + 1)
                for t in range(T):
                    dve.tensor_scalar(xn[:, t, :], x[:, b * T + t, :], mean[:, bass.ds(b * T + t, 1)],
                                      rstd[:, bass.ds(b * T + t, 1)], ALU.subtract, ALU.mult).then_inc(xn_ready, 1)
                for r, (name, c) in enumerate((("k", 0), ("k", 1), ("q", 0), ("q", 1))):
                    if r >= 2:
                        dve.wait_ge(rope, b * 4 + r - 1)
                    dve.wait_ge(proj, b * 8 + 2 * r + 1)
                    dve.scalar_tensor_tensor(rope_a[:, r % 2, :], bank[(2 * r) % 4][:, :], bcol(name, c),
                                             const(cst, "cos"), ALU.add, ALU.mult).then_inc(rope_mul, 1)
                    dve.wait_ge(proj, b * 8 + 2 * r + 2)
                    dve.scalar_tensor_tensor(rope_b[:, r % 2, :], bank[(2 * r + 1) % 4][:, :], bcol(name + "s", c),
                                             const(cst, "sin"), ALU.add, ALU.mult).then_inc(rope_mul, 1)
                for t in range(T):
                    dve.wait_ge(v_ps, b * T + t + 1)
                    dve.tensor_tensor(v[:, t, :], bank[6 + t % 2][:, 0:D], row("v"), ALU.add).then_inc(v_ready, 1)
                dve.wait_ge(gate_ps, b + 1)
                dve.tensor_tensor(gate[:, 0, :].rearrange("p (t h) -> p t h", t=T),
                                  bank[5][:, 0:T * H].rearrange("p (t h) -> p t h", t=T),
                                  row("gate").unsqueeze(1).broadcast_to([P, T, H]), ALU.add).then_inc(gate_z, 1)
                dve.wait_ge(gate_e, b + 1)
                step(dve.tensor_scalar(gate[:, 0, :], gate[:, 1, :], 1.0, None, ALU.add))
                dve.reciprocal(gate[:, 2, :], gate[:, 0, :]).then_inc(gate_ready, 1)

                bd = const(cst, "bd16")
                hm = const(cst, "headmask")

                sv = bank[7][:, :].rearrange("p (n s) -> p n s", n=NB)
                av = a_s[:, :].rearrange("p (n s) -> p n s", n=NB)

                def attend_max(a):
                    dve.wait_ge(at_s, b * 2 + a + 1)
                    step(dve.tensor_reduce(a_stat[:, 0, :], sv, AX.X, ALU.max))
                    dve.tensor_tensor(av, sv, a_stat[:, 0, :].unsqueeze(2).broadcast_to([P, NB, S]),
                                      ALU.subtract).then_inc(at_sub, 1)

                def attend_norm(a):
                    dve.wait_ge(at_e, b * 2 + a + 1)
                    step(dve.tensor_reduce(a_stat[:, 1, :], av, AX.X, ALU.add))
                    step(dve.reciprocal(a_stat[:, 2, :], a_stat[:, 1, :]))
                    dve.tensor_tensor(av, av, a_stat[:, 2, :].unsqueeze(2).broadcast_to([P, NB, S]),
                                      ALU.mult).then_inc(at_p, 1)

                def attend_out(a, dst, c):
                    dve.wait_ge(at_o, b * 4 + a * 2 + c + 1)
                    step(dve.tensor_tensor(
                        a_m[:, :, :].rearrange("p (n m) h -> p n h m", n=NB),
                        bank[7][:, :].rearrange("p (n h m) -> p n h m", n=NB, h=HC),
                        bd.unsqueeze(1).unsqueeze(3).broadcast_to([P, NB, HC, M]), ALU.mult))
                    dve.tensor_reduce(lmT[:, dst, c, :], a_m[:, :, :], AX.X, ALU.add).then_inc(at_red, 1)

                def spread(dst, src, value, signal):
                    for i in range(HQ):
                        dve.tensor_copy(dst[32 * i:32 * i + 32, :, DH * i:DH * i + DH],
                                        src[:, :].rearrange("k (c i d) -> k c i d", i=HQ, d=DH)[:, :, i, :])\
                           .then_inc(signal, 1)

                def block_diagonal(dst, src, signal):
                    for c in range(KC):
                        dve.tensor_tensor(dst[:, c, :, :], src[c].unsqueeze(1).broadcast_to([P, HC, NL]),
                                          bd.unsqueeze(2).broadcast_to([P, HC, NL]), ALU.mult).then_inc(signal, 1)

                def landmarks_qkv():
                    dve.wait_ge(lm_ps, b * 2 + 1)
                    for c in range(KC):
                        dve.tensor_scalar(lmT[:, lq, c, :], bank[7][:, c * NL:(c + 1) * NL], bcol("lq", c), None,
                                          ALU.add).then_inc(lkbd_ready, 1)
                    for c in range(KC):
                        dve.tensor_scalar(lmT[:, lk, c, :], bank[7][:, (2 + c) * NL:(3 + c) * NL], bcol("lk", c), None,
                                          ALU.add).then_inc(lkbd_ready, 1)
                    step(dve.tensor_tensor(lv[:, :], bank[7][0:NL, P:P + D], row("lv", slice(0, NL)), ALU.add))
                    block_diagonal(lkbd, [lmT[:, lk, c, :] for c in range(KC)], lkbd_ready)
                    spread(lvd, lv, None, lvd_ready)

                def la_max(c):
                    dve.wait_ge(la_s, b * 2 + c + 1)
                    lsv = bank[7][0:NL, :].rearrange("q (h k) -> q h k", h=HC)
                    step(dve.tensor_reduce(lstat[:, 0, HC * c:HC * c + HC], lsv, AX.X, ALU.max))
                    dve.tensor_tensor(le[:, HC * c:HC * c + HC, :], lsv,
                                      lstat[:, 0, HC * c:HC * c + HC].unsqueeze(2).broadcast_to([NL, HC, NL]),
                                      ALU.subtract).then_inc(la_sub, 1)

                def la_norm():
                    dve.wait_ge(la_e, b + 1)
                    step(dve.tensor_reduce(lstat[:, 1, :], le[:, :, :], AX.X, ALU.add))
                    step(dve.reciprocal(lstat[:, 2, :], lstat[:, 1, :]))
                    dve.tensor_tensor(le[:, :, :], le[:, :, :],
                                      lstat[:, 2, :].unsqueeze(2).broadcast_to([NL, H, NL]), ALU.mult).then_inc(la_p, 1)

                def linear(n, name, dst, add):
                    dve.wait_ge(lin_ps, b * 3 + n + 1)
                    for c in range(KC):
                        src = bank[7][:, c * NL:(c + 1) * NL]
                        if add is None:
                            ins = dve.tensor_scalar(lmT[:, dst, c, :], src, bcol(name, c), None, ALU.add)
                        else:
                            ins = dve.scalar_tensor_tensor(lmT[:, dst, c, :], src, bcol(name, c), lmT[:, add, c, :],
                                                           ALU.add, ALU.add)
                        ins.then_inc(lin_ready, 1)

                def queries_to_blocks():
                    dve.wait_ge(lin_ready, b * 8 + 4)
                    for c in range(KC):
                        dve.tensor_tensor(l2qbd[:, c, :, :].rearrange("p n (h m) -> p n h m", h=HC),
                                          lmT[:, l2q, c, :].rearrange("p (n m) -> p n m", n=NB).unsqueeze(2)
                                          .broadcast_to([P, NB, HC, M]),
                                          bd.unsqueeze(1).unsqueeze(3).broadcast_to([P, NB, HC, M]),
                                          ALU.mult).then_inc(lin_ready, 1)

                def landmarks_kv():
                    dve.wait_ge(lm_ps, b * 2 + 2)
                    for c in range(KC):
                        ins = dve.tensor_scalar(gkT[:, c, :], bank[7][:, c * NL:(c + 1) * NL], bcol("gk", c), None,
                                                ALU.add)
                        step(ins)
                    step(dve.tensor_tensor(gv[:, :], bank[7][0:NL, P:P + D], row("gv", slice(0, NL)), ALU.add))
                    block_diagonal(gkbd, [gkT[:, c, :] for c in range(KC)], gkbd_ready)
                    spread(gvd, gv, None, gvd_ready)

                def expand_k(t):
                    if t == 0:
                        dve.wait_ge(stack, b * 16 + 16)
                    if t >= 2:
                        dve.wait_ge(s_ps, b * 16 + 4 * (t - 1))
                    for i in range(HQ):
                        dve.tensor_scalar(kd[0:PARTS, t % 2, :, i, :], ks[0:PARTS, :, t * P:(t + 1) * P],
                                          hm[0:PARTS, i:i + 1], None, ALU.mult).then_inc(kd_ready, 1)

                def maximum(t, g):
                    dve.wait_ge(s_ps, b * 16 + 4 * t + g + 1)
                    dve.tensor_reduce(nm[:, t % 2, 8 * g:8 * g + 8],
                                      bank[g % 2][:, :].rearrange("p (h k) -> p h k", h=8), AX.X, ALU.max,
                                      negate=True).then_inc(smax, 1)
                    if g == 3:
                        dve.wait_ge(smax, b * 16 + 4 * t + 4)
                        step(dve.tensor_copy(nmh[:, t % 2, :, 0], nm[:, t % 2, :]))
                        dve.tensor_tensor(nmh[:, t % 2, :, 1], nm[:, t % 2, :], nmh[:, t % 2, :, 0],
                                          ALU.subtract).then_inc(nmh_ready, 1)

                def expand_q(t):
                    dve.wait_ge(nm_row, b * T + t + 1)
                    if t >= 1:
                        dve.wait_ge(st_ps, b * 16 + 4 * t)
                    for i in range(HQ):
                        dve.tensor_scalar(qd[0:ROWS, :, i, :], qs[0:ROWS, :, t * P:(t + 1) * P],
                                          hm[0:ROWS, i:i + 1], None, ALU.mult).then_inc(qd_ready, 1)

                def normalise(t, hf):
                    dve.wait_ge(r_t, b * 8 + 2 * t + hf + 1)
                    rv = bank[6][0:S, :].rearrange("q (h c) -> q h c", c=32)
                    for blk in range(2):
                        dve.reciprocal(rec[:, blk, :], rv[:, :, 16 * blk + DH]).then_inc(rec_ready, 1)
                    for blk in range(2):
                        dve.wait_ge(rec_ready, b * 16 + 4 * t + 2 * hf + blk + 1)
                        dve.tensor_tensor(
                            ol[S * blk:S * blk + S, t, hf * P:(hf + 1) * P].rearrange("q (h d) -> q h d", d=DH),
                            rv[:, :, 16 * blk:16 * blk + DH],
                            rec[:, blk, :].unsqueeze(2).broadcast_to([S, 16, DH]), ALU.mult).then_inc(ol_ready, 1)

                def queries():
                    linear(1, "l2t_q", l2q, None)
                    queries_to_blocks()

                landmarks = {0: lambda: attend_norm(0), 2: lambda: attend_out(0, lmf, 0),
                             3: lambda: attend_out(0, lmf, 1), 4: landmarks_qkv, 5: lambda: la_max(0),
                             6: lambda: la_max(1), 7: la_norm, 10: lambda: linear(0, "lm_out", lmf2, lmf), 11: queries,
                             12: lambda: attend_max(1), 13: lambda: attend_norm(1),
                             15: lambda: attend_out(1, roT, 0)}

                expand_k(0)
                attend_max(0)
                expand_k(1)
                for g in range(4):
                    maximum(0, g)
                for t in range(T):
                    if t + 1 < T:
                        maximum(t + 1, 0)
                        maximum(t + 1, 1)
                    expand_q(t)
                    for g in range(4):
                        if t >= 1 and g < 2:
                            normalise(t - 1, g)
                        if 1 <= g < 3 and t + 1 < T:
                            maximum(t + 1, g + 1)
                        if g == 3 and t + 2 < T:
                            expand_k(t + 2)
                        if 4 * t + g in landmarks:
                            landmarks[4 * t + g]()
                normalise(T - 1, 0)
                attend_out(1, roT, 1)
                normalise(T - 1, 1)
                linear(2, "l2t_out", lmf3, lmf2)

                landmarks_kv()
                for t in range(T):
                    for c in range(KC):
                        dve.wait_ge(sg, b * 8 + 2 * t + c + 1)
                        dve.tensor_reduce(gnm[:, t, HC * c:HC * c + HC],
                                          bank[2 * (t % 2) + c][:, :].rearrange("p (h k) -> p h k", h=HC), AX.X,
                                          ALU.max, negate=True).then_inc(gmax, 1)
                dve.wait_ge(gmax, b * 9 + 2)
                dve.tensor_scalar(gnm[:, 0, :], gnm[:, 0, :], const(cst, "valid"), None, ALU.mult).then_inc(gmax, 1)
                dve.wait_ge(mm_hi, b + 1)
                dve.tensor_tensor(mm_[H:2 * H, :], bank[4][0:H, :], mm_[0:H, :], ALU.subtract).then_inc(mm_lo, 1)
                for t in range(T):
                    dve.wait_ge(rg_t, b * T + t + 1)
                    gvw = bank[t][:, :].rearrange("p (c j) -> p c j", c=C8)
                    step(dve.tensor_scalar(grec[:, 0, :].rearrange("p (c i) -> p c i", c=C8), gvw[:, :, 32:36],
                                           SUM_EPS, None, ALU.max))
                    step(dve.reciprocal(grec[:, 1, :], grec[:, 0, :]))
                    dve.tensor_tensor(og[:, t, :].rearrange("p (c i d) -> p c i d", c=C8, i=HQ),
                                      gvw[:, :, 0:32].rearrange("p c (i d) -> p c i d", i=HQ),
                                      grec[:, 1, :].rearrange("p (c i) -> p c i", c=C8).unsqueeze(3)
                                      .broadcast_to([P, C8, HQ, DH]), ALU.mult).then_inc(og_ready, 1)
                for t in range(T):
                    dve.wait_ge(y_ps, b * T + t + 1)
                    dve.wait_ge(xb, b * T + t + 1)
                    ins = dve.tensor_tensor(x[:, b * T + t, :], bank[4 + t][:, D:2 * D], x[:, b * T + t, :], ALU.add)
                    if t + 1 < T:
                        ins.then_inc(x_new, 1)
                dve.wait_ge(x_new, b * (T - 1) + T - 1)
                ins.then_inc(batch_open, 1)
                assert count[0] == PER, count[0]

        @block.tensor
        def _(pe):
            def mm(out, lhs, rhs, start=True, stop=True):
                return pe.matmul(out, lhs, rhs, start=start, stop=stop, skip_group_check=True)

            pe.wait_ge(d_w, 96)
            pe.wait_ge(c_cast, 9)
            with pe.Fori(0, B) as b:
                pe.wait_ge(batch_open, b + 1)
                for t in range(T):
                    pe.wait_ge(xn_ready, b * T + t + 1)
                    for k in range(KC):
                        ins = pe.transpose(bank[5 + t // 2][:, (t % 2) * 256 + k * P:(t % 2) * 256 + (k + 1) * P],
                                           xn[:, t, k * P:(k + 1) * P], ident)
                    ins.then_inc(xn_t, 1)
                pe.wait_ge(xnT_ready, b * 2 + 2)
                for j, (name, c) in enumerate((n, c) for n0 in ("k", "q") for c in range(KC) for n in (n0, n0 + "s")):
                    if j >= 4:
                        pe.wait_ge(rope_mul, b * 8 + j - 3)
                    for k in range(KC):
                        ins = mm(bank[j % 4][:, :], wcol(name, k, c * P, P), xnT[:, k, :], k == 0, k == KC - 1)
                    ins.then_inc(proj, 1)
                for t in range(T):
                    for k in range(KC):
                        ins = mm(bank[5][:, t * H:(t + 1) * H], xnT[:, k, t * P:(t + 1) * P], wcol("gate", k),
                                 k == 0, k == KC - 1)
                ins.then_inc(gate_ps, 1)
                for t in range(T):
                    if t >= 2:
                        pe.wait_ge(v_ready, b * T + t - 1)
                    for k in range(KC):
                        ins = mm(bank[6 + t % 2][:, 0:D], xnT[:, k, t * P:(t + 1) * P], wcol("v", k),
                                 k == 0, k == KC - 1)
                    ins.then_inc(v_ps, 1)
                pe.wait_ge(rope_mul, b * 8 + 8)
                for s in range(16):
                    r = s // 4
                    pe.wait_ge(lo_ready, b * 4 + r + 1)
                    if s >= 4:
                        pe.wait_ge(stack, b * 16 + s - 3)
                    sel = selk if s < 8 else selq
                    mm(bank[s % 4][0:PARTS, :], sel[:, s % 4, 0, :], hi[:, r, :], True, False)
                    mm(bank[s % 4][0:PARTS, :], sel[:, s % 4, 1, :], lo[:, r, :], False, True).then_inc(stack_ps, 1)

                def attend_scores(a):
                    if a == 0:
                        pe.wait_ge(rope, b * 4 + 4)
                        pe.wait_ge(v_ready, b * T + T)
                        for c in range(KC):
                            ins = mm(bank[7][64 * c:64 * c + 64, :], pq[:, c, :], kqT[:, c, :])
                    else:
                        pe.wait_ge(lin_ready, b * 8 + 6)
                        for n in range(NB):
                            for c in range(KC):
                                ins = mm(bank[7][64 * c:64 * c + 64, n * S:(n + 1) * S], l2qbd[:, c, n, :],
                                         kqT[:, c, n * S:(n + 1) * S])
                    ins.then_inc(at_s, 1)

                def attend_turn(a):
                    pe.wait_ge(at_p, b * 2 + a + 1)
                    for t in range(T):
                        ins = pe.transpose(bank[7][:, t * P:(t + 1) * P], a_s[:, t * P:(t + 1) * P], ident)
                    ins.then_inc(at_t, 1)

                def attend_out(a, c):
                    pe.wait_ge(at_pt, b * 4 + 2 * a + 2)
                    if c:
                        pe.wait_ge(at_red, b * 4 + 2 * a + 1)
                    for t in range(T):
                        ins = mm(bank[7][:, t * P:(t + 1) * P], v[:, t, c * P:(c + 1) * P],
                                 a_pt[:, t, :, 64 * c:64 * c + 64])
                    ins.then_inc(at_o, 1)

                def project(name, src, lo_, n, chunks):
                    for c in range(chunks):
                        for k in range(KC):
                            ins = mm(bank[7][:, c * NL:(c + 1) * NL], wcol(name, k, lo_ + c * P, P), lmT[:, src, k, :],
                                     k == 0, k == KC - 1)
                    return ins

                def rows(name, src, lo_):
                    for k in range(KC):
                        ins = mm(bank[7][0:NL, P:P + D], lmT[:, src, k, :], wcol(name, k, lo_, D), k == 0, k == KC - 1)
                    return ins

                def landmarks_qkv():
                    pe.wait_ge(at_red, b * 4 + 2)
                    project("lm", lmf, 0, P, 4)
                    rows("lm", lmf, 2 * D).then_inc(lm_ps, 1)

                def la_scores(c):
                    if c == 0:
                        pe.wait_ge(lkbd_ready, b * 6 + 6)
                        pe.wait_ge(lvd_ready, b * 4 + 4)
                    else:
                        pe.wait_ge(la_sub, b * 2 + 1)
                    mm(bank[7][0:NL, :], lmT[:, lq, c, :], lkbd[:, c, :, :], True, False)
                    mm(bank[7][0:NL, :], ident[0:NL, 0:NL],
                       const(cst, "lamask", slice(0, NL)).unsqueeze(1).broadcast_to([NL, HC, NL]),
                       False, True).then_inc(la_s, 1)

                def la_turn():
                    pe.wait_ge(d_w, 96)
                    pe.wait_ge(la_p, b + 1)
                    for c in range(C8):
                        ins = pe.transpose(bank[7][:, c * NL:(c + 1) * NL],
                                           le[:, HQ * c:HQ * c + HQ, :].rearrange("q h k -> q (h k)"),
                                           ident[0:NL, 0:NL])
                    ins.then_inc(la_t, 1)

                def la_weighted():
                    pe.wait_ge(la_pt, b + 1)
                    for c in range(C8):
                        i = c % 4
                        ins = mm(bank[7][32 * i:32 * i + 32, (c // 4) * NL:(c // 4 + 1) * NL], lvd[:, c, :],
                                 lpt[:, c, :])
                    ins.then_inc(la_o, 1)

                def la_project():
                    pe.wait_ge(lo_ready_, b + 1)
                    project("lm_out", lo_T, 0, P, KC).then_inc(lin_ps, 1)

                def queries():
                    pe.wait_ge(lin_ready, b * 8 + 2)
                    project("l2t_q", lmf2, 0, P, KC).then_inc(lin_ps, 1)

                def token_project():
                    pe.wait_ge(at_red, b * 4 + 4)
                    project("l2t_out", roT, 0, P, KC).then_inc(lin_ps, 1)

                def scores(t, g):
                    u = 4 * t + g
                    if g == 0:
                        pe.wait_ge(kd_ready, b * 16 + 4 * t + 4)
                    if u >= 2:
                        pe.wait_ge(smax, b * 16 + u - 1)
                    mm(bank[g % 2][:, :], identb[:, :], causal[:, :, :].rearrange("p h k -> p (h k)"), True, False)
                    for c in (2 * g, 2 * g + 1):
                        for blk in range(2):
                            ins = mm(bank[g % 2][S * blk:S * blk + S, (c % 2) * 256:(c % 2) * 256 + 256],
                                     qs[0:PARTS, c, t * P + S * blk:t * P + S * blk + S],
                                     kd[0:PARTS, t % 2, c, :, S * blk:S * blk + S], False, c % 2 == 1)
                    ins.then_inc(s_ps, 1)

                def maxima_rows(t):
                    pe.wait_ge(nmh_ready, b * T + t + 1)
                    if t >= 1:
                        pe.wait_ge(nm_row, b * T + t)
                    for c in range(C8):
                        ins = pe.transpose(bank5b[0:2 * HQ, c * P:(c + 1) * P],
                                           nmh[:, t % 2, HQ * c:HQ * c + HQ, :].rearrange("p h j -> p (h j)"),
                                           identb[:, :])
                    ins.then_inc(nm_t, 1)

                def scores_t(t, g):
                    u = 4 * t + g
                    if g == 0:
                        pe.wait_ge(qd_ready, b * 16 + 4 * t + 4)
                    if u >= 2:
                        pe.wait_ge(exps, b * 16 + u - 1)
                    mm(bank[2 + g % 2][:, :], identb[:, :], causal_t[:, :, :].rearrange("p h k -> p (h k)"), True, False)
                    for c in (2 * g, 2 * g + 1):
                        for blk in range(2):
                            ins = mm(bank[2 + g % 2][S * blk:S * blk + S, (c % 2) * 256:(c % 2) * 256 + 256],
                                     ks[0:ROWS, c, t * P + S * blk:t * P + S * blk + S],
                                     qd[0:ROWS, c, :, S * blk:S * blk + S], False, c % 2 == 1)
                    ins.then_inc(st_ps, 1)

                def weighted(t, g):
                    u = 4 * t + g
                    if g == 0:
                        pe.wait_ge(vd_ready, b * 8 + 2 * t + 2)
                        if t >= 1:
                            pe.wait_ge(r_ready, b * T + t)
                    pe.wait_ge(exps, b * 16 + u + 1)
                    for j in range(8):
                        h = 8 * g + j
                        c, i = h // HQ, h % HQ
                        ins = mm(bank[4][32 * i:32 * i + 32, c * S:(c + 1) * S], vd[:, t, h, :], pt[:, g % 2, j, :])
                    ins.then_inc(pv, 1)

                def turn(t, hf):
                    pe.wait_ge(d_w, 96)
                    if hf == 0:
                        pe.wait_ge(r_ready, b * T + t + 1)
                    if 2 * t + hf >= 1:
                        pe.wait_ge(ol_ready, b * 16 + 2 * (2 * t + hf))
                    for j in range(4):
                        ins = pe.transpose(bank[6][0:S, j * P:(j + 1) * P], r_sb[:, 4 * hf + j, :], ident)
                    ins.then_inc(r_t, 1)

                attend_scores(0)
                landmarks = {1: lambda: attend_turn(0), 2: lambda: attend_out(0, 0), 3: lambda: attend_out(0, 1),
                             4: landmarks_qkv, 5: lambda: la_scores(0), 6: lambda: la_scores(1), 8: la_turn,
                             9: la_weighted, 10: la_project, 11: queries, 12: lambda: attend_scores(1),
                             14: lambda: attend_turn(1), 15: lambda: attend_out(1, 0)}
                for g in range(4):
                    scores(0, g)
                for t in range(T):
                    maxima_rows(t)
                    if t + 1 < T:
                        scores(t + 1, 0)
                        scores(t + 1, 1)
                    if t >= 1:
                        weighted(t - 1, 3)
                    for g in range(4):
                        if t >= 1 and g < 2:
                            turn(t - 1, g)
                        if 4 * t + g in landmarks:
                            landmarks[4 * t + g]()
                        scores_t(t, g)
                        if 1 <= g + 1 < 3 and t + 1 < T:
                            scores(t + 1, g + 2)
                        if g >= 1:
                            weighted(t, g - 1)
                weighted(T - 1, 3)
                attend_out(1, 1)
                turn(T - 1, 0)
                turn(T - 1, 1)
                token_project()

                pe.wait_ge(lin_ready, b * 8 + 8)
                project("lm_kv", lmf3, 0, P, KC)
                rows("lm_kv", lmf3, D).then_inc(lm_ps, 1)
                pe.wait_ge(gkbd_ready, b * 2 + 2)
                pe.wait_ge(smax, b * 16 + 16)
                for t in range(T):
                    for c in range(KC):
                        if t >= 2:
                            pe.wait_ge(gmax, b * 9 + 2 * (t - 2) + c + 1)
                        out = bank[2 * (t % 2) + c][:, :]
                        mm(out, onehot[:, t * P:(t + 1) * P], gmask[:, :, :].rearrange("n h k -> n (h k)"), True, False)
                        mm(out, kqT[:, 2 + c, t * P:(t + 1) * P], gkbd[:, c, :, :].rearrange("p h k -> p (h k)"),
                           False, True).then_inc(sg, 1)
                pe.wait_ge(gmax, b * 9 + 9)
                pe.wait_ge(r_ready, b * T + T)
                for t in range(T):
                    ins = pe.transpose(bank[4][0:H, t * P:(t + 1) * P], gnm[:, t, :], ident)
                ins.then_inc(gm_t, 1)

                def global_scores(c):
                    if c >= 4:
                        pe.wait_ge(gexp, b * C8 + c - 3)
                    mm(bank[c % 4][:, :], selg[0:2 * H + NB, c, :], mm_[0:2 * H + NB, :], True, False)
                    mm(bank[c % 4][:, :], gkbd[:, c // 4, HQ * (c % 4):HQ * (c % 4) + HQ, :]
                       .rearrange("p h k -> p (h k)"), kqT[:, 2 + c // 4, :], False, True).then_inc(sgt, 1)

                def global_weighted(c):
                    if c == 2:
                        pe.wait_ge(nm_row, b * T + T)
                    if c == 4:
                        pe.wait_ge(ol_ready, b * 16 + 16)
                    pe.wait_ge(gexp, b * C8 + c + 1)
                    mm(bank[4 + c // 2][64 * (c % 2):64 * (c % 2) + 64, :], gvd[:, c, :],
                       pg[:, c % 2, :, :].rearrange("p h q -> p (h q)")).then_inc(gpv, 1)

                pe.wait_ge(mm_lo, b + 1)
                pe.wait_ge(gvd_ready, b * 4 + 4)
                global_scores(0)
                for c in range(1, C8):
                    global_scores(c)
                    global_weighted(c - 1)
                global_weighted(C8 - 1)
                pe.wait_ge(rg_ready, b * 4 + 4)
                for t in range(T):
                    for j in range(4):
                        ins = pe.transpose(bank[t][:, j * P:(j + 1) * P], rg[:, j, t * P:(t + 1) * P], ident)
                    ins.then_inc(rg_t, 1)
                for t in range(T):
                    pe.wait_ge(o_ready, b * T + t + 1)
                    for k in range(KC):
                        ins = pe.transpose(bank[4 + t][:, k * P:(k + 1) * P], ol[:, t, k * P:(k + 1) * P], ident)
                    ins.then_inc(o_t, 1)
                    pe.wait_ge(oT_ready, b * T + t + 1)
                    for k in range(KC):
                        ins = mm(bank[4 + t][:, D:2 * D], oT[:, t % 2, k, :], wcol("out", k), k == 0, k == KC - 1)
                    ins.then_inc(y_ps, 1)


DVE_LINKS_A = 31


def experts_and_attention_b(nc, x, cst, mean, rstd, bank, wb_d, pb_d, wg_d, we_d, slots_x, slots_y, out_d):
    with ExitStack() as ctx:
        def sb(name, shape, dt=F32):
            return ctx.enter_context(nc.sbuf_tensor(name, shape, dt))

        def sem(name):
            return ctx.enter_context(nc.semaphore(name))

        wh = sb("wh", [P, 3 * NW, WCOL], BF16)
        wl = sb("wl", [P, 3 * NW, WCOL], BF16)
        stage = sb("stage", [P, 3, WCOL])
        wb = sb("wb", [P, KC, QKVB])
        pb = sb("pb", [P, KC, D])
        wg = sb("wg", [P, KC, E])
        st6 = sb("st6b", [P, NT, 6])
        mv = sb("mvb", [P, NT, 2])
        var = sb("var", [P, NT])
        xn = sb("xnb", [P, NT, D])
        xT = sb("xTb", [P, 2, KC, P])
        oT = sb("oTb", [P, 2, KC, P])
        prob = sb("prob", [P, NT, E])
        key = sb("key", [P, NT, E])
        eq = sb("eq", [P, NT, E])
        pick = sb("pick", [P, 2, NT, E])
        pickb = sb("pickb", [P, NT, E], BF16)
        trib = sb("trib", [P, P], BF16)
        onesb = sb("onesb", [P, P], BF16)
        best = sb("best", [P, 8, NT])
        seg = sb("seg", [P, 4, E])
        wide = sb("wide", [P, ROUTED * E])
        slot_f = sb("slot_f", [P, 2, NT])
        slot_i = sb("slot_i", [P, 2, NT], I32)
        etab = sb("etab", [P, TILES + 1], I32)
        etab_f = sb("etab_f", [P, ROUTED])
        weight = sb("weight", [P, 2, NT])
        xs = sb("xs", [P, 2, D])
        xh = sb("xh", [P, 2, KC, P], BF16)
        xl = sb("xl", [P, 2, KC, P], BF16)
        NPAIR = SEQ * (SEQ + 1) // 2
        work = sb("work", [P, NPAIR * D])
        sg = work[:, 0:2 * FF].rearrange("p (a n) -> p a n", a=2)
        hh = work[:, 2 * FF:4 * FF].rearrange("p (a n) -> p a n", a=2)
        ysb = work[:, 4 * FF:4 * FF + 2 * D].rearrange("p (a n) -> p a n", a=2)
        hTh = sb("hTh", [P, 2, FC, P], BF16)
        hTl = sb("hTl", [P, 2, FC, P], BF16)
        RING = 4
        gat = sb("gat", [P, 3, RING, D])

        d_stage = [sem(f"d_stage{m}") for m in range(3)]
        y_out = [sem("y_out_even"), sem("y_out_odd")]
        g_in = [sem(f"g_in{r}") for r in range(RING)]
        s_in = [sem(f"s_in{r}") for r in range(RING)]
        PER = ((TILES + 1) // 2, TILES // 2)
        d_b, w_hi, w_lo, casts = sem("d_b"), sem("w_hi"), sem("w_lo"), sem("casts")
        (bstat, bvar, bstd, brs, xn_ready, xn_t, xT_ready, logits, r_sub, r_exp, r_step, pick_ready, ranks, slot_ready,
         xn_out, scattered) = [sem(n) for n in (
             "bstat bvar bstd brs bxn_ready bxn_t bxT_ready logits r_sub r_exp r_step pick_ready ranks slot_ready "
             "xn_out scattered").split()]
        (xs_t, xh_ready, xl_ready, gu, sg_ready, h_ready, h_t, hTh_ready, hTl_ready, y_ps, y_ready,
         combined) = [sem(n) for n in (
             "xs_t xh_ready xl_ready gu sg_ready h_ready h_t hTh_ready hTl_ready by_ps by_ready "
             "combined").split()]
        xs_in = [sem("xs_in_even"), sem("xs_in_odd")]
        (b_qkv, b_q, b_mul, b_sub, b_exp, b_p, b_o, b_ot, b_oT, b_y, b_x, b_step, b_pool) = [sem(n) for n in (
            "b_qkv b_q b_mul b_sub b_exp b_p b_o b_ot b_oT b_y b_x b_step b_pool").split()]
        done = sem("done")

        ident = const(cst, "ident")
        X, G, U, HT, Y = 0, (1, 2), (3, 4), 5, 6
        FULL = NT * P
        qkv = stage[:, :, :].rearrange("p a b -> p (a b)").rearrange("p (c s n) -> p c s n", c=2, s=SEQ)
        prod = work[:, :].rearrange("p (a n) -> p a n", a=NPAIR)
        sc = sb("scb", [P, NPAIR, NH])
        sstat = sb("sstat", [P, 3, SEQ, NH])
        block = ctx.enter_context(nc.Block())

        def pair(s, t=0):
            return s * (s + 1) // 2 + t

        def tile_b(n):
            return (n % SEQ) * T + n // SEQ

        @block.sync
        def _(sp):
            sp.dma_start(wg[:, :, :], wg_d).then_inc(d_b, 16)
            sp.dma_start(wb[:, :, :], wb_d).then_inc(d_b, 16)
            sp.dma_start(pb[:, :, :], pb_d).then_inc(d_b, 16)
            for m in range(3):
                sp.dma_start(stage[:, m, :], we_d[0, m]).then_inc(d_stage[m], 16)
            rows_x = slots_x.rearrange("(j p) d -> j p d", p=P)
            rows_y = slots_y.rearrange("(j p) d -> j p d", p=P)
            we_v = we_d.rearrange("e m p n -> (e m) p n")
            BEHIND = 5
            assert E == NT // 2
            for layer in range(2):
                first = layer == 0
                for t in range(NT):
                    sp.wait_ge(xn_ready, layer * 2 * NT + t + 1)
                    sp.dma_start(rows_x[t], xn[:, t, :]).then_inc(xn_out, 16)
                sp.wait_ge(xn_out, (layer + 1) * 16 * NT)

                def load(j, par):
                    sp.dma_start(xs[:, par, :], rows_x[j]).then_inc(xs_in[par], 16)

                def store(j, par):
                    sp.wait_ge(y_ready, layer * TILES + j + 1)
                    sp.dma_start(rows_y[j], ysb[:, par, :]).then_inc(y_out[par], 16)

                for par in range(2):
                    if layer:
                        sp.wait_ge(xs_t, layer * TILES)
                    load(par, par)
                def tiles_of(i):
                    for par in range(2):
                        sp.wait_ge(xs_t, layer * TILES + 2 * i + par - 1)
                        load(2 * i + par, par)
                        if not isinstance(i, int) or 2 * i + par >= BEHIND:
                            store(2 * i + par - BEHIND, 1 - par)

                def weights_of(e):
                    for m in range(3):
                        sp.wait_ge(w_hi, 3 * e - 2 + m)
                        sp.wait_ge(w_lo, 3 * e - 2 + m)
                        sp.dma_start(stage[:, m, :], we_v[3 * e + m]).then_inc(d_stage[m], 16)

                for i in (1, 2):
                    tiles_of(i)
                    if first:
                        weights_of(i)
                with sp.Fori(3, NT // 2) as i:
                    tiles_of(i)
                    if first:
                        weights_of(i)
                if first:
                    weights_of(E)
                sp.wait_ge(scattered, (layer + 1) * 32 * NT)
                with sp.Fori(NT // 2, TILES // 2) as i:
                    tiles_of(i)
                sp.wait_ge(xs_t, layer * TILES + TILES - 2)
                load(TILES - 1, 0)
                for j in range(TILES - 1 - BEHIND, TILES):
                    store(j, j % 2)
                for t in range(NT):
                    if t == 0:
                        for par in range(2):
                            sp.wait_ge(y_out[par], (layer + 1) * 16 * PER[par])
                    if t >= RING:
                        sp.wait_ge(combined, layer * NT + t - RING + 1)
                    elif layer:
                        sp.wait_ge(combined, layer * NT)
                    sp.dma_start(gat[:, 2, t % RING, :], rows_y[t]).then_inc(s_in[t % RING], 16)
            out_v = out_d.rearrange("b (t p) d -> b p t d", p=P)
            for b in range(B):
                sp.wait_ge(combined, NT + (b + 1) * T)
                sp.dma_start(out_v[b], x[:, b * T:(b + 1) * T, :]).then_inc(done, 16)
            sp.wait_ge(done, 16 * B)

        @block.gpsimd
        def _(pool):
            for m in range(3):
                pool.wait_ge(w_hi, m + 1)
                pool.tensor_tensor(wl[:, m, :], stage[:, m, :], wh[:, m, :], ALU.subtract).then_inc(w_lo, 1)
            for layer in range(2):
                pool.wait_ge(slot_ready, layer + 1)
                pool.wait_ge(xn_ready, layer * 2 * NT + NT)
                for t in range(NT):
                    for k in range(2):
                        pool.indirect_dma_start(slots_x, bass.IndirectOffsetOnAxis(ap=slot_i[:, k, t:t + 1], axis=0),
                                                xn[:, t, :], None).then_inc(scattered, 16)
                if layer == 0:
                    with pool.Fori(1, NW) as e:
                        for m in range(3):
                            pool.wait_ge(w_hi, 3 * e + m + 1)
                            pool.tensor_tensor(wl[:, bass.ds(3 * e + m, 1), :], stage[:, m:m + 1, :],
                                               wh[:, bass.ds(3 * e + m, 1), :], ALU.subtract).then_inc(w_lo, 1)
                for par in range(2):
                    pool.wait_ge(y_out[par], (layer + 1) * 16 * PER[par])
                for t in range(NT):
                    if t >= RING:
                        pool.wait_ge(combined, layer * NT + t - RING + 1)
                    for k in range(2):
                        pool.indirect_dma_start(gat[:, k, t % RING, :], None, slots_y,
                                                bass.IndirectOffsetOnAxis(ap=slot_i[:, k, t:t + 1], axis=0))\
                            .then_inc(g_in[t % RING], 16)

        @block.scalar
        def _(act):
            act.activation(trib[:, :], const(cst, "tri"), ACT.Copy).then_inc(casts, 1)
            act.activation(onesb[:, :], const(cst, "ones"), ACT.Copy).then_inc(casts, 1)

            def std(n):
                act.wait_ge(bvar, n + 1)
                act.activation(var[:, :], var[:, :], ACT.Sqrt).then_inc(bstd, 1)

            def turned(n0):
                for t in range(NT):
                    act.wait_ge(xn_t, n0 + t + 1)
                    act.activation(xT[:, t % 2, :, :].rearrange("p k c -> p (k c)"), bank[t % 2][:, 0:D],
                                   ACT.Copy).then_inc(xT_ready, 1)

            def moe(layer):
                std(2 * layer)
                turned(layer * 2 * NT)
                act.wait_ge(r_sub, layer + 1)
                act.activation(prob[:, :, :], prob[:, :, :], ACT.Exp).then_inc(r_exp, 1)
                n0 = layer * TILES

                def x_high(j, par):
                    act.wait_ge(xs_t, n0 + j + 1)
                    act.activation(xh[:, par, :, :].rearrange("p k c -> p (k c)"), bank[X][:, 0:D],
                                   ACT.Copy).then_inc(xh_ready, 1)

                def gates(j, par):
                    act.wait_ge(gu, n0 + j + 1)
                    act.activation(sg[:, par, :], bank[G[par]][:, :], ACT.Silu).then_inc(sg_ready, 1)

                def h_high(j, par):
                    act.wait_ge(h_t, n0 + j + 1)
                    act.activation(hTh[:, par, :, :].rearrange("p c t -> p (c t)"), bank[HT][:, :],
                                   ACT.Copy).then_inc(hTh_ready, 1)

                def rows_out(j, par, nth):
                    act.wait_ge(y_ps, n0 + j + 1)
                    if not isinstance(nth, int) or layer * PER[par] + nth:
                        act.wait_ge(y_out[par], 16 * (layer * PER[par] + nth))
                    act.activation(ysb[:, par, :], bank[Y][:, 0:D], ACT.Copy).then_inc(y_ready, 1)

                x_high(0, 0)
                x_high(1, 1)
                gates(0, 0)
                x_high(2, 0)
                gates(1, 1)
                h_high(0, 0)
                def pair_of_tiles(i):
                    for par in range(2):
                        j = 2 * i + par
                        x_high(j + 1, 1 - par)
                        rows_out(j - 2, par, i - 1)
                        gates(j, par)
                        h_high(j - 1, 1 - par)

                pair_of_tiles(1)
                with act.Fori(2, TILES // 2) as i:
                    pair_of_tiles(i)
                j = TILES - 1
                rows_out(j - 2, 0, j // 2 - 1)
                gates(j, 0)
                h_high(j - 1, 1)
                rows_out(j - 1, 1, j // 2 - 1)
                h_high(j, 0)
                rows_out(j, 0, j // 2)

            def attention_b():
                std(1)

                def turned_b(n):
                    act.wait_ge(xn_t, NT + n + 1)
                    act.activation(xT[:, n % 2, :, :].rearrange("p k c -> p (k c)"), bank[n % 2][:, 0:D],
                                   ACT.Copy).then_inc(xT_ready, 1)

                def qkv_rows(c):
                    for s in range(SEQ):
                        n = c * SEQ + s
                        if n + 1 < NT:
                            turned_b(n + 1)
                        act.wait_ge(b_qkv, n + 1)
                        if s == 0 and c >= 2:
                            act.wait_ge(b_mul, 2 * (c - 1) * NPAIR)
                        act.activation(qkv[:, c % 2, s, :], bank[2 + n % 2][:, 0:QKVB], ACT.Copy).then_inc(b_q, 1)

                turned_b(0)
                qkv_rows(0)
                for c in range(T):
                    if c + 1 < T:
                        qkv_rows(c + 1)
                    act.wait_ge(b_sub, c + 1)
                    act.activation(sc[:, :, :], sc[:, :, :], ACT.Exp, scale=SCALE_B).then_inc(b_exp, 1)
                    for s in range(SEQ):
                        n = c * SEQ + s
                        act.wait_ge(b_ot, n + 1)
                        if n >= 2:
                            act.wait_ge(b_y, n - 1)
                        act.activation(oT[:, n % 2, :, :].rearrange("p k c -> p (k c)"), bank[4 + n % 2][:, 0:D],
                                       ACT.Copy).then_inc(b_oT, 1)

            moe(0)
            attention_b()
            moe(1)

        @block.vector
        def _(dve):
            steps = [0]

            def step(ins):
                steps[0] += 1
                ins.then_inc(r_step, 1)
                dve.wait_ge(r_step, steps[0])

            def statistics(n, ready):
                for t in range(NT):
                    ready(t)
                    dve.bn_stats(st6[:, t, :], x[:, t, :]).then_inc(bstat, 1)
                for t in range(NT):
                    dve.wait_ge(bstat, n * 2 * NT + t + 1)
                    dve.bn_aggr(mv[:, t, :], st6[:, t, :]).then_inc(bstat, 1)
                dve.wait_ge(bstat, (n + 1) * 2 * NT)
                dve.tensor_copy(mean[:, :], mv[:, :, 0]).then_inc(brs, 1)
                dve.tensor_scalar(var[:, :], mv[:, :, 1], LN_EPS, None, ALU.add).then_inc(bvar, 1)
                dve.wait_ge(bstd, n + 1)
                dve.reciprocal(rstd[:, :], var[:, :]).then_inc(brs, 1)
                dve.wait_ge(brs, 2 * n + 2)

            def normalised(t):
                dve.tensor_scalar(xn[:, t, :], x[:, t, :], mean[:, t:t + 1], rstd[:, t:t + 1], ALU.subtract,
                                  ALU.mult).then_inc(xn_ready, 1)

            def router(layer):
                dve.wait_ge(logits, layer + 1)
                lg = bank[7][:, 0:NT * E].rearrange("p (t e) -> p t e", e=E)

                def over(a):
                    return a.unsqueeze(2).broadcast_to([P, NT, E])

                step(dve.tensor_reduce(best[:, 0, :], lg, AX.X, ALU.max))
                dve.tensor_tensor(prob[:, :, :], lg, over(best[:, 0, :]), ALU.subtract).then_inc(r_sub, 1)
                dve.wait_ge(r_exp, layer + 1)
                step(dve.tensor_reduce(best[:, 1, :], prob[:, :, :], AX.X, ALU.add))
                step(dve.reciprocal(best[:, 2, :], best[:, 1, :]))
                step(dve.tensor_tensor(prob[:, :, :], prob[:, :, :], over(best[:, 2, :]), ALU.mult))
                iota = const(cst, "iota8").unsqueeze(1).broadcast_to([P, NT, E])
                for k in range(2):
                    step(dve.tensor_reduce(best[:, 3 + k, :], prob[:, :, :], AX.X, ALU.max))
                    step(dve.tensor_tensor(eq[:, :, :], prob[:, :, :], over(best[:, 3 + k, :]), ALU.is_equal))
                    step(dve.scalar_tensor_tensor(key[:, :, :], eq[:, :, :], float(-E), iota, ALU.mult, ALU.add))
                    step(dve.tensor_reduce(best[:, 5, :], key[:, :, :], AX.X, ALU.min))
                    step(dve.tensor_tensor(pick[:, k, :, :], key[:, :, :], over(best[:, 5, :]), ALU.is_equal))
                    if k == 0:
                        step(dve.scalar_tensor_tensor(prob[:, :, :], pick[:, 0, :, :], -2.0, prob[:, :, :],
                                                      ALU.mult, ALU.add))
                dve.tensor_tensor(pickb[:, :, :], pick[:, 0, :, :], pick[:, 1, :, :], ALU.add).then_inc(pick_ready, 1)
                step(dve.tensor_tensor(best[:, 6, :], best[:, 3, :], best[:, 4, :], ALU.add))
                step(dve.reciprocal(best[:, 7, :], best[:, 6, :]))
                for k in range(2):
                    step(dve.tensor_tensor(weight[:, k, :], best[:, 3 + k, :], best[:, 7, :], ALU.mult))
                dve.wait_ge(ranks, layer + 1)
                rk = bank[7][:, P:P + (NT + 1) * E].rearrange("p (t e) -> p t e", e=E)
                cnt, tiles, base, end = (seg[:, i, :] for i in range(4))
                step(dve.tensor_copy(cnt, rk[:, NT, :]))
                starts = const(cst, "tilestart")
                wv = wide[:, 0:E * NT].rearrange("p (e j) -> p e j", e=E)
                step(dve.tensor_tensor(wv, cnt.unsqueeze(2).broadcast_to([P, E, NT]),
                                       starts[:, 0:NT].unsqueeze(1).broadcast_to([P, E, NT]), ALU.is_gt))
                step(dve.tensor_reduce(tiles, wv, AX.X, ALU.add))
                bv = wide[:, 0:E * E].rearrange("p (e f) -> p e f", e=E)
                step(dve.tensor_tensor(bv, tiles.unsqueeze(1).broadcast_to([P, E, E]),
                                       const(cst, "tri8").rearrange("p (e f) -> p e f", e=E), ALU.mult))
                step(dve.tensor_reduce(base, bv, AX.X, ALU.add))
                step(dve.tensor_tensor(end, base, tiles, ALU.add))
                step(dve.tensor_scalar(base, base, float(P), float(FULL), ALU.mult, ALU.add))
                step(dve.tensor_scalar(end, end, float(P), None, ALU.mult))
                step(dve.tensor_tensor(eq[:, :, :], rk[:, 0:NT, :], base.unsqueeze(1).broadcast_to([P, NT, E]),
                                       ALU.add))
                for k in range(2):
                    step(dve.tensor_tensor(key[:, :, :], eq[:, :, :], pick[:, k, :, :], ALU.mult))
                    step(dve.tensor_reduce(slot_f[:, k, :], key[:, :, :], AX.X, ALU.add))
                tv = wide[:, :].rearrange("p (j e) -> p j e", e=E)
                step(dve.tensor_tensor(tv, starts.unsqueeze(2).broadcast_to([P, ROUTED, E]),
                                       end.unsqueeze(1).broadcast_to([P, ROUTED, E]), ALU.is_ge))
                step(dve.tensor_reduce(etab_f[:, :], tv, AX.X, ALU.add))
                step(dve.tensor_scalar(etab_f[:, :], etab_f[:, :], float(E - 1), 1.0, ALU.min, ALU.add))
                step(dve.tensor_scalar(etab[:, NT:TILES], etab_f[:, :], 3.0, None, ALU.mult))
                dve.tensor_copy(slot_i[:, :, :], slot_f[:, :, :]).then_inc(slot_ready, 1)

            def moe(layer):
                if layer == 0:
                    statistics(0, lambda t: None)
                else:
                    dve.wait_ge(b_x, NT)
                    statistics(2, lambda t: None)
                for t in range(NT):
                    normalised(t)
                if layer == 0:
                    step(dve.memset(etab[:, 0:NT], 0))
                    for m in range(3):
                        dve.wait_ge(d_stage[m], 16)
                        dve.tensor_copy(wh[:, m, :], stage[:, m, :]).then_inc(w_hi, 1)
                router(layer)
                n0 = layer * TILES

                def x_low(j, par):
                    dve.wait_ge(xh_ready, n0 + j + 1)
                    dve.tensor_tensor(xl[:, par, :, :].rearrange("p k c -> p (k c)"), bank[X][:, 0:D],
                                      xh[:, par, :, :].rearrange("p k c -> p (k c)"), ALU.subtract)\
                       .then_inc(xl_ready, 1)

                def hidden(j, par):
                    dve.wait_ge(sg_ready, n0 + j + 1)
                    dve.tensor_tensor(hh[:, par, :], bank[U[par]][:, :], sg[:, par, :], ALU.mult).then_inc(h_ready, 1)

                def h_low(j, par):
                    dve.wait_ge(hTh_ready, n0 + j + 1)
                    dve.tensor_tensor(hTl[:, par, :, :].rearrange("p c t -> p (c t)"), bank[HT][:, :],
                                      hTh[:, par, :, :].rearrange("p c t -> p (c t)"), ALU.subtract)\
                       .then_inc(hTl_ready, 1)

                x_low(0, 0)
                x_low(1, 1)
                hidden(0, 0)
                x_low(2, 0)
                hidden(1, 1)
                h_low(0, 0)

                def pair_of_tiles(i, split):
                    if split:
                        for m in range(3):
                            dve.wait_ge(d_stage[m], 16 * i + 16)
                            dve.tensor_copy(wh[:, bass.ds(3 * i + m, 1), :], stage[:, m:m + 1, :]).then_inc(w_hi, 1)
                    for par in range(2):
                        j = 2 * i + par
                        x_low(j + 1, 1 - par)
                        hidden(j, par)
                        h_low(j - 1, 1 - par)

                if layer == 0:
                    with dve.Fori(1, NW) as i:
                        pair_of_tiles(i, True)
                    with dve.Fori(NW, TILES // 2) as i:
                        pair_of_tiles(i, False)
                else:
                    with dve.Fori(1, TILES // 2) as i:
                        pair_of_tiles(i, False)
                j = TILES - 1
                hidden(j, 0)
                h_low(j - 1, 1)
                h_low(j, 0)
                for t in range(NT):
                    nth = layer * (NT // RING) + t // RING + 1
                    dve.wait_ge(g_in[t % RING], 32 * nth)
                    dve.wait_ge(s_in[t % RING], 16 * nth)
                    step(dve.tensor_tensor(x[:, t, :], gat[:, 2, t % RING, :], x[:, t, :], ALU.add))
                    for k in range(2):
                        ins = dve.scalar_tensor_tensor(x[:, t, :], gat[:, k, t % RING, :], weight[:, k, t:t + 1],
                                                       x[:, t, :], ALU.mult, ALU.add)
                        if k == 0:
                            step(ins)
                    ins.then_inc(combined, 1)

            def attention_b():
                def ready(t):
                    dve.wait_ge(combined, t + 1)
                statistics(1, ready)
                for n in range(NT):
                    normalised(tile_b(n))

                def head(a):
                    return a.rearrange("p (g n) -> p g n", g=NKV)

                for c in range(T):
                    dve.wait_ge(b_q, (c + 1) * SEQ)
                    for s in range(SEQ):
                        q = head(qkv[:, c % 2, s, :])[:, :, 0:64].rearrange("p g (r d) -> p g r d", d=HD)
                        for t in range(s + 1):
                            k = head(qkv[:, c % 2, t, :])[:, :, 64:80].unsqueeze(2).broadcast_to([P, NKV, 4, HD])
                            dve.tensor_tensor(prod[:, pair(s, t), :].rearrange("p (g r d) -> p g r d", g=NKV, r=4),
                                              q, k, ALU.mult).then_inc(b_mul, 1)
                    dve.wait_ge(b_mul, (2 * c + 1) * NPAIR)
                    step(dve.tensor_reduce(sc[:, :, :].rearrange("p a h -> p (a h)"),
                                           prod[:, :, :].rearrange("p a (h d) -> p (a h) d", d=HD), AX.X, ALU.add))
                    for s in range(SEQ):
                        own = sc[:, pair(s):pair(s) + s + 1, :]
                        step(dve.tensor_reduce(sstat[:, 0, s, :], own.rearrange("p a h -> p h a"), AX.X, ALU.max))
                        ins = dve.tensor_tensor(own, own, sstat[:, 0, s, :].unsqueeze(1)
                                                .broadcast_to([P, s + 1, NH]), ALU.subtract)
                        if s + 1 < SEQ:
                            step(ins)
                    ins.then_inc(b_sub, 1)
                    dve.wait_ge(b_exp, c + 1)
                    for s in range(SEQ):
                        own = sc[:, pair(s):pair(s) + s + 1, :]
                        step(dve.tensor_reduce(sstat[:, 1, s, :], own.rearrange("p a h -> p h a"), AX.X, ALU.add))
                        step(dve.reciprocal(sstat[:, 2, s, :], sstat[:, 1, s, :]))
                        step(dve.tensor_tensor(own, own, sstat[:, 2, s, :].unsqueeze(1)
                                               .broadcast_to([P, s + 1, NH]), ALU.mult))
                    for s in range(SEQ):
                        for t in range(s + 1):
                            vv = head(qkv[:, c % 2, t, :])[:, :, 80:96].unsqueeze(2).broadcast_to([P, NKV, 4, HD])
                            pp = sc[:, pair(s, t), :].rearrange("p (g r) -> p g r", g=NKV).unsqueeze(3)\
                                .broadcast_to([P, NKV, 4, HD])
                            dve.tensor_tensor(prod[:, pair(s, t), :].rearrange("p (g r d) -> p g r d", g=NKV, r=4),
                                              vv, pp, ALU.mult).then_inc(b_mul, 1)
                    dve.wait_ge(b_mul, (2 * c + 2) * NPAIR)
                    for s in range(SEQ):
                        if s == 0:
                            ins = dve.tensor_copy(xn[:, c, :], prod[:, 0, :])
                        else:
                            ins = dve.tensor_reduce(xn[:, s * T + c, :], prod[:, pair(s):pair(s) + s + 1, :]
                                                    .rearrange("p a n -> p n a"), AX.X, ALU.add)
                        ins.then_inc(b_o, 1)
                    for s in range(SEQ):
                        n = c * SEQ + s
                        dve.wait_ge(b_y, n + 1)
                        dve.tensor_tensor(x[:, s * T + c, :], bank[6 + n % 2][:, 0:D], x[:, s * T + c, :],
                                          ALU.add).then_inc(b_x, 1)

            moe(0)
            attention_b()
            moe(1)

        @block.tensor
        def _(pe):
            def mm(out, lhs, rhs, start=True, stop=True):
                return pe.matmul(out, lhs, rhs, start=start, stop=stop, skip_group_check=True)

            def turn(n0, t, tile=None):
                pe.wait_ge(xn_ready, n0 + t + 1)
                if n0 + t >= 2:
                    pe.wait_ge(xT_ready, n0 + t - 1)
                for k in range(KC):
                    ins = pe.transpose(bank[t % 2][:, k * P:(k + 1) * P],
                                       xn[:, t if tile is None else tile, k * P:(k + 1) * P], ident)
                ins.then_inc(xn_t, 1)

            pe.wait_ge(d_b, 48)
            pe.wait_ge(casts, 2)

            def moe(layer):
                t0 = layer * 2 * NT
                turn(t0, 0)
                for t in range(NT):
                    if t + 1 < NT:
                        turn(t0, t + 1)
                    pe.wait_ge(xT_ready, t0 + t + 1)
                    for k in range(KC):
                        ins = mm(bank[7][:, t * E:(t + 1) * E], xT[:, t % 2, k, :], wg[:, k, :], k == 0, k == KC - 1)
                ins.then_inc(logits, 1)
                pe.wait_ge(pick_ready, layer + 1)
                mm(bank[7][:, P:P + NT * E], trib[:, :], pickb[:, :, :].rearrange("p t e -> p (t e)"), True, False)
                for s in range(1, NT + 1):
                    n = (NT + 1 - s) * E
                    ins = mm(bank[7][:, P + s * E:P + s * E + n], onesb[:, :],
                             pickb[:, :, :].rearrange("p t e -> p (t e)")[:, 0:n], False, s == NT)
                ins.then_inc(ranks, 1)
                n0 = layer * TILES

                def rows_in(j, par, waits=True, nth=None):
                    if waits:
                        pe.wait_ge(xl_ready, n0 + j)
                    pe.wait_ge(xs_in[par], 16 * (layer * PER[par] + (nth if nth is not None else j // 2) + 1))
                    for k in range(KC):
                        ins = pe.transpose(bank[X][:, k * P:(k + 1) * P], xs[:, par, k * P:(k + 1) * P], ident)
                    ins.then_inc(xs_t, 1)

                def weights(e, part, m, k, cols):
                    buf = (wh, wl)[part]
                    if isinstance(e, int):
                        return buf[:, e + m, k * cols:(k + 1) * cols]
                    return buf[:, bass.ds(e + m, 1), k * cols:(k + 1) * cols]

                def gate_up(j, par, e, waits=True):
                    pe.wait_ge(xl_ready, n0 + j + 1)
                    if waits:
                        pe.wait_ge(h_ready, n0 + j - 1)
                    outs = (bank[G[par]][:, :], bank[U[par]][:, :])
                    for k in range(KC):
                        for m in range(2):
                            mm(outs[m], xh[:, par, k, :], weights(e, 0, m, k, FF), k == 0, False)
                            mm(outs[m], xh[:, par, k, :], weights(e, 1, m, k, FF), False, False)
                        for m in range(2):
                            ins = mm(outs[m], xl[:, par, k, :], weights(e, 0, m, k, FF), False, k == KC - 1)
                    ins.then_inc(gu, 1)

                def down(j, par, e, waits=True):
                    pe.wait_ge(hTl_ready, n0 + j + 1)
                    if waits:
                        pe.wait_ge(y_ready, n0 + j)
                    for c in range(FC):
                        mm(bank[Y][:, 0:D], hTh[:, par, c, :], weights(e, 0, 2, c, D), c == 0, False)
                        mm(bank[Y][:, 0:D], hTh[:, par, c, :], weights(e, 1, 2, c, D), False, False)
                        ins = mm(bank[Y][:, 0:D], hTl[:, par, c, :], weights(e, 0, 2, c, D), False, c == FC - 1)
                    ins.then_inc(y_ps, 1)

                def turn_hidden(j, par):
                    pe.wait_ge(h_ready, n0 + j + 1)
                    for c in range(FC):
                        ins = pe.transpose(bank[HT][:, c * P:(c + 1) * P], hh[:, par, c * P:(c + 1) * P], ident)
                    ins.then_inc(h_t, 1)

                def expert(j):
                    return pe.snap(pe.value_load(etab[0:1, bass.ds(j, 1)], min_val=0, max_val=3 * E))

                rows_in(0, 0, waits=False)
                rows_in(1, 1)
                pe.wait_ge(w_lo, 3)
                gate_up(0, 0, 0, waits=False)
                rows_in(2, 0)
                gate_up(1, 1, 0, waits=False)
                turn_hidden(0, 0)

                def pair_of_tiles(i, shared):
                    for par in range(2):
                        j = 2 * i + par
                        rows_in(j + 1, 1 - par, nth=i + par)
                        gate_up(j, par, 0 if shared else expert(j))
                        down(j - 2, par, 0 if shared else expert(j - 2), waits=not isinstance(j, int) or j > 2 or layer > 0)
                        turn_hidden(j - 1, 1 - par)

                pair_of_tiles(1, True)
                with pe.Fori(2, NT // 2) as i:
                    pair_of_tiles(i, True)
                pe.wait_ge(w_lo, 3 * NW)
                pe.wait_ge(slot_ready, layer + 1)
                with pe.Fori(NT // 2, TILES // 2) as i:
                    pair_of_tiles(i, False)
                j = TILES - 1
                gate_up(j, 0, expert(j))
                down(j - 2, 0, expert(j - 2))
                turn_hidden(j - 1, 1)
                down(j - 1, 1, expert(j - 1))
                turn_hidden(j, 0)
                down(j, 0, expert(j))

            def attention_b():
                def project(c):
                    for s in range(SEQ):
                        n = c * SEQ + s
                        if n + 1 < NT:
                            turn(NT, n + 1, tile_b(n + 1))
                        pe.wait_ge(xT_ready, NT + n + 1)
                        if n >= 2:
                            pe.wait_ge(b_q, n - 1)
                        for k in range(KC):
                            ins = mm(bank[2 + n % 2][:, 0:QKVB], xT[:, n % 2, k, :], wb[:, k, :], k == 0, k == KC - 1)
                        ins.then_inc(b_qkv, 1)

                turn(NT, 0, tile_b(0))
                project(0)
                for c in range(T):
                    if c + 1 < T:
                        project(c + 1)
                    for s in range(SEQ):
                        n = c * SEQ + s
                        pe.wait_ge(b_o, n + 1)
                        if n >= 2:
                            pe.wait_ge(b_oT, n - 1)
                        for k in range(KC):
                            ins = pe.transpose(bank[4 + n % 2][:, k * P:(k + 1) * P],
                                               xn[:, tile_b(n), k * P:(k + 1) * P], ident)
                        ins.then_inc(b_ot, 1)
                        pe.wait_ge(b_oT, n + 1)
                        if n >= 2:
                            pe.wait_ge(b_x, n - 1)
                        for k in range(KC):
                            ins = mm(bank[6 + n % 2][:, 0:D], oT[:, n % 2, k, :], pb[:, k, :], k == 0, k == KC - 1)
                        ins.then_inc(b_y, 1)

            moe(0)
            attention_b()
            moe(1)


def kernel(**inputs):
    import concourse.bacc as bacc
    from concourse.bass_utils import run_bass_kernel_spmd

    a = {k.replace("L0_", ""): np.asarray(v) for k, v in inputs.items()}
    swap = np.arange(D) ^ 1

    def chunks(m):
        return np.ascontiguousarray(m.reshape(m.shape[0] // P, P, m.shape[1]).transpose(1, 0, 2))

    wq, wk, wv = (a["attn_a_w_qkv"][:, i * D:(i + 1) * D] for i in range(3))
    bq, bk, bv = (a["attn_a_b_qkv"][i * D:(i + 1) * D] for i in range(3))
    wa = chunks(np.concatenate([wk, wk[:, swap], wq, wq[:, swap], wv, a["attn_a_w_gate"], a["attn_a_w_lm_qkv"],
                                a["attn_a_w_lm_out"], a["attn_a_w_l2t_q"], a["attn_a_w_l2t_out"],
                                a["attn_a_w_lm_kv"], a["attn_a_w_out"]], axis=1))
    blm, bkv = a["attn_a_b_lm_qkv"], a["attn_a_b_lm_kv"]
    cols = [bk, bk[swap], bq, bq[swap], blm[0:D], blm[D:2 * D], a["attn_a_b_lm_out"], a["attn_a_b_l2t_q"],
            a["attn_a_b_l2t_out"], bkv[0:D]]
    ba = np.ascontiguousarray(np.concatenate(cols).reshape(B_TOTAL, P).T)
    ra = np.concatenate([bv, a["attn_a_b_gate"], blm[2 * D:], bkv[D:], a["attn_a_b_out"]])
    ra = np.ascontiguousarray(np.broadcast_to(ra, (P, R_TOTAL)))
    pool_q = a["attn_a_pool_q"].reshape(M, H, DH)
    pq = np.zeros((P, KC, HC, M), np.float32)
    for h in range(H):
        pq[DH * (h % HC):DH * (h % HC) + DH, h // HC, h % HC, :] = pool_q[:, h, :].T
    pq = pq.reshape(P, KC, HC * M)

    wb = chunks(a["attn_b_weight_qkv"].T)
    pb = chunks(a["attn_b_weight_proj"].T)
    wg = chunks(a["ffn_wg"].T)
    we = np.stack([np.stack([chunks(g.T).reshape(P, -1), chunks(u.T).reshape(P, -1), chunks(d.T).reshape(P, -1)])
                   for g, u, d in zip(*([a["ffn_sh_" + n]] + list(a["ffn_ex_" + n]) for n in ("gate", "up", "down")))])

    host = {"x": a["attn_a_x"], "const": CONST, "table": TABLE, "wa": wa, "pq": pq, "ba": ba, "ra": ra, "wb": wb, "pb": pb,
            "wg": wg, "we": we}
    nc = bacc.Bacc("TRN2", target_bir_lowering=False, num_devices=1)
    host = {n: np.ascontiguousarray(h) for n, h in host.items()}
    args = [nc.dram_tensor("in_" + n, h.shape, mybir.dt.from_np(h.dtype), kind="ExternalInput").ap()
            for n, h in host.items()]
    out = nc.dram_tensor("out", (B, L, D), F32, kind="ExternalOutput").ap()
    build(nc, *args, out)
    result = run_bass_kernel_spmd(nc, [{"in_" + n: h for n, h in host.items()}], core_ids=[0])
    return result.results[0]["out"]
```

```python
from contextlib import ExitStack

import numpy as np

import concourse.bass as bass
from concourse import mybir

F32 = mybir.dt.float32
BF16 = mybir.dt.bfloat16
I32 = mybir.dt.int32
U32 = mybir.dt.uint32
ALU = mybir.AluOpType
ACT = mybir.ActivationFunctionType
AX = mybir.AxisListType

P = 128
B, L, D = 4, 512, 256
T = L // P
NT = B * T
KC = D // P
LN_EPS = 1e-5

H, DH = 32, 8
S = 64
NB = L // S
M = 4
NL = NB * M
HC = P // DH
HQ = 4
C8 = H // HQ
SCALE = DH ** -0.5
NEG = -1e30
SUM_EPS = 1e-9
PARTS = 3 * HQ * DH
ROWS = PARTS + 2 * HQ

SEQ, BATCH = B, L
NH, NKV, HD = 16, 4, 16
GROUP = (NH // NKV + 2) * HD
QKVB = NKV * GROUP
SCALE_B = float(np.float32(1.0 / np.sqrt(HD)))

E, TOPK, FF = 8, 2, 512
NW = E + 1
FC = FF // P
ROUTED = (NT * P * TOPK - E) // P + E
TILES = NT + ROUTED
SLOTS = ROUTED * P
WCOL = KC * FF


def constants():
    p = np.arange(P)
    f = np.float32
    inv = (f(1.0) / f(10000.0) ** (np.arange(0, DH, 2, dtype=f) / f(DH))).astype(f)
    angle = np.arange(L, dtype=f)[None, :] * inv[(p % DH) // 2][:, None]
    sign = np.where(p % 2 == 0, f(-1), f(1))[:, None]
    tab = {"ident": np.eye(P), "cos": np.cos(angle), "sin": np.sin(angle) * sign}
    r = np.arange(PARTS)
    part, feat = r // (HQ * DH), r % (HQ * DH)
    for name, hi_parts in (("selk", (0, 1)), ("selq", (0, 2))):
        sel = np.zeros((P, 4, 2, PARTS))
        for a in range(4):
            is_hi = np.isin(part, hi_parts)
            sel[HQ * DH * a + feat, a, np.where(is_hi, 0, 1), r] = 1.0
        tab[name] = sel.reshape(P, -1)
    tab["headmask"] = np.where(p[:, None] < PARTS, (p[:, None] % (HQ * DH)) // DH == np.arange(HQ),
                               (p[:, None] - PARTS) // 2 == np.arange(HQ)) * 1.0
    k = np.arange(S)
    tab["causal"] = np.where(k[None, :] > (p % S)[:, None], NEG, 0.0)
    tab["causalT"] = np.where((p % S)[:, None] > k[None, :], NEG, 0.0)
    tab["bd16"] = (p[:, None] // DH == np.arange(HC)) * 1.0
    lm = np.arange(NL)
    la = np.zeros((P, NL))
    la[:NL] = np.where((lm // M)[:, None] < (lm // M)[None, :], NEG, 0.0)
    tab["lamask"] = la
    selg = np.zeros((P, C8, HQ, NL))
    for h in range(H):
        selg[h, h // HQ, h % HQ] = 1.0
        selg[H + h, h // HQ, h % HQ] = 1.0
    below = np.where(np.arange(NB)[:, None] > (lm // M)[None, :], 0.0, NEG)
    selg[2 * H:2 * H + NB] = below[:, None, None, :]
    tab["selg"] = selg.reshape(P, -1)
    oh = np.zeros((P, L))
    oh[2 * H:2 * H + NB] = np.arange(L)[None, :] // S == np.arange(NB)[:, None]
    oh[0:NB] = oh[2 * H:2 * H + NB]
    tab["onehot"] = oh
    gm = np.zeros((P, NL))
    gm[0:NB] = below
    tab["gmask"] = gm
    tab["valid"] = (p[:, None] >= S) * 1.0
    tab["tri"] = (p[:, None] < p[None, :]) * 1.0
    tab["ones"] = np.ones((P, P))
    tab["iota8"] = np.broadcast_to(np.arange(E), (P, E))
    e = np.arange(E)
    tab["tri8"] = np.broadcast_to((e[None, :] < e[:, None]).reshape(1, E * E) * 1.0, (P, E * E))
    tab["tilestart"] = np.broadcast_to(np.arange(ROUTED) * float(P), (P, ROUTED))
    def pack(names):
        at, off = {}, 0
        for name in names:
            at[name] = (off, tab[name].shape[1])
            off += tab[name].shape[1]
        return np.ascontiguousarray(np.concatenate([tab[n] for n in names], 1, dtype=np.float64).astype(f)), at

    return pack([n for n in tab if n not in CAST]), pack(CAST)


CAST = ("selk", "selq", "causal", "causalT", "selg", "onehot", "gmask")
(CONST, CONST_AT), (TABLE, TABLE_AT) = constants()

W_COLS = {"k": (0, 256), "ks": (256, 256), "q": (512, 256), "qs": (768, 256), "v": (1024, 256),
          "gate": (1280, 32), "lm": (1312, 768), "lm_out": (2080, 256), "l2t_q": (2336, 256),
          "l2t_out": (2592, 256), "lm_kv": (2848, 512), "out": (3360, 256)}
W_TOTAL = 3616
B_COLS = {"k": 0, "ks": 2, "q": 4, "qs": 6, "lq": 8, "lk": 10, "lm_out": 12, "l2t_q": 14, "l2t_out": 16, "gk": 18}
B_TOTAL = 20
R_COLS = {"v": (0, 256), "gate": (256, 32), "lv": (288, 256), "gv": (544, 256), "out": (800, 256)}
R_TOTAL = 1056


def build(nc, x_d, const_d, table_d, wa_d, pq_d, ba_d, ra_d, wb_d, pb_d, wg_d, we_d, out_d):
    with ExitStack() as ctx:
        x = ctx.enter_context(nc.sbuf_tensor("x", [P, NT, D], F32))
        cst = ctx.enter_context(nc.sbuf_tensor("cst", [P, CONST.shape[1]], F32))
        mean = ctx.enter_context(nc.sbuf_tensor("mean", [P, NT], F32))
        rstd = ctx.enter_context(nc.sbuf_tensor("rstd", [P, NT], F32))
        rows_s = nc.dram_tensor("rows_s", (NT * P, D), F32, kind="Internal").ap()
        slots_x = nc.dram_tensor("slots_x", (SLOTS, D), F32, kind="Internal").ap()
        slots_y = nc.dram_tensor("slots_y", (SLOTS, D), F32, kind="Internal").ap()
        banks = [ctx.enter_context(nc.psum_tensor(f"bank{i}", [P, 512], F32)) for i in range(8)]
        attention_a(nc, x, cst, mean, rstd, banks, x_d, const_d, table_d, wa_d, pq_d, ba_d, ra_d, slots_x)
        experts_and_attention_b(nc, x, cst, mean, rstd, banks, wb_d, pb_d, wg_d, we_d, rows_s, slots_x, slots_y, out_d)


def const(cst, name, rows=slice(0, P)):
    off, n = CONST_AT[name]
    return cst[rows, off:off + n]


def table(stage, name, rows=slice(0, P)):
    off, n = TABLE_AT[name]
    return stage[rows, off:off + n]


def attention_a(nc, x, cst, mean, rstd, bank, x_d, const_d, table_d, wa_d, pq_d, ba_d, ra_d, slots_x):
    with ExitStack() as ctx:
        def sb(name, shape, dt=F32):
            return ctx.enter_context(nc.sbuf_tensor(name, shape, dt))

        def sem(name):
            return ctx.enter_context(nc.semaphore(name))

        w = sb("wa", [P, KC, W_TOTAL])
        pq = sb("pq", [P, KC, HC * M])
        ba = sb("ba", [P, B_TOTAL])
        rb = sb("ra", [P, R_TOTAL])
        identb = sb("identb", [P, P], BF16)
        selk = sb("selk", [P, 4, 2, PARTS], BF16)
        selq = sb("selq", [P, 4, 2, PARTS], BF16)
        causal = sb("causal", [P, 8, S], BF16)
        causal_t = sb("causal_t", [P, 8, S], BF16)
        selg = sb("selg", [P, C8, P], BF16)
        onehot = sb("onehot", [NB, L], BF16)
        gmask = sb("gmask", [NB, HC, NL], BF16)
        zero = sb("zero", [P, D])
        st6 = sb("st6", [P, NT, 6])
        mv = sb("mv", [P, NT, 2])
        newton = sb("newton", [P, 2, NT])

        xn = sb("xn", [P, T, D])
        xnT = sb("xnT", [P, KC, L])
        rope_ab = sb("rope_ab", [P, 4, L])
        rope_a, rope_b = rope_ab[:, 0:2, :], rope_ab[:, 2:4, :]
        kqT = sb("kqT", [P, 4, L])
        hi = sb("hi", [P, 4, L], BF16)
        lo = sb("lo", [P, 4, L], BF16)
        ks = sb("ks", [P, C8, L], BF16)
        qs = sb("qs", [P, C8, L], BF16)
        kd = sb("kd", [P, 2, C8, HQ, P], BF16)
        qd = sb("qd", [P, C8, HQ, P], BF16)
        v = sb("v", [P, T, D])
        vd = sb("vd", [P, T, H, 32])
        gate = sb("gate", [P, 3, T * H])
        nm = sb("nm", [P, 2, H])
        nmh = sb("nmh", [P, 2, H, 2], BF16)
        pt = sb("pt", [P, 2, 8, S])
        r_sb = sb("r_sb", [P, C8, S])
        rec = sb("rec", [S, 2, 16])
        ol = sb("ol", [P, T, D])
        a_s = sb("a_s", [P, L])
        a_stat = sb("a_stat", [P, 4, NB])
        a_pt = sb("a_pt", [P, T, 2, P])
        a_m = sb("a_m", [P, NL, HC])
        lmT = sb("lmT", [P, 8, KC, NL])
        lmf, lq, lk, lo_T, lmf2, l2q, roT, lmf3 = range(8)
        gkT = sb("gkT", [P, KC, NL])
        lv = sb("lv", [NL, D])
        gv = sb("gv", [NL, D])
        lkbd = sb("lkbd", [P, KC, HC, NL])
        lvd = sb("lvd", [P, C8, 32])
        le = sb("le", [NL, H, NL])
        lstat = sb("lstat", [NL, 3, H])
        lpt = sb("lpt", [P, C8, NL])
        l2qbd = lkbd[:, :, :, :].rearrange("p c h k -> p c (h k)").rearrange("p c (n j) -> p c n j", n=NB)
        gkp = sb("gkp", [P, 2, KC, NL], BF16)
        gkd = sb("gkd", [PARTS, C8, HQ, NL], BF16)
        gvd = sb("gvd", [P, C8, 64])
        gnm = sb("gnm", [P, T, H])
        mm_ = sb("mm_", [P, L], BF16)
        pg = pt
        rg = rope_ab
        grec = sb("grec", [P, 2, H])
        og = xn
        oT = sb("oT", [P, 2, KC, P])

        stage = kd[:, :, :, :, :].rearrange("p a b c d -> p (a b c d)").bitcast(F32)
        d_w, d_x, x_in = sem("d_w"), [sem(f"d_x{i}") for i in range(B)], sem("x_in")
        c_ones, c_cast, c_stats, c_var, c_std = sem("c_ones"), sem("c_cast"), sem("c_stats"), sem("c_var"), sem("c_std")
        c_zero = sem("c_zero")
        c_rstd, batch_open = sem("c_rstd"), sem("batch_open")
        (xn_ready, xn_t, xnT_ready, proj, rope_mul, rope, hi_ready, lo_ready, v_ps, v_ready, vd_ready, gate_ps,
         gate_z, gate_e, gate_ready, stack_ps, stack, xb) = [sem(n) for n in (
             "xn_ready xn_t xnT_ready proj rope_mul rope hi_ready lo_ready v_ps v_ready vd_ready gate_ps "
             "gate_z gate_e gate_ready stack_ps stack xb").split()]
        (kd_ready, s_ps, smax, nmh_ready, nm_t, nm_row, qd_ready, st_ps, exps, pv, r_ready, r_t, rec_ready,
         ol_ready) = [sem(n) for n in (
             "kd_ready s_ps smax nmh_ready nm_t nm_row qd_ready st_ps exps pv r_ready r_t rec_ready "
             "ol_ready").split()]
        (at_s, at_sub, at_e, at_p, at_t, at_pt, at_o, at_red, lm_ps, lkbd_ready, lvd_ready, la_s, la_sub, la_e,
         la_p, la_t, la_pt, la_o, lo_ready_, lin_ps, lin_ready, gk_parts, gk_stack, gkd_ready, gvd_ready) = [sem(n) for n in (
             "at_s at_sub at_e at_p at_t at_pt at_o at_red lm_ps lkbd_ready lvd_ready la_s la_sub la_e "
             "la_p la_t la_pt la_o lo_T_ready lin_ps lin_ready gk_parts gk_stack gkd_ready gvd_ready").split()]
        (sg, gmax, gm_t, mm_hi, mm_lo, sgt, gexp, gpv, rg_ready, rg_t, og_ready, o_ready, o_t, oT_ready, y_ps,
         x_new) = [sem(n) for n in (
             "sg gmax gm_t mm_hi mm_lo sgt gexp gpv rg_ready rg_t og_ready o_ready o_t oT_ready y_ps "
             "x_new").split()]
        dve_step, pool_step = sem("dve_step"), sem("pool_step")

        ident = const(cst, "ident")
        bank5b = bank[5][:, :].bitcast(BF16)
        block = ctx.enter_context(nc.Block())

        def wcol(name, k, lo_=0, n=None):
            off, full = W_COLS[name]
            return w[:, k, off + lo_:off + lo_ + (full if n is None else n)]

        def bcol(name, c):
            return ba[:, B_COLS[name] + c:B_COLS[name] + c + 1]

        def row(name, rows=slice(0, P)):
            off, n = R_COLS[name]
            return rb[rows, off:off + n]

        @block.sync
        def _(sp):
            xv = x_d.rearrange("b (t p) d -> b p t d", p=P)
            for b in range(B):
                sp.dma_start(x[:, b * T:(b + 1) * T, :], xv[b]).then_inc(d_x[b], 16)
                if b == 0:
                    sp.dma_start(cst[:, :], const_d).then_inc(d_w, 16)
                    sp.dma_start(stage[:, 0:TABLE.shape[1]], table_d).then_inc(d_w, 16)
                    sp.dma_start(rb[:, :], ra_d).then_inc(d_w, 16)
                    sp.dma_start(ba[:, :], ba_d).then_inc(d_w, 16)
                    sp.dma_start(pq[:, :, :], pq_d).then_inc(d_w, 16)
                    sp.dma_start(w[:, :, :], wa_d).then_inc(d_w, 16)
            sp.wait_ge(c_zero, 1)
            sp.dma_start(slots_x.rearrange("(j p) d -> p j d", p=P),
                         zero[:, :].unsqueeze(1).broadcast_to([P, ROUTED, D])).then_inc(x_in, 16)
            sp.wait_ge(x_in, 16)

        @block.gpsimd
        def _(pool):
            pool.memset(zero[:, :], 0.0).then_inc(c_zero, 1)
            n = 0
            for buf in (vd[:, :, :, :], a_pt[:, :, :, :], lvd[:, :, :], gvd[:, :, :]):
                pool.memset(buf, 0.0).then_inc(c_ones, 1)
                n += 1
            pool.wait_ge(d_w, 96)
            def projections(b):
                for t in range(T):
                    pool.wait_ge(xn_ready, b * T + t + 1)
                    pool.tensor_tensor(x[:, b * T + t, :], x[:, b * T + t, :], row("out"), ALU.add).then_inc(xb, 1)
                for r in range(4):
                    pool.wait_ge(rope_mul, b * 8 + 2 * r + 2)
                    pool.tensor_tensor(kqT[:, r, :], rope_a[:, r % 2, :], rope_b[:, r % 2, :],
                                       ALU.add).then_inc(rope, 1)
                    pool.wait_ge(hi_ready, b * 4 + r + 1)
                    pool.tensor_tensor(lo[:, r, :], kqT[:, r, :], hi[:, r, :], ALU.subtract).then_inc(lo_ready, 1)

            def local_share(b):
                pool.wait_ge(gate_ready, b + 1)
                for t in range(T):
                    pool.wait_ge(ol_ready, b * 16 + 4 * t + 4)
                    olv = ol[:, t, :].rearrange("p (h d) -> p h d", d=DH)
                    g = gate[:, 0, t * H:(t + 1) * H].unsqueeze(2).broadcast_to([P, H, DH])
                    pool.tensor_tensor(olv, olv, g, ALU.mult).then_inc(o_ready, 1)

            projections(0)
            with pool.Fori(0, B - 1) as b:
                local_share(b)
                projections(b + 1)
            local_share(B - 1)

        @block.scalar
        def _(act):
            act.wait_ge(d_w, 96)
            act.activation(identb[:, :], ident, ACT.Copy).then_inc(c_cast, 1)
            for dst, name in ((selk, "selk"), (selq, "selq")):
                act.activation(dst[:, :, :, :].rearrange("p a b c -> p (a b c)"), table(stage, name),
                               ACT.Copy).then_inc(c_cast, 1)
            for dst, name in ((causal, "causal"), (causal_t, "causalT")):
                act.activation(dst[:, :, :], table(stage, name).unsqueeze(1).broadcast_to([P, 8, S]),
                               ACT.Copy).then_inc(c_cast, 1)
            act.activation(selg[:, :, :].rearrange("p a b -> p (a b)"), table(stage, "selg"), ACT.Copy).then_inc(c_cast, 1)
            act.activation(onehot[:, :], table(stage, "onehot", slice(0, NB)), ACT.Copy).then_inc(c_cast, 1)
            act.activation(gmask[:, :, :], table(stage, "gmask", slice(0, NB)).unsqueeze(1).broadcast_to([NB, HC, NL]),
                           ACT.Copy).then_inc(c_cast, 1)
            act.activation(mm_[2 * H:2 * H + NB, :], table(stage, "onehot", slice(2 * H, 2 * H + NB)),
                           ACT.Copy).then_inc(c_cast, 1)
            act.wait_ge(c_var, 1)
            act.activation(newton[:, 0, :], newton[:, 0, :], ACT.Sqrt).then_inc(c_std, 1)

            def rows_turned(b):
                for p in range(2):
                    act.wait_ge(xn_t, b * T + 2 * p + 2)
                    act.activation(xnT[:, :, 2 * p * P:(2 * p + 2) * P].rearrange("p k (t c) -> p t k c", t=2),
                                   bank[p][:, :].rearrange("p (t k c) -> p t k c", t=2, k=KC),
                                   ACT.Copy).then_inc(xnT_ready, 1)

            def high_part(b, r):
                act.wait_ge(rope, b * 4 + r + 1)
                act.activation(hi[:, r, :], kqT[:, r, :], ACT.Copy).then_inc(hi_ready, 1)

            def values(b, t):
                act.wait_ge(v_ready, b * T + t + 1)
                vv = v[:, t, :].rearrange("p (h d) -> p h d", d=DH)
                for blk in range(2):
                    rows = slice(S * blk, S * blk + S)
                    act.activation(vd[rows, t, :, 16 * blk:16 * blk + DH], vv[rows], ACT.Copy).then_inc(vd_ready, 1)

            rows_turned(0)
            for r in range(4):
                high_part(0, r)
            for t in range(T):
                values(0, t)

            def batch(b, last):
                act.wait_ge(batch_open, b + 1)
                act.wait_ge(gate_z, b + 1)
                act.activation(gate[:, 1, :], gate[:, 0, :], ACT.Exp, scale=-1.0).then_inc(gate_e, 1)
                for s in range(16):
                    act.wait_ge(stack_ps, b * 16 + s + 1)
                    dst = ks if s < 8 else qs
                    act.activation(dst[0:PARTS, s % 8, :], bank[s % 4][0:PARTS, :], ACT.Copy).then_inc(stack, 1)

                def attend_exp(a):
                    act.wait_ge(at_sub, b * 2 + a + 1)
                    act.activation(a_s[:, :], a_s[:, :], ACT.Exp, scale=SCALE).then_inc(at_e, 1)

                def attend_turned(a):
                    act.wait_ge(at_t, b * 2 + a + 1)
                    for blk in range(2):
                        rows = slice(S * blk, S * blk + S)
                        act.activation(a_pt[rows, :, blk, :],
                                       bank[7][rows, :].rearrange("p (t c) -> p t c", t=T),
                                       ACT.Copy).then_inc(at_pt, 1)

                def la_exp():
                    act.wait_ge(la_sub, b * 2 + 2)
                    act.activation(le[:, :, :], le[:, :, :], ACT.Exp, scale=SCALE).then_inc(la_e, 1)

                def la_turned():
                    act.wait_ge(la_t, b + 1)
                    act.activation(lpt[:, :, :].rearrange("p c q -> p (c q)"), bank[7][:, 0:C8 * NL],
                                   ACT.Copy).then_inc(la_pt, 1)

                def la_out():
                    act.wait_ge(la_o, b + 1)
                    act.activation(lmT[:, lo_T, :, :].rearrange("p c q -> p (c q)"), bank[7][:, 0:KC * NL],
                                   ACT.Copy).then_inc(lo_ready_, 1)

                def exp_unit(t, g):
                    u = 4 * t + g
                    act.wait_ge(st_ps, b * 16 + u + 1)
                    if u >= 2:
                        act.wait_ge(pv, b * 16 + u - 1)
                    act.activation(pt[:, g % 2, :, :].rearrange("p h q -> p (h q)"), bank[2 + g % 2][:, :],
                                   ACT.Exp, scale=SCALE).then_inc(exps, 1)

                def weighted_out(t):
                    act.wait_ge(pv, b * 16 + 4 * t + 4)
                    if t >= 1:
                        act.wait_ge(r_t, b * 8 + 2 * t)
                    act.activation(r_sb[:, :, :].rearrange("p c q -> p (c q)"), bank[4][:, :],
                                   ACT.Copy).then_inc(r_ready, 1)

                landmarks = {1: lambda: attend_turned(0), 6: la_exp, 8: la_turned, 9: la_out,
                             12: lambda: attend_exp(1), 14: lambda: attend_turned(1)}
                attend_exp(0)
                for t in range(T):
                    act.wait_ge(nm_t, b * T + t + 1)
                    act.activation(qs[PARTS:ROWS, :, t * P:(t + 1) * P],
                                   bank5b[0:2 * HQ, :].rearrange("p (c q) -> p c q", c=C8),
                                   ACT.Copy).then_inc(nm_row, 1)
                    if t >= 1:
                        weighted_out(t - 1)
                    for g in range(4):
                        exp_unit(t, g)
                        if 4 * t + g in landmarks:
                            landmarks[4 * t + g]()
                weighted_out(T - 1)
                if not last:
                    rows_turned(b + 1)
                    for r in range(3):
                        high_part(b + 1, r)
                act.wait_ge(gm_t, b + 1)
                act.activation(mm_[0:H, :], bank[4][0:H, :], ACT.Copy).then_inc(mm_hi, 1)
                for c in range(C8):
                    act.wait_ge(sgt, b * C8 + c + 1)
                    if c >= 2:
                        act.wait_ge(gpv, b * C8 + c - 1)
                    act.activation(pg[:, c % 2, :, :].rearrange("p h q -> p (h q)"), bank[c % 4][:, :],
                                   ACT.Exp, scale=SCALE).then_inc(gexp, 1)
                    if c == 1 and not last:
                        high_part(b + 1, 3)
                for j in range(4):
                    act.wait_ge(gpv, b * C8 + 2 * j + 2)
                    act.activation(rg[:, j, :], bank[4 + j][:, :], ACT.Copy).then_inc(rg_ready, 1)
                for t in range(T):
                    act.wait_ge(o_t, b * T + t + 1)
                    if t >= 2:
                        act.wait_ge(y_ps, b * T + t - 1)
                    act.activation(oT[:, t % 2, :, :].rearrange("p k c -> p (k c)"), bank[4 + t % 2][:, 0:KC * P],
                                   ACT.Copy).then_inc(oT_ready, 1)
                if not last:
                    for t in range(T):
                        values(b + 1, t)

            with act.Fori(0, B - 1) as b:
                batch(b, False)
            batch(B - 1, True)

        @block.vector
        def _(dve):
            def link(ins, b, per, n):
                ins.then_inc(dve_step, 1)
                dve.wait_ge(dve_step, b * per + n)

            dve.wait_ge(c_ones, 4)
            dve.memset(vd[0:S, :, :, 8:9], 1.0).then_inc(c_ones, 1)
            dve.memset(vd[S:P, :, :, 24:25], 1.0).then_inc(c_ones, 1)
            for i in range(HQ):
                dve.memset(gvd[32 * i:32 * i + 32, :, 32 + i:33 + i], 1.0).then_inc(c_ones, 1)
            dve.memset(ks[PARTS:P, :, :], 1.0).then_inc(c_ones, 1)
            for b in range(B):
                dve.wait_ge(d_x[b], 16)
                for t in range(b * T, (b + 1) * T):
                    dve.bn_stats(st6[:, t, :], x[:, t, :]).then_inc(c_stats, 1)
            for t in range(NT):
                dve.wait_ge(c_stats, t + 1)
                dve.bn_aggr(mv[:, t, :], st6[:, t, :]).then_inc(c_stats, 1)
            dve.wait_ge(c_stats, 2 * NT)
            dve.tensor_copy(mean[:, :], mv[:, :, 0]).then_inc(c_rstd, 1)
            dve.tensor_scalar(newton[:, 0, :], mv[:, :, 1], LN_EPS, None, ALU.add).then_inc(c_var, 1)
            dve.wait_ge(c_std, 1)
            dve.reciprocal(rstd[:, :], newton[:, 0, :]).then_inc(c_rstd, 1)
            dve.wait_ge(c_rstd, 2)
            dve.wait_ge(c_ones, 11)
            dve.wait_ge(c_cast, 9)
            dve.memset(newton[:, 1, 0:1], 0.0).then_inc(batch_open, 1)
            def rows(b):
                for t in range(T):
                    dve.tensor_scalar(xn[:, t, :], x[:, b * T + t, :],
                                      mean[:, bass.ds(b * T + t, 1)],
                                      rstd[:, bass.ds(b * T + t, 1)], ALU.subtract, ALU.mult).then_inc(xn_ready, 1)

            def rope_products(b, j):
                r = j // 2
                if r >= 2:
                    dve.wait_ge(rope, b * 4 + r - 1)
                dve.wait_ge(proj, b * 8 + j + 1)
                name, c = ("k", "k", "q", "q")[r], r % 2
                buf, name, tab = ((rope_a, name, "cos"), (rope_b, name + "s", "sin"))[j % 2]
                dve.scalar_tensor_tensor(buf[:, r % 2, :], bank[5 + j % 2][:, :], bcol(name, c), const(cst, tab),
                                         ALU.add, ALU.mult).then_inc(rope_mul, 1)

            def values(b, t):
                dve.wait_ge(v_ps, b * T + t + 1)
                dve.tensor_tensor(v[:, t, :], bank[6 + t % 2][:, 0:D], row("v"), ALU.add).then_inc(v_ready, 1)

            rows(0)
            for j in range(8):
                rope_products(0, j)
            for t in range(T):
                values(0, t)

            def batch(b, last):
                count = [0]
                PER = DVE_LINKS_A

                def step(ins):
                    count[0] += 1
                    link(ins, b, PER, count[0])

                dve.wait_ge(batch_open, b + 1)
                dve.wait_ge(gate_ps, b + 1)
                dve.tensor_tensor(gate[:, 0, :].rearrange("p (t h) -> p t h", t=T),
                                  bank[5][:, 0:T * H].rearrange("p (t h) -> p t h", t=T),
                                  row("gate").unsqueeze(1).broadcast_to([P, T, H]), ALU.add).then_inc(gate_z, 1)
                dve.wait_ge(gate_e, b + 1)
                step(dve.tensor_scalar(gate[:, 0, :], gate[:, 1, :], 1.0, None, ALU.add))
                step(dve.reciprocal(gate[:, 2, :], gate[:, 0, :]))
                dve.tensor_scalar(gate[:, 0, :], gate[:, 2, :], -1.0, 1.0, ALU.mult, ALU.add).then_inc(gate_ready, 1)

                bd = const(cst, "bd16")
                hm = const(cst, "headmask")

                sv = bank[7][:, :].rearrange("p (n s) -> p n s", n=NB)
                av = a_s[:, :].rearrange("p (n s) -> p n s", n=NB)

                def attend_max(a):
                    dve.wait_ge(at_s, b * 2 + a + 1)
                    step(dve.tensor_reduce(a_stat[:, 0, :], sv, AX.X, ALU.max))
                    dve.tensor_tensor(av, sv, a_stat[:, 0, :].unsqueeze(2).broadcast_to([P, NB, S]),
                                      ALU.subtract).then_inc(at_sub, 1)

                def attend_norm(a):
                    dve.wait_ge(at_e, b * 2 + a + 1)
                    step(dve.tensor_reduce(a_stat[:, 1, :], av, AX.X, ALU.add))
                    step(dve.reciprocal(a_stat[:, 2, :], a_stat[:, 1, :]))
                    dve.tensor_tensor(av, av, a_stat[:, 2, :].unsqueeze(2).broadcast_to([P, NB, S]),
                                      ALU.mult).then_inc(at_p, 1)

                def attend_out(a, dst, c):
                    dve.wait_ge(at_o, b * 4 + a * 2 + c + 1)
                    step(dve.tensor_tensor(
                        a_m[:, :, :].rearrange("p (n m) h -> p n h m", n=NB),
                        bank[7][:, :].rearrange("p (n h m) -> p n h m", n=NB, h=HC),
                        bd.unsqueeze(1).unsqueeze(3).broadcast_to([P, NB, HC, M]), ALU.mult))
                    dve.tensor_reduce(lmT[:, dst, c, :], a_m[:, :, :], AX.X, ALU.add).then_inc(at_red, 1)

                def spread(dst, src, value, signal):
                    for i in range(HQ):
                        dve.tensor_copy(dst[32 * i:32 * i + 32, :, DH * i:DH * i + DH],
                                        src[:, :].rearrange("k (c i d) -> k c i d", i=HQ, d=DH)[:, :, i, :])\
                           .then_inc(signal, 1)

                def block_diagonal(dst, src, signal):
                    for c in range(KC):
                        dve.tensor_tensor(dst[:, c, :, :], src[c].unsqueeze(1).broadcast_to([P, HC, NL]),
                                          bd.unsqueeze(2).broadcast_to([P, HC, NL]), ALU.mult).then_inc(signal, 1)

                def landmarks_qkv():
                    dve.wait_ge(lm_ps, b * 2 + 1)
                    for c in range(KC):
                        dve.tensor_scalar(lmT[:, lq, c, :], bank[7][:, c * NL:(c + 1) * NL], bcol("lq", c), None,
                                          ALU.add).then_inc(lkbd_ready, 1)
                    for c in range(KC):
                        dve.tensor_scalar(lmT[:, lk, c, :], bank[7][:, (2 + c) * NL:(3 + c) * NL], bcol("lk", c), None,
                                          ALU.add).then_inc(lkbd_ready, 1)
                    step(dve.tensor_tensor(lv[:, :], bank[7][0:NL, P:P + D], row("lv", slice(0, NL)), ALU.add))
                    block_diagonal(lkbd, [lmT[:, lk, c, :] for c in range(KC)], lkbd_ready)
                    spread(lvd, lv, None, lvd_ready)

                def la_max(c):
                    dve.wait_ge(la_s, b * 2 + c + 1)
                    lsv = bank[7][0:NL, :].rearrange("q (h k) -> q h k", h=HC)
                    step(dve.tensor_reduce(lstat[:, 0, HC * c:HC * c + HC], lsv, AX.X, ALU.max))
                    dve.tensor_tensor(le[:, HC * c:HC * c + HC, :], lsv,
                                      lstat[:, 0, HC * c:HC * c + HC].unsqueeze(2).broadcast_to([NL, HC, NL]),
                                      ALU.subtract).then_inc(la_sub, 1)

                def la_norm():
                    dve.wait_ge(la_e, b + 1)
                    step(dve.tensor_reduce(lstat[:, 1, :], le[:, :, :], AX.X, ALU.add))
                    step(dve.reciprocal(lstat[:, 2, :], lstat[:, 1, :]))
                    dve.tensor_tensor(le[:, :, :], le[:, :, :],
                                      lstat[:, 2, :].unsqueeze(2).broadcast_to([NL, H, NL]), ALU.mult).then_inc(la_p, 1)

                def linear(n, name, dst, add):
                    dve.wait_ge(lin_ps, b * 3 + n + 1)
                    for c in range(KC):
                        src = bank[7][:, c * NL:(c + 1) * NL]
                        if add is None:
                            ins = dve.tensor_scalar(lmT[:, dst, c, :], src, bcol(name, c), None, ALU.add)
                        else:
                            ins = dve.scalar_tensor_tensor(lmT[:, dst, c, :], src, bcol(name, c), lmT[:, add, c, :],
                                                           ALU.add, ALU.add)
                        ins.then_inc(lin_ready, 1)

                def queries_to_blocks():
                    dve.wait_ge(lin_ready, b * 8 + 4)
                    for c in range(KC):
                        dve.tensor_tensor(l2qbd[:, c, :, :].rearrange("p n (h m) -> p n h m", h=HC),
                                          lmT[:, l2q, c, :].rearrange("p (n m) -> p n m", n=NB).unsqueeze(2)
                                          .broadcast_to([P, NB, HC, M]),
                                          bd.unsqueeze(1).unsqueeze(3).broadcast_to([P, NB, HC, M]),
                                          ALU.mult).then_inc(lin_ready, 1)

                def landmarks_kv():
                    dve.wait_ge(lm_ps, b * 2 + 2)
                    for c in range(KC):
                        ins = dve.tensor_scalar(gkT[:, c, :], bank[7][:, c * NL:(c + 1) * NL], bcol("gk", c), None,
                                                ALU.add)
                        step(ins)
                    step(dve.tensor_tensor(gv[:, :], bank[7][0:NL, P:P + D], row("gv", slice(0, NL)), ALU.add))
                    step(dve.tensor_copy(gkp[:, 0, :, :], gkT[:, :, :]))
                    dve.tensor_tensor(gkp[:, 1, :, :], gkT[:, :, :], gkp[:, 0, :, :], ALU.subtract)\
                       .then_inc(gk_parts, 1)
                    spread(gvd, gv, None, gvd_ready)
                    if not last:
                        rope_products(b + 1, 0)
                    dve.wait_ge(gk_stack, b + 1)
                    dve.tensor_tensor(gkd[:, :, :, :], bank[7][0:PARTS, 0:C8 * NL].rearrange("p (c k) -> p c k", c=C8)
                                      .unsqueeze(2).broadcast_to([PARTS, C8, HQ, NL]),
                                      hm[0:PARTS, :].unsqueeze(1).unsqueeze(3).broadcast_to([PARTS, C8, HQ, NL]),
                                      ALU.mult).then_inc(gkd_ready, 1)

                def expand_k(t):
                    if t == 0:
                        dve.wait_ge(stack, b * 16 + 16)
                    if t >= 2:
                        dve.wait_ge(s_ps, b * 16 + 4 * (t - 1))
                    for i in range(HQ):
                        dve.tensor_scalar(kd[0:PARTS, t % 2, :, i, :], ks[0:PARTS, :, t * P:(t + 1) * P],
                                          hm[0:PARTS, i:i + 1], None, ALU.mult).then_inc(kd_ready, 1)

                def maximum(t, g):
                    dve.wait_ge(s_ps, b * 16 + 4 * t + g + 1)
                    dve.tensor_reduce(nm[:, t % 2, 8 * g:8 * g + 8],
                                      bank[g % 2][:, :].rearrange("p (h k) -> p h k", h=8), AX.X, ALU.max,
                                      negate=True).then_inc(smax, 1)
                    if g == 3:
                        dve.wait_ge(smax, b * 16 + 4 * t + 4)
                        step(dve.tensor_copy(nmh[:, t % 2, :, 0], nm[:, t % 2, :]))
                        dve.tensor_tensor(nmh[:, t % 2, :, 1], nm[:, t % 2, :], nmh[:, t % 2, :, 0],
                                          ALU.subtract).then_inc(nmh_ready, 1)

                def expand_q(t):
                    dve.wait_ge(nm_row, b * T + t + 1)
                    if t >= 1:
                        dve.wait_ge(st_ps, b * 16 + 4 * t)
                    for i in range(HQ):
                        dve.tensor_scalar(qd[0:ROWS, :, i, :], qs[0:ROWS, :, t * P:(t + 1) * P],
                                          hm[0:ROWS, i:i + 1], None, ALU.mult).then_inc(qd_ready, 1)

                def normalise(t, hf):
                    dve.wait_ge(r_t, b * 8 + 2 * t + hf + 1)
                    rv = bank[6][0:S, :].rearrange("q (h c) -> q h c", c=32)
                    for blk in range(2):
                        dve.reciprocal(rec[:, blk, :], rv[:, :, 16 * blk + DH]).then_inc(rec_ready, 1)
                    for blk in range(2):
                        dve.wait_ge(rec_ready, b * 16 + 4 * t + 2 * hf + blk + 1)
                        dve.tensor_tensor(
                            ol[S * blk:S * blk + S, t, hf * P:(hf + 1) * P].rearrange("q (h d) -> q h d", d=DH),
                            rv[:, :, 16 * blk:16 * blk + DH],
                            rec[:, blk, :].unsqueeze(2).broadcast_to([S, 16, DH]), ALU.mult).then_inc(ol_ready, 1)

                def queries():
                    linear(1, "l2t_q", l2q, None)
                    queries_to_blocks()

                landmarks = {0: lambda: attend_norm(0), 2: lambda: attend_out(0, lmf, 0),
                             3: lambda: attend_out(0, lmf, 1), 4: landmarks_qkv, 5: lambda: la_max(0),
                             6: lambda: la_max(1), 7: la_norm, 10: lambda: linear(0, "lm_out", lmf2, lmf), 11: queries,
                             12: lambda: attend_max(1), 13: lambda: attend_norm(1),
                             15: lambda: attend_out(1, roT, 0)}
                if not last:
                    landmarks[14] = lambda: rows(b + 1)

                expand_k(0)
                attend_max(0)
                expand_k(1)
                for g in range(4):
                    maximum(0, g)
                for t in range(T):
                    if t + 1 < T:
                        maximum(t + 1, 0)
                        maximum(t + 1, 1)
                    expand_q(t)
                    for g in range(4):
                        if t >= 1 and g < 2:
                            normalise(t - 1, g)
                        if 1 <= g < 3 and t + 1 < T:
                            maximum(t + 1, g + 1)
                        if g == 3 and t + 2 < T:
                            expand_k(t + 2)
                        if 4 * t + g in landmarks:
                            landmarks[4 * t + g]()
                normalise(T - 1, 0)
                attend_out(1, roT, 1)
                normalise(T - 1, 1)
                linear(2, "l2t_out", lmf3, lmf2)

                landmarks_kv()
                if not last:
                    rope_products(b + 1, 1)
                for t in range(T):
                    for c in range(KC):
                        dve.wait_ge(sg, b * 8 + 2 * t + c + 1)
                        dve.tensor_reduce(gnm[:, t, HC * c:HC * c + HC],
                                          bank[2 * (t % 2) + c][:, :].rearrange("p (h k) -> p h k", h=HC), AX.X,
                                          ALU.max, negate=True).then_inc(gmax, 1)
                    if not last:
                        rope_products(b + 1, 2 + t)
                dve.wait_ge(gmax, b * 9 + 2)
                dve.tensor_scalar(gnm[:, 0, :], gnm[:, 0, :], const(cst, "valid"), None, ALU.mult).then_inc(gmax, 1)
                dve.wait_ge(mm_hi, b + 1)
                dve.tensor_tensor(mm_[H:2 * H, :], bank[4][0:H, :], mm_[0:H, :], ALU.subtract).then_inc(mm_lo, 1)
                if not last:
                    rope_products(b + 1, 6)
                    rope_products(b + 1, 7)
                for t in range(T):
                    dve.wait_ge(rg_t, b * T + t + 1)
                    gvw = bank[t][:, :].rearrange("p (c j) -> p c j", c=C8)
                    step(dve.tensor_scalar(grec[:, 0, :].rearrange("p (c i) -> p c i", c=C8), gvw[:, :, 32:36],
                                           SUM_EPS, None, ALU.max))
                    step(dve.reciprocal(grec[:, 1, :], grec[:, 0, :]))
                    step(dve.tensor_tensor(grec[:, 1, :], grec[:, 1, :], gate[:, 2, t * H:(t + 1) * H], ALU.mult))
                    dve.tensor_tensor(og[:, t, :].rearrange("p (c i d) -> p c i d", c=C8, i=HQ),
                                      gvw[:, :, 0:32].rearrange("p c (i d) -> p c i d", i=HQ),
                                      grec[:, 1, :].rearrange("p (c i) -> p c i", c=C8).unsqueeze(3)
                                      .broadcast_to([P, C8, HQ, DH]), ALU.mult).then_inc(og_ready, 1)
                for t in range(T):
                    if not last and t < 2:
                        values(b + 1, 2 * t)
                        values(b + 1, 2 * t + 1)
                    dve.wait_ge(y_ps, b * T + t + 1)
                    dve.wait_ge(xb, b * T + t + 1)
                    dve.tensor_tensor(x[:, b * T + t, :], bank[4 + t % 2][:, D:2 * D], x[:, b * T + t, :],
                                      ALU.add).then_inc(x_new, 1)
                dve.wait_ge(x_new, b * T + T)
                dve.memset(newton[:, 1, 0:1], 0.0).then_inc(batch_open, 1)
                assert count[0] == PER, count[0]

            with dve.Fori(0, B - 1) as b:
                batch(b, False)
            batch(B - 1, True)

        @block.tensor
        def _(pe):
            def mm(out, lhs, rhs, start=True, stop=True):
                return pe.matmul(out, lhs, rhs, start=start, stop=stop, skip_group_check=True)

            pe.wait_ge(d_w, 96)
            pe.wait_ge(c_cast, 9)

            def rows_turned(b):
                for t in range(T):
                    pe.wait_ge(xn_ready, b * T + t + 1)
                    for k in range(KC):
                        ins = pe.transpose(bank[t // 2][:, (t % 2) * 256 + k * P:(t % 2) * 256 + (k + 1) * P],
                                           xn[:, t, k * P:(k + 1) * P], ident)
                    ins.then_inc(xn_t, 1)

            def projection(b, j):
                if j == 0:
                    pe.wait_ge(xnT_ready, b * 2 + 2)
                if j >= 2:
                    pe.wait_ge(rope_mul, b * 8 + j - 1)
                name, c = ("k", "ks", "k", "ks", "q", "qs", "q", "qs")[j], j // 2 % 2
                for k in range(KC):
                    ins = mm(bank[5 + j % 2][:, :], wcol(name, k, c * P, P), xnT[:, k, :], k == 0, k == KC - 1)
                ins.then_inc(proj, 1)

            def values(b, t):
                if t >= 2:
                    pe.wait_ge(v_ready, b * T + t - 1)
                for k in range(KC):
                    ins = mm(bank[6 + t % 2][:, 0:D], xnT[:, k, t * P:(t + 1) * P], wcol("v", k),
                             k == 0, k == KC - 1)
                ins.then_inc(v_ps, 1)

            rows_turned(0)
            for j in range(8):
                projection(0, j)
            pe.wait_ge(rope_mul, 8)
            for t in range(T):
                values(0, t)

            def batch(b, last):
                pe.wait_ge(batch_open, b + 1)
                for t in range(T):
                    for k in range(KC):
                        ins = mm(bank[5][:, t * H:(t + 1) * H], xnT[:, k, t * P:(t + 1) * P], wcol("gate", k),
                                 k == 0, k == KC - 1)
                ins.then_inc(gate_ps, 1)
                for s in range(16):
                    r = s // 4
                    pe.wait_ge(lo_ready, b * 4 + r + 1)
                    if s >= 4:
                        pe.wait_ge(stack, b * 16 + s - 3)
                    sel = selk if s < 8 else selq
                    mm(bank[s % 4][0:PARTS, :], sel[:, s % 4, 0, :], hi[:, r, :], True, False)
                    mm(bank[s % 4][0:PARTS, :], sel[:, s % 4, 1, :], lo[:, r, :], False, True).then_inc(stack_ps, 1)

                def attend_scores(a):
                    if a == 0:
                        pe.wait_ge(rope, b * 4 + 4)
                        pe.wait_ge(v_ready, b * T + T)
                        for c in range(KC):
                            ins = mm(bank[7][64 * c:64 * c + 64, :], pq[:, c, :], kqT[:, c, :])
                    else:
                        pe.wait_ge(lin_ready, b * 8 + 6)
                        for n in range(NB):
                            for c in range(KC):
                                ins = mm(bank[7][64 * c:64 * c + 64, n * S:(n + 1) * S], l2qbd[:, c, n, :],
                                         kqT[:, c, n * S:(n + 1) * S])
                    ins.then_inc(at_s, 1)

                def attend_turn(a):
                    pe.wait_ge(at_p, b * 2 + a + 1)
                    for t in range(T):
                        ins = pe.transpose(bank[7][:, t * P:(t + 1) * P], a_s[:, t * P:(t + 1) * P], ident)
                    ins.then_inc(at_t, 1)

                def attend_out(a, c):
                    pe.wait_ge(at_pt, b * 4 + 2 * a + 2)
                    if c:
                        pe.wait_ge(at_red, b * 4 + 2 * a + 1)
                    for t in range(T):
                        ins = mm(bank[7][:, t * P:(t + 1) * P], v[:, t, c * P:(c + 1) * P],
                                 a_pt[:, t, :, 64 * c:64 * c + 64])
                    ins.then_inc(at_o, 1)

                def project(name, src, lo_, n, chunks):
                    for c in range(chunks):
                        for k in range(KC):
                            ins = mm(bank[7][:, c * NL:(c + 1) * NL], wcol(name, k, lo_ + c * P, P), lmT[:, src, k, :],
                                     k == 0, k == KC - 1)
                    return ins

                def rows(name, src, lo_):
                    for k in range(KC):
                        ins = mm(bank[7][0:NL, P:P + D], lmT[:, src, k, :], wcol(name, k, lo_, D), k == 0, k == KC - 1)
                    return ins

                def landmarks_qkv():
                    pe.wait_ge(at_red, b * 4 + 2)
                    project("lm", lmf, 0, P, 4)
                    rows("lm", lmf, 2 * D).then_inc(lm_ps, 1)

                def la_scores(c):
                    if c == 0:
                        pe.wait_ge(lkbd_ready, b * 6 + 6)
                        pe.wait_ge(lvd_ready, b * 4 + 4)
                    else:
                        pe.wait_ge(la_sub, b * 2 + 1)
                    mm(bank[7][0:NL, :], lmT[:, lq, c, :], lkbd[:, c, :, :], True, False)
                    mm(bank[7][0:NL, :], ident[0:NL, 0:NL],
                       const(cst, "lamask", slice(0, NL)).unsqueeze(1).broadcast_to([NL, HC, NL]),
                       False, True).then_inc(la_s, 1)

                def la_turn():
                    pe.wait_ge(d_w, 96)
                    pe.wait_ge(la_p, b + 1)
                    for c in range(C8):
                        ins = pe.transpose(bank[7][:, c * NL:(c + 1) * NL],
                                           le[:, HQ * c:HQ * c + HQ, :].rearrange("q h k -> q (h k)"),
                                           ident[0:NL, 0:NL])
                    ins.then_inc(la_t, 1)

                def la_weighted():
                    pe.wait_ge(la_pt, b + 1)
                    for c in range(C8):
                        i = c % 4
                        ins = mm(bank[7][32 * i:32 * i + 32, (c // 4) * NL:(c // 4 + 1) * NL], lvd[:, c, :],
                                 lpt[:, c, :])
                    ins.then_inc(la_o, 1)

                def la_project():
                    pe.wait_ge(lo_ready_, b + 1)
                    project("lm_out", lo_T, 0, P, KC).then_inc(lin_ps, 1)

                def queries():
                    pe.wait_ge(lin_ready, b * 8 + 2)
                    project("l2t_q", lmf2, 0, P, KC).then_inc(lin_ps, 1)

                def token_project():
                    pe.wait_ge(at_red, b * 4 + 4)
                    project("l2t_out", roT, 0, P, KC).then_inc(lin_ps, 1)

                def scores(t, g):
                    u = 4 * t + g
                    if g == 0:
                        pe.wait_ge(kd_ready, b * 16 + 4 * t + 4)
                    if u >= 2:
                        pe.wait_ge(smax, b * 16 + u - 1)
                    mm(bank[g % 2][:, :], identb[:, :], causal[:, :, :].rearrange("p h k -> p (h k)"), True, False)
                    for c in (2 * g, 2 * g + 1):
                        for blk in range(2):
                            ins = mm(bank[g % 2][S * blk:S * blk + S, (c % 2) * 256:(c % 2) * 256 + 256],
                                     qs[0:PARTS, c, t * P + S * blk:t * P + S * blk + S],
                                     kd[0:PARTS, t % 2, c, :, S * blk:S * blk + S], False, c % 2 == 1)
                    ins.then_inc(s_ps, 1)

                def maxima_rows(t):
                    pe.wait_ge(nmh_ready, b * T + t + 1)
                    if t >= 1:
                        pe.wait_ge(nm_row, b * T + t)
                    for c in range(C8):
                        ins = pe.transpose(bank5b[0:2 * HQ, c * P:(c + 1) * P],
                                           nmh[:, t % 2, HQ * c:HQ * c + HQ, :].rearrange("p h j -> p (h j)"),
                                           identb[:, :])
                    ins.then_inc(nm_t, 1)

                def scores_t(t, g):
                    u = 4 * t + g
                    if g == 0:
                        pe.wait_ge(qd_ready, b * 16 + 4 * t + 4)
                    if u >= 2:
                        pe.wait_ge(exps, b * 16 + u - 1)
                    mm(bank[2 + g % 2][:, :], identb[:, :], causal_t[:, :, :].rearrange("p h k -> p (h k)"), True, False)
                    for c in (2 * g, 2 * g + 1):
                        for blk in range(2):
                            ins = mm(bank[2 + g % 2][S * blk:S * blk + S, (c % 2) * 256:(c % 2) * 256 + 256],
                                     ks[0:ROWS, c, t * P + S * blk:t * P + S * blk + S],
                                     qd[0:ROWS, c, :, S * blk:S * blk + S], False, c % 2 == 1)
                    ins.then_inc(st_ps, 1)

                def weighted(t, g):
                    u = 4 * t + g
                    if g == 0:
                        pe.wait_ge(vd_ready, b * 8 + 2 * t + 2)
                        if t >= 1:
                            pe.wait_ge(r_ready, b * T + t)
                    pe.wait_ge(exps, b * 16 + u + 1)
                    for j in range(8):
                        h = 8 * g + j
                        c, i = h // HQ, h % HQ
                        ins = mm(bank[4][32 * i:32 * i + 32, c * S:(c + 1) * S], vd[:, t, h, :], pt[:, g % 2, j, :])
                    ins.then_inc(pv, 1)

                def turn(t, hf):
                    pe.wait_ge(d_w, 96)
                    if hf == 0:
                        pe.wait_ge(r_ready, b * T + t + 1)
                    if 2 * t + hf >= 1:
                        pe.wait_ge(ol_ready, b * 16 + 2 * (2 * t + hf))
                    for j in range(4):
                        ins = pe.transpose(bank[6][0:S, j * P:(j + 1) * P], r_sb[:, 4 * hf + j, :], ident)
                    ins.then_inc(r_t, 1)

                attend_scores(0)
                landmarks = {1: lambda: attend_turn(0), 2: lambda: attend_out(0, 0), 3: lambda: attend_out(0, 1),
                             4: landmarks_qkv, 5: lambda: la_scores(0), 6: lambda: la_scores(1), 8: la_turn,
                             9: la_weighted, 10: la_project, 11: queries, 12: lambda: attend_scores(1),
                             14: lambda: attend_turn(1), 15: lambda: attend_out(1, 0)}
                for g in range(4):
                    scores(0, g)
                for t in range(T):
                    maxima_rows(t)
                    if t + 1 < T:
                        scores(t + 1, 0)
                        scores(t + 1, 1)
                    if t >= 1:
                        weighted(t - 1, 3)
                    for g in range(4):
                        if t >= 1 and g < 2:
                            turn(t - 1, g)
                        if 4 * t + g in landmarks:
                            landmarks[4 * t + g]()
                        scores_t(t, g)
                        if 1 <= g + 1 < 3 and t + 1 < T:
                            scores(t + 1, g + 2)
                        if g >= 1:
                            weighted(t, g - 1)
                weighted(T - 1, 3)
                attend_out(1, 1)
                turn(T - 1, 0)
                if not last:
                    pe.wait_ge(smax, b * 16 + 16)
                    rows_turned(b + 1)
                turn(T - 1, 1)
                token_project()

                pe.wait_ge(lin_ready, b * 8 + 8)
                project("lm_kv", lmf3, 0, P, KC)
                rows("lm_kv", lmf3, D).then_inc(lm_ps, 1)
                if not last:
                    pe.wait_ge(nm_row, b * T + T)
                    projection(b + 1, 0)
                pe.wait_ge(d_w, 96)
                pe.wait_ge(gk_parts, b + 1)
                for c in range(C8):
                    out = bank[7][0:PARTS, c * NL:(c + 1) * NL]
                    mm(out, selk[:, c % 4, 0, :], gkp[:, 0, c // 4, :], True, False)
                    ins = mm(out, selk[:, c % 4, 1, :], gkp[:, 1, c // 4, :], False, True)
                ins.then_inc(gk_stack, 1)
                if not last:
                    pe.wait_ge(ol_ready, b * 16 + 16)
                    projection(b + 1, 1)
                pe.wait_ge(gkd_ready, b + 1)
                pe.wait_ge(smax, b * 16 + 16)
                for t in range(T):
                    for c in range(KC):
                        if t >= 2:
                            pe.wait_ge(gmax, b * 9 + 2 * (t - 2) + c + 1)
                        out = bank[2 * (t % 2) + c][:, :]
                        mm(out, onehot[:, t * P:(t + 1) * P], gmask[:, :, :].rearrange("n h k -> n (h k)"), True, False)
                        for j in range(4):
                            ins = mm(out[:, j * P:(j + 1) * P], qs[0:PARTS, 4 * c + j, t * P:(t + 1) * P],
                                     gkd[:, 4 * c + j, :, :].rearrange("p h k -> p (h k)"), False, j == 3)
                        ins.then_inc(sg, 1)
                    if not last:
                        projection(b + 1, 2 + t)
                pe.wait_ge(gmax, b * 9 + 9)
                pe.wait_ge(r_ready, b * T + T)
                for t in range(T):
                    ins = pe.transpose(bank[4][0:H, t * P:(t + 1) * P], gnm[:, t, :], ident)
                ins.then_inc(gm_t, 1)

                def global_scores(c):
                    if c >= 4:
                        pe.wait_ge(gexp, b * C8 + c - 3)
                    mm(bank[c % 4][:, :], selg[0:2 * H + NB, c, :], mm_[0:2 * H + NB, :], True, False)
                    mm(bank[c % 4][:, :], gkd[:, c, :, :].rearrange("p h k -> p (h k)"), qs[0:PARTS, c, :],
                       False, True).then_inc(sgt, 1)

                def global_weighted(c):
                    if c == 2:
                        if last:
                            pe.wait_ge(ol_ready, b * 16 + 16)
                            pe.wait_ge(nm_row, b * T + T)
                        else:
                            pe.wait_ge(rope_mul, (b + 1) * 8 + 8)
                    pe.wait_ge(gexp, b * C8 + c + 1)
                    mm(bank[4 + c // 2][64 * (c % 2):64 * (c % 2) + 64, :], gvd[:, c, :],
                       pg[:, c % 2, :, :].rearrange("p h q -> p (h q)")).then_inc(gpv, 1)

                if not last:
                    projection(b + 1, 6)
                    projection(b + 1, 7)
                pe.wait_ge(mm_lo, b + 1)
                pe.wait_ge(gvd_ready, b * 4 + 4)
                global_scores(0)
                for c in range(1, C8):
                    global_scores(c)
                    global_weighted(c - 1)
                global_weighted(C8 - 1)
                pe.wait_ge(rg_ready, b * 4 + 4)
                for t in range(T):
                    for j in range(4):
                        ins = pe.transpose(bank[t][:, j * P:(j + 1) * P], rg[:, j, t * P:(t + 1) * P], ident)
                    ins.then_inc(rg_t, 1)
                if not last:
                    values(b + 1, 0)
                    values(b + 1, 1)
                for t in range(T):
                    pe.wait_ge(o_ready, b * T + t + 1)
                    pe.wait_ge(og_ready, b * T + t + 1)
                    if t >= 2:
                        pe.wait_ge(x_new, b * T + t - 1)
                    for k in range(KC):
                        out = bank[4 + t % 2][:, k * P:(k + 1) * P]
                        mm(out, ol[:, t, k * P:(k + 1) * P], ident, True, False)
                        ins = mm(out, og[:, t, k * P:(k + 1) * P], ident, False, True)
                    ins.then_inc(o_t, 1)
                    if not last and t < 2:
                        values(b + 1, 2 + t)
                    pe.wait_ge(oT_ready, b * T + t + 1)
                    for k in range(KC):
                        ins = mm(bank[4 + t % 2][:, D:2 * D], oT[:, t % 2, k, :], wcol("out", k), k == 0, k == KC - 1)
                    ins.then_inc(y_ps, 1)

            with pe.Fori(0, B - 1) as b:
                batch(b, False)
            batch(B - 1, True)


DVE_LINKS_A = 37


def experts_and_attention_b(nc, x, cst, mean, rstd, bank, wb_d, pb_d, wg_d, we_d, rows_s, slots_x, slots_y, out_d):
    with ExitStack() as ctx:
        def sb(name, shape, dt=F32):
            return ctx.enter_context(nc.sbuf_tensor(name, shape, dt))

        def sem(name):
            return ctx.enter_context(nc.semaphore(name))

        wh = sb("wh", [P, 3 * NW, WCOL], BF16)
        wl = sb("wl", [P, 3 * NW, WCOL], BF16)
        stage = sb("stage", [P, 3, WCOL])
        wb = sb("wb", [P, KC, QKVB])
        pb = sb("pb", [P, KC, D])
        wg = sb("wg", [P, KC, E])
        st6 = sb("st6b", [P, 2 * NT, 6])
        mv = sb("mvb", [P, 2 * NT, 2])
        var = sb("var", [P, 2 * NT])
        mean = sb("meanb", [P, 2 * NT])
        rstd = sb("rstdb", [P, 2 * NT])
        xn = sb("xnb", [P, NT, D])
        xT = sb("xTb", [P, 2, 2, KC, P])
        oT = sb("oTb", [P, 2, KC, P])
        prob = sb("prob", [P, NT, E])
        key = sb("key", [P, NT, E])
        eq = sb("eq", [P, NT, E])
        pick = sb("pick", [P, 2, NT, E])
        pickb = sb("pickb", [P, NT, E], BF16)
        trib = sb("trib", [P, P], BF16)
        onesb = sb("onesb", [P, P], BF16)
        best = sb("best", [P, 8, NT])
        seg = sb("seg", [P, 4, E])
        wide = sb("wide", [P, ROUTED * E])
        slot_f = sb("slot_f", [P, 2, NT])
        slot_i = sb("slot_i", [P, 2, NT], I32)
        etab = sb("etab", [P, TILES + 1], I32)
        etab_f = sb("etab_f", [P, ROUTED])
        weight = sb("weight", [P, 2, NT])
        xs = sb("xs", [P, 2, D])
        xh = sb("xh", [P, 2, KC, P], BF16)
        xl = sb("xl", [P, 2, KC, P], BF16)
        NPAIR = SEQ * (SEQ + 1) // 2
        work = sb("work", [P, NPAIR * D])
        sg = work[:, 0:2 * FF].rearrange("p (a n) -> p a n", a=2)
        hh = work[:, 2 * FF:4 * FF].rearrange("p (a n) -> p a n", a=2)
        ysb = work[:, 4 * FF:4 * FF + 2 * D].rearrange("p (a n) -> p a n", a=2)
        hTh = sb("hTh", [P, 2, FC, P], BF16)
        hTl = sb("hTl", [P, 2, FC, P], BF16)
        RING = 4
        gat = sb("gat", [P, 2, RING, D])

        d_stage = [sem(f"d_stage{m}") for m in range(3)]
        y_out = [sem("y_out_even"), sem("y_out_odd")]
        g_in = [sem(f"g_in{r}") for r in range(RING)]
        PER = ((TILES + 1) // 2, TILES // 2)
        STORED = ((ROUTED + 1) // 2, ROUTED // 2)
        w_lo2 = sem("w_lo2")
        d_b, shared_added, w_hi, w_lo, casts = sem("d_b"), sem("shared_added"), sem("w_hi"), sem("w_lo"), sem("casts")
        (bstat, bvar, bstd, brs, xn_t, xT_ready, logits, r_sub, r_exp, r_step, pick_ready, ranks, slot_ready,
         xn_out, scattered) = [sem(n) for n in (
             "bstat bvar bstd brs bxn_t bxT_ready logits r_sub r_exp r_step pick_ready ranks slot_ready "
             "xn_out scattered").split()]
        (xs_t, xh_ready, xl_ready, gu, sg_ready, h_ready, h_t, hTh_ready, hTl_ready, y_ps, y_ready,
         combined) = [sem(n) for n in (
             "xs_t xh_ready xl_ready gu sg_ready h_ready h_t hTh_ready hTl_ready by_ps by_ready "
             "combined").split()]
        xn_ready = [sem(f"bxn_ready{i}") for i in range(3)]
        xs_in = [sem("xs_in_even"), sem("xs_in_odd")]
        (b_qkv, b_q, b_mul, b_sub, b_exp, b_ot, b_oT, b_y, b_x, b_step) = [sem(n) for n in (
            "b_qkv b_q b_mul b_sub b_exp b_ot b_oT b_y b_x b_step").split()]
        done, brs_r = sem("done"), sem("brs_r")

        ident = const(cst, "ident")
        X, G, U, HT, Y, RT = 0, (1, 2), (3, 4), 7, 6, 5
        qkv = stage[:, :, :].rearrange("p a b -> p (a b)").rearrange("p (c s n) -> p c s n", c=2, s=SEQ)
        prod = work[:, :].rearrange("p (a n) -> p a n", a=NPAIR)
        sc = sb("scb", [P, NPAIR, NH])
        sstat = sb("sstat", [P, 3, SEQ, NH])
        block = ctx.enter_context(nc.Block())

        def pair(s, t=0):
            return s * (s + 1) // 2 + t

        def y_slot(n):
            return bank[6 + n // 2 % 2][:, (n % 2) * D:(n % 2 + 1) * D]

        def tile_b(n):
            return (n % SEQ) * T + n // SEQ

        TURNS = [(0, 0), (0, 1), (0, 2), (0, 3), (1, 0), (1, 1), (1, 2), (2, 0), (1, 3), (2, 1), (2, 2), (2, 3)]

        def nth_turn(which, n):
            return (TURNS.index((which, n // SEQ)) * SEQ + n % SEQ) // 2

        def tile_moe(layer, n):
            return n if layer == 0 else tile_b(n)

        @block.sync
        def _(sp):
            sp.dma_start(wg[:, :, :], wg_d).then_inc(d_b, 16)
            sp.dma_start(wb[:, :, :], wb_d).then_inc(d_b, 16)
            sp.dma_start(pb[:, :, :], pb_d).then_inc(d_b, 16)
            for m in range(3):
                sp.dma_start(stage[:, m, :], we_d[0, m]).then_inc(d_stage[m], 16)
            shared_rows = rows_s.rearrange("(j p) d -> j p d", p=P)
            rows_x = slots_x.rearrange("(j p) d -> j p d", p=P)
            rows_y = slots_y.rearrange("(j p) d -> j p d", p=P)
            we_v = we_d.rearrange("e m p n -> (e m) p n")
            BEHIND = 5
            assert E == NT // 2
            for layer in range(2):
                first = layer == 0
                for n in range(NT):
                    t = tile_moe(layer, n)
                    sp.wait_ge(xn_ready[2 * layer], n + 1)
                    sp.dma_start(shared_rows[t], xn[:, t, :]).then_inc(xn_out, 16)
                sp.wait_ge(xn_out, (layer + 1) * 16 * NT)

                def load(j, par, routed):
                    sp.dma_start(xs[:, par, :], rows_x[j - NT] if routed else shared_rows[j]).then_inc(xs_in[par], 16)

                def store(j, par):
                    sp.wait_ge(y_ready, layer * ROUTED + j - NT + 1)
                    sp.dma_start(rows_y[j - NT], ysb[:, par, :]).then_inc(y_out[par], 16)

                for par in range(2):
                    if layer:
                        sp.wait_ge(xs_t, layer * TILES)
                    load(par, par, False)

                def tiles_of(i, routed):
                    for par in range(2):
                        sp.wait_ge(xs_t, layer * TILES + 2 * i + par - 1)
                        load(2 * i + par, par, routed)
                        if routed and (not isinstance(i, int) or 2 * i + par - BEHIND >= NT):
                            store(2 * i + par - BEHIND, 1 - par)

                def weights_of(e):
                    for m in range(3):
                        sp.wait_ge(w_hi, 3 * e - 2 + m)
                        if m < 2:
                            sp.wait_ge(w_lo, 2 * e - 1 + m)
                        else:
                            sp.wait_ge(w_lo2, e)
                        sp.dma_start(stage[:, m, :], we_v[3 * e + m]).then_inc(d_stage[m], 16)

                if first:
                    weights_of(1)
                with sp.Fori(1, NT // 2) as i:
                    tiles_of(i, False)
                    if first:
                        weights_of(i + 1)
                sp.wait_ge(scattered, (layer + 1) * 32 * NT)
                for i in range(NT // 2, NT // 2 + 3):
                    tiles_of(i, True)
                with sp.Fori(NT // 2 + 3, TILES // 2) as i:
                    tiles_of(i, True)
                sp.wait_ge(xs_t, layer * TILES + TILES - 2)
                load(TILES - 1, 0, True)
                for j in range(TILES - 1 - BEHIND, TILES):
                    store(j, j % 2)
            out_v = out_d.rearrange("b (t p) d -> b p t d", p=P)
            for b in range(B):
                sp.wait_ge(combined, NT + (b + 1) * T)
                sp.dma_start(out_v[b], x[:, b * T:(b + 1) * T, :]).then_inc(done, 16)
            sp.wait_ge(done, 16 * B)

        @block.gpsimd
        def _(pool):
            def low_parts(e):
                for m in range(2):
                    pool.wait_ge(w_hi, 3 * e + m + 1)
                    pool.tensor_tensor(wl[:, 3 * e + m, :], stage[:, m, :], wh[:, 3 * e + m, :],
                                       ALU.subtract).then_inc(w_lo, 1)

            low_parts(0)
            low_parts(1)
            for layer in range(2):
                for e in range(2, NW):
                    if layer == 0:
                        low_parts(e)
                    if e == 2:
                        pool.wait_ge(slot_ready, layer + 1)
                        pool.wait_ge(xn_ready[2 * layer], NT)
                    for t in range(3 * (e - 2), min(3 * (e - 1), NT)):
                        for k in range(2):
                            pool.indirect_dma_start(slots_x,
                                                    bass.IndirectOffsetOnAxis(ap=slot_i[:, k, t:t + 1], axis=0),
                                                    xn[:, t, :], None).then_inc(scattered, 16)
                for par in range(2):
                    pool.wait_ge(y_out[par], (layer + 1) * 16 * STORED[par])
                for n in range(NT):
                    t = tile_b(n) if layer == 0 else n
                    if n >= RING:
                        pool.wait_ge(combined, layer * NT + n - RING + 1)
                    for k in range(2):
                        pool.indirect_dma_start(gat[:, k, n % RING, :], None, slots_y,
                                                bass.IndirectOffsetOnAxis(ap=slot_i[:, k, t:t + 1], axis=0))\
                            .then_inc(g_in[n % RING], 16)

        @block.scalar
        def _(act):
            act.activation(trib[:, :], const(cst, "tri"), ACT.Copy).then_inc(casts, 1)
            act.activation(onesb[:, :], const(cst, "ones"), ACT.Copy).then_inc(casts, 1)

            def std(n, cols=slice(0, NT)):
                act.wait_ge(bvar, n + 1)
                act.activation(var[:, cols], var[:, cols], ACT.Sqrt).then_inc(bstd, 1)

            def turned(which, n):
                i = nth_turn(which, n)
                act.wait_ge(xn_t, i + 1)
                act.activation(xT[:, i % 2, :, :, :].rearrange("p t k c -> p (t k c)"), bank[i % 2][:, :], ACT.Copy)\
                   .then_inc(xT_ready, 1)

            def moe(layer):
                if layer == 0:
                    std(0)
                for n in range(0 if layer == 0 else NT - SEQ, NT, 2):
                    turned(2 * layer, n)
                n0 = layer * TILES

                def x_high(j, par):
                    act.wait_ge(xs_t, n0 + j + 1)
                    act.activation(xh[:, par, :, :].rearrange("p k c -> p (k c)"), bank[X][:, 0:D],
                                   ACT.Copy).then_inc(xh_ready, 1)

                def gates(j, par):
                    act.wait_ge(gu, n0 + j + 1)
                    act.activation(sg[:, par, :], bank[G[par]][:, :], ACT.Silu).then_inc(sg_ready, 1)

                def h_high(j, par):
                    act.wait_ge(h_t, n0 + j + 1)
                    act.activation(hTh[:, par, :, :].rearrange("p c t -> p (c t)"), bank[HT][:, :],
                                   ACT.Copy).then_inc(hTh_ready, 1)

                def rows_out(j, par, nth):
                    act.wait_ge(y_ps, n0 + j + 1)
                    if not isinstance(nth, int) or layer * STORED[par] + nth:
                        act.wait_ge(y_out[par], 16 * (layer * STORED[par] + nth))
                    act.activation(ysb[:, par, :], bank[Y][:, 0:D], ACT.Copy).then_inc(y_ready, 1)

                x_high(0, 0)
                x_high(1, 1)
                act.wait_ge(r_sub, layer + 1)
                act.activation(prob[:, :, :], prob[:, :, :], ACT.Exp).then_inc(r_exp, 1)
                gates(0, 0)
                x_high(2, 0)
                gates(1, 1)
                h_high(0, 0)

                def pair_of_tiles(i, out):
                    for par in range(2):
                        j = 2 * i + par
                        x_high(j + 1, 1 - par)
                        if out:
                            rows_out(j - 2, par, i - 1 - NT // 2)
                        gates(j, par)
                        h_high(j - 1, 1 - par)

                with act.Fori(1, NT // 2 + 1) as i:
                    pair_of_tiles(i, False)
                pair_of_tiles(NT // 2 + 1, True)
                with act.Fori(NT // 2 + 2, TILES // 2) as i:
                    pair_of_tiles(i, True)
                j, last = TILES - 1, ROUTED // 2
                rows_out(j - 2, 0, last - 1)
                gates(j, 0)
                h_high(j - 1, 1)
                rows_out(j - 1, 1, last - 1)
                h_high(j, 0)
                rows_out(j, 0, last)

            def attention_b():
                LN1, LN2 = (1, 2, 3, 5), (4, 6, 7, 8)

                def qkv_rows(c):
                    for s in range(0, SEQ, 2):
                        turned(1, c * SEQ + s)
                    for s in range(SEQ):
                        n = c * SEQ + s
                        act.wait_ge(b_qkv, n + 1)
                        if s == 0 and c >= 2:
                            act.wait_ge(b_mul, 2 * (c - 1) * NPAIR)
                        act.activation(qkv[:, c % 2, s, :], bank[2 + n % 2][:, 0:QKVB], ACT.Copy).then_inc(b_q, 1)

                std(LN1[0], slice(0, SEQ))
                qkv_rows(0)
                for c in range(T):
                    if c + 1 < T:
                        std(LN1[c + 1], slice((c + 1) * SEQ, (c + 2) * SEQ))
                        qkv_rows(c + 1)
                    act.wait_ge(b_sub, SEQ * (c + 1))
                    act.activation(sc[:, :, :], sc[:, :, :], ACT.Exp, scale=SCALE_B).then_inc(b_exp, 1)
                    if c:
                        std(LN2[c - 1], slice(NT + (c - 1) * SEQ, NT + c * SEQ))
                    for i in range(c * SEQ // 2, (c + 1) * SEQ // 2):
                        act.wait_ge(b_ot, i + 1)
                        if i >= 1:
                            act.wait_ge(b_y, i)
                        act.activation(oT[:, :, :, :].rearrange("p t k c -> p (t k c)"), bank[4][:, :], ACT.Copy)\
                           .then_inc(b_oT, 1)
                    if c:
                        for s in range(0, SEQ, 2):
                            turned(2, (c - 1) * SEQ + s)
                std(LN2[T - 1], slice(NT + (T - 1) * SEQ, NT + T * SEQ))

            moe(0)
            attention_b()
            moe(1)

        @block.vector
        def _(dve):
            steps = [0]

            def step(ins):
                steps[0] += 1
                ins.then_inc(r_step, 1)
                dve.wait_ge(r_step, steps[0])

            stats = [0, 0]

            def row_statistics(col, tile):
                stats[0] += 1
                dve.bn_stats(st6[:, col, :], x[:, tile, :]).then_inc(bstat, 1)

            def variances(cols):
                dve.wait_ge(bstat, stats[0])
                for col in cols:
                    stats[0] += 1
                    dve.bn_aggr(mv[:, col, :], st6[:, col, :]).then_inc(bstat, 1)
                dve.wait_ge(bstat, stats[0])
                sl = slice(cols[0], cols[-1] + 1)
                dve.tensor_copy(mean[:, sl], mv[:, sl, 0]).then_inc(brs, 1)
                dve.tensor_scalar(var[:, sl], mv[:, sl, 1], LN_EPS, None, ALU.add).then_inc(bvar, 1)

            def normalised(cols, tiles, which):
                sl = slice(cols[0], cols[-1] + 1)
                stats[1] += 1
                dve.wait_ge(bstd, stats[1])
                dve.wait_ge(brs, stats[1])
                dve.reciprocal(rstd[:, sl], var[:, sl]).then_inc(brs_r, 1)
                dve.wait_ge(brs_r, stats[1])
                for col, tile in zip(cols, tiles):
                    dve.tensor_scalar(xn[:, tile, :], x[:, tile, :], mean[:, col:col + 1], rstd[:, col:col + 1],
                                      ALU.subtract, ALU.mult).then_inc(xn_ready[which], 1)

            lg = bank[RT][:, 0:NT * E].rearrange("p (t e) -> p t e", e=E)
            rk = bank[RT][:, P:P + (NT + 1) * E].rearrange("p (t e) -> p t e", e=E)
            cnt, tiles, base, end = (seg[:, i, :] for i in range(4))
            starts = const(cst, "tilestart")

            def over(a):
                return a.unsqueeze(2).broadcast_to([P, NT, E])

            def router_probabilities(layer):
                dve.wait_ge(logits, layer + 1)
                step(dve.tensor_reduce(best[:, 0, :], lg, AX.X, ALU.max))
                dve.tensor_tensor(prob[:, :, :], lg, over(best[:, 0, :]), ALU.subtract).then_inc(r_sub, 1)
                dve.wait_ge(r_exp, layer + 1)
                step(dve.tensor_reduce(best[:, 1, :], prob[:, :, :], AX.X, ALU.add))
                step(dve.reciprocal(best[:, 2, :], best[:, 1, :]))
                step(dve.tensor_tensor(prob[:, :, :], prob[:, :, :], over(best[:, 2, :]), ALU.mult))
                router_pick(0)
                step(dve.scalar_tensor_tensor(prob[:, :, :], pick[:, 0, :, :], -2.0, prob[:, :, :], ALU.mult, ALU.add))

            def router_pick(k):
                iota = const(cst, "iota8").unsqueeze(1).broadcast_to([P, NT, E])
                step(dve.tensor_reduce(best[:, 3 + k, :], prob[:, :, :], AX.X, ALU.max))
                step(dve.tensor_tensor(eq[:, :, :], prob[:, :, :], over(best[:, 3 + k, :]), ALU.is_equal))
                step(dve.scalar_tensor_tensor(key[:, :, :], eq[:, :, :], float(-E), iota, ALU.mult, ALU.add))
                step(dve.tensor_reduce(best[:, 5, :], key[:, :, :], AX.X, ALU.min))
                step(dve.tensor_tensor(pick[:, k, :, :], key[:, :, :], over(best[:, 5, :]), ALU.is_equal))

            def router_weights(layer):
                router_pick(1)
                dve.tensor_tensor(pickb[:, :, :], pick[:, 0, :, :], pick[:, 1, :, :], ALU.add).then_inc(pick_ready, 1)
                step(dve.tensor_tensor(best[:, 6, :], best[:, 3, :], best[:, 4, :], ALU.add))
                step(dve.reciprocal(best[:, 7, :], best[:, 6, :]))
                for k in range(2):
                    step(dve.tensor_tensor(weight[:, k, :], best[:, 3 + k, :], best[:, 7, :], ALU.mult))

            def router_bases(layer):
                dve.wait_ge(ranks, layer + 1)
                step(dve.tensor_copy(cnt, rk[:, NT, :]))
                wv = wide[:, 0:E * NT].rearrange("p (e j) -> p e j", e=E)
                step(dve.tensor_tensor(wv, cnt.unsqueeze(2).broadcast_to([P, E, NT]),
                                       starts[:, 0:NT].unsqueeze(1).broadcast_to([P, E, NT]), ALU.is_gt))
                step(dve.tensor_reduce(tiles, wv, AX.X, ALU.add))
                bv = wide[:, 0:E * E].rearrange("p (e f) -> p e f", e=E)
                step(dve.tensor_tensor(bv, tiles.unsqueeze(1).broadcast_to([P, E, E]),
                                       const(cst, "tri8").rearrange("p (e f) -> p e f", e=E), ALU.mult))
                step(dve.tensor_reduce(base, bv, AX.X, ALU.add))
                step(dve.tensor_tensor(end, base, tiles, ALU.add))
                step(dve.tensor_scalar(base, base, float(P), None, ALU.mult))
                step(dve.tensor_scalar(end, end, float(P), None, ALU.mult))
                step(dve.tensor_tensor(eq[:, :, :], rk[:, 0:NT, :], base.unsqueeze(1).broadcast_to([P, NT, E]),
                                       ALU.add))

            def router_slots(layer):
                for k in range(2):
                    step(dve.tensor_tensor(key[:, :, :], eq[:, :, :], pick[:, k, :, :], ALU.mult))
                    step(dve.tensor_reduce(slot_f[:, k, :], key[:, :, :], AX.X, ALU.add))
                tv = wide[:, :].rearrange("p (j e) -> p j e", e=E)
                step(dve.tensor_tensor(tv, starts.unsqueeze(2).broadcast_to([P, ROUTED, E]),
                                       end.unsqueeze(1).broadcast_to([P, ROUTED, E]), ALU.is_ge))
                step(dve.tensor_reduce(etab_f[:, :], tv, AX.X, ALU.add))
                step(dve.tensor_scalar(etab_f[:, :], etab_f[:, :], float(E - 1), 1.0, ALU.min, ALU.add))
                step(dve.tensor_scalar(etab[:, NT:TILES], etab_f[:, :], 3.0, None, ALU.mult))
                dve.tensor_copy(slot_i[:, :, :], slot_f[:, :, :]).then_inc(slot_ready, 1)

            def split(e):
                for m in range(3):
                    dve.wait_ge(d_stage[m], 16 * e + 16)
                    dve.tensor_copy(wh[:, bass.ds(3 * e + m, 1), :], stage[:, m:m + 1, :]).then_inc(w_hi, 1)
                dve.wait_ge(w_hi, 3 * e + 3)
                dve.tensor_tensor(wl[:, bass.ds(3 * e + 2, 1), :], stage[:, 2:3, :], wh[:, bass.ds(3 * e + 2, 1), :],
                                  ALU.subtract).then_inc(w_lo2, 1)

            def moe(layer):
                if layer == 0:
                    for t in range(NT):
                        row_statistics(t, t)
                    variances(range(NT))
                    normalised(range(NT), range(NT), 0)
                    step(dve.memset(etab[:, 0:NT], 0))
                    split(0)
                    split(1)
                n0 = layer * TILES

                def x_low(j, par):
                    dve.wait_ge(xh_ready, n0 + j + 1)
                    dve.tensor_tensor(xl[:, par, :, :].rearrange("p k c -> p (k c)"), bank[X][:, 0:D],
                                      xh[:, par, :, :].rearrange("p k c -> p (k c)"), ALU.subtract)\
                       .then_inc(xl_ready, 1)

                def hidden(j, par):
                    dve.wait_ge(sg_ready, n0 + j + 1)
                    dve.tensor_tensor(hh[:, par, :], bank[U[par]][:, :], sg[:, par, :], ALU.mult).then_inc(h_ready, 1)

                def h_low(j, par):
                    dve.wait_ge(hTh_ready, n0 + j + 1)
                    dve.tensor_tensor(hTl[:, par, :, :].rearrange("p c t -> p (c t)"), bank[HT][:, :],
                                      hTh[:, par, :, :].rearrange("p c t -> p (c t)"), ALU.subtract)\
                       .then_inc(hTl_ready, 1)

                def add_shared(j):
                    dve.wait_ge(y_ps, n0 + j + 1)
                    if isinstance(j, int):
                        tile, out = x[:, j, :], bank[Y][:, 0:D]
                    else:
                        tile, out = x[:, bass.ds(j, 1), :], bank[Y][:, 0:D].unsqueeze(1)
                    dve.tensor_tensor(tile, out, tile, ALU.add).then_inc(shared_added, 1)

                x_low(0, 0)
                x_low(1, 1)
                router_probabilities(layer)
                hidden(0, 0)
                x_low(2, 0)
                router_weights(layer)
                hidden(1, 1)
                h_low(0, 0)

                def pair_of_tiles(i, splits, shared, routing=False):
                    if splits:
                        split(i + 1)
                    for par in range(2):
                        j = 2 * i + par
                        x_low(j + 1, 1 - par)
                        hidden(j, par)
                        if shared:
                            add_shared(j - 2)
                        h_low(j - 1, 1 - par)
                        if routing:
                            (router_bases, router_slots)[par](layer)

                pair_of_tiles(1, layer == 0, True, routing=True)
                with dve.Fori(2, NT // 2) as i:
                    pair_of_tiles(i, layer == 0, True)
                pair_of_tiles(NT // 2, False, True)
                with dve.Fori(NT // 2 + 1, TILES // 2) as i:
                    pair_of_tiles(i, False, False)
                j = TILES - 1
                hidden(j, 0)
                h_low(j - 1, 1)
                h_low(j, 0)

            def combine(layer, n, t):
                dve.wait_ge(g_in[n % RING], 32 * (layer * (NT // RING) + n // RING + 1))
                for k in range(2):
                    ins = dve.scalar_tensor_tensor(x[:, t, :], gat[:, k, n % RING, :], weight[:, k, t:t + 1],
                                                   x[:, t, :], ALU.mult, ALU.add)
                    if k == 0:
                        step(ins)
                ins.then_inc(combined, 1)

            def attention_b():
                def columns(c, half):
                    return range(half * NT + c * SEQ, half * NT + (c + 1) * SEQ)

                def chunk_tiles(c):
                    return [tile_b(c * SEQ + s) for s in range(SEQ)]

                def combine_chunk(c):
                    for s in range(SEQ):
                        combine(0, c * SEQ + s, tile_b(c * SEQ + s))
                    for s in range(SEQ):
                        dve.wait_ge(combined, c * SEQ + s + 1)
                        row_statistics(c * SEQ + s, tile_b(c * SEQ + s))
                    variances(columns(c, 0))

                def head(a):
                    return a.rearrange("p (g n) -> p g n", g=NKV)

                def products_qk(c):
                    dve.wait_ge(b_q, (c + 1) * SEQ)
                    if c:
                        dve.wait_ge(b_ot, c * SEQ // 2)
                    for s in range(SEQ):
                        q = head(qkv[:, c % 2, s, :])[:, :, 0:64].rearrange("p g (r d) -> p g r d", d=HD)
                        for t in range(s + 1):
                            k = head(qkv[:, c % 2, t, :])[:, :, 64:80].unsqueeze(2).broadcast_to([P, NKV, 4, HD])
                            dve.tensor_tensor(prod[:, pair(s, t), :].rearrange("p (g r d) -> p g r d", g=NKV, r=4),
                                              q, k, ALU.mult).then_inc(b_mul, 1)

                def softmax(c):
                    dve.wait_ge(b_mul, (2 * c + 1) * NPAIR)
                    step(dve.tensor_reduce(sc[:, :, :].rearrange("p a h -> p (a h)"),
                                           prod[:, :, :].rearrange("p a (h d) -> p (a h) d", d=HD), AX.X, ALU.add))

                    def own(s):
                        return sc[:, pair(s):pair(s) + s + 1, :]

                    for s in range(SEQ):
                        ins = dve.tensor_reduce(sstat[:, 0, s, :], own(s).rearrange("p a h -> p h a"), AX.X, ALU.max)
                        if s + 1 < SEQ:
                            ins.then_inc(b_step, 1)
                    step(ins)
                    dve.wait_ge(b_step, (3 * c + 1) * (SEQ - 1))
                    for s in range(SEQ):
                        dve.tensor_tensor(own(s), own(s), sstat[:, 0, s, :].unsqueeze(1).broadcast_to([P, s + 1, NH]),
                                          ALU.subtract).then_inc(b_sub, 1)
                    dve.wait_ge(b_exp, c + 1)
                    for s in range(SEQ):
                        ins = dve.tensor_reduce(sstat[:, 1, s, :], own(s).rearrange("p a h -> p h a"), AX.X, ALU.add)
                        if s + 1 < SEQ:
                            ins.then_inc(b_step, 1)
                    step(ins)
                    dve.wait_ge(b_step, (3 * c + 2) * (SEQ - 1))
                    step(dve.reciprocal(sstat[:, 2, :, :], sstat[:, 1, :, :]))
                    for s in range(SEQ):
                        ins = dve.tensor_tensor(own(s), own(s), sstat[:, 2, s, :].unsqueeze(1)
                                                .broadcast_to([P, s + 1, NH]), ALU.mult)
                        if s + 1 < SEQ:
                            ins.then_inc(b_step, 1)
                    step(ins)
                    dve.wait_ge(b_step, (3 * c + 3) * (SEQ - 1))

                def products_pv(c):
                    for s in range(SEQ):
                        for t in range(s + 1):
                            vv = head(qkv[:, c % 2, t, :])[:, :, 80:96].unsqueeze(2).broadcast_to([P, NKV, 4, HD])
                            pp = sc[:, pair(s, t), :].rearrange("p (g r) -> p g r", g=NKV).unsqueeze(3)\
                                .broadcast_to([P, NKV, 4, HD])
                            dve.tensor_tensor(prod[:, pair(s, t), :].rearrange("p (g r d) -> p g r d", g=NKV, r=4),
                                              vv, pp, ALU.mult).then_inc(b_mul, 1)

                def output_onto_x(c):
                    for s in range(SEQ):
                        n = c * SEQ + s
                        dve.wait_ge(b_y, n // 2 + 1)
                        dve.tensor_tensor(x[:, s * T + c, :], y_slot(n), x[:, s * T + c, :], ALU.add)\
                           .then_inc(b_x, 1)
                    for s in range(SEQ):
                        dve.wait_ge(b_x, c * SEQ + s + 1)
                        row_statistics(NT + c * SEQ + s, s * T + c)
                    variances(columns(c, 1))

                combine_chunk(0)
                normalised(columns(0, 0), chunk_tiles(0), 1)
                for c in range(T):
                    if c + 1 < T:
                        combine_chunk(c + 1)
                    products_qk(c)
                    if c + 1 < T:
                        normalised(columns(c + 1, 0), chunk_tiles(c + 1), 1)
                    softmax(c)
                    if c:
                        output_onto_x(c - 1)
                    products_pv(c)
                    if c:
                        normalised(columns(c - 1, 1), chunk_tiles(c - 1), 2)
                output_onto_x(T - 1)
                normalised(columns(T - 1, 1), chunk_tiles(T - 1), 2)

            moe(0)
            attention_b()
            moe(1)
            for t in range(NT):
                combine(1, t, t)

        @block.tensor
        def _(pe):
            def mm(out, lhs, rhs, start=True, stop=True):
                return pe.matmul(out, lhs, rhs, start=start, stop=stop, skip_group_check=True)

            def turn(which, n, tiles):
                i = nth_turn(which, n)
                pe.wait_ge(xn_ready[which], n + 2)
                if i >= 2:
                    pe.wait_ge(xT_ready, i - 1)
                for j, tile in enumerate(tiles):
                    for k in range(KC):
                        ins = pe.transpose(bank[i % 2][:, j * D + k * P:j * D + (k + 1) * P],
                                           xn[:, tile, k * P:(k + 1) * P], ident)
                ins.then_inc(xn_t, 1)

            def turns_and_logits(layer, ns):
                def tiles(n):
                    return tile_moe(layer, n), tile_moe(layer, n + 1)

                ns = list(ns)
                turn(2 * layer, ns[0], tiles(ns[0]))
                for n in ns:
                    if n % 2 == 0 and n + 2 <= ns[-1]:
                        turn(2 * layer, n + 2, tiles(n + 2))
                    i = nth_turn(2 * layer, n)
                    pe.wait_ge(xT_ready, i + 1)
                    t = tile_moe(layer, n)
                    for k in range(KC):
                        ins = mm(bank[RT][:, t * E:(t + 1) * E], xT[:, i % 2, n % 2, k, :], wg[:, k, :],
                                 k == 0, k == KC - 1)
                return ins

            pe.wait_ge(d_b, 48)
            pe.wait_ge(casts, 2)

            def moe(layer):
                turns_and_logits(layer, range(NT) if layer == 0 else range(NT - SEQ, NT)).then_inc(logits, 1)

                def rank():
                    pe.wait_ge(pick_ready, layer + 1)
                    mm(bank[RT][:, P:P + NT * E], trib[:, :], pickb[:, :, :].rearrange("p t e -> p (t e)"), True, False)
                    for s in range(1, NT + 1):
                        n = (NT + 1 - s) * E
                        ins = mm(bank[RT][:, P + s * E:P + s * E + n], onesb[:, :],
                                 pickb[:, :, :].rearrange("p t e -> p (t e)")[:, 0:n], False, s == NT)
                    ins.then_inc(ranks, 1)

                n0 = layer * TILES

                def rows_in(j, par, waits=True, nth=None):
                    if waits:
                        pe.wait_ge(xl_ready, n0 + j)
                    pe.wait_ge(xs_in[par], 16 * (layer * PER[par] + (nth if nth is not None else j // 2) + 1))
                    for k in range(KC):
                        ins = pe.transpose(bank[X][:, k * P:(k + 1) * P], xs[:, par, k * P:(k + 1) * P], ident)
                    ins.then_inc(xs_t, 1)

                def weights(e, part, m, k, cols):
                    buf = (wh, wl)[part]
                    if isinstance(e, int):
                        return buf[:, e + m, k * cols:(k + 1) * cols]
                    return buf[:, bass.ds(e + m, 1), k * cols:(k + 1) * cols]

                def gate_up(j, par, e, waits=True):
                    pe.wait_ge(xl_ready, n0 + j + 1)
                    if waits:
                        pe.wait_ge(h_ready, n0 + j - 1)
                    outs = (bank[G[par]][:, :], bank[U[par]][:, :])
                    for k in range(KC):
                        for m in range(2):
                            mm(outs[m], xh[:, par, k, :], weights(e, 0, m, k, FF), k == 0, False)
                            mm(outs[m], xh[:, par, k, :], weights(e, 1, m, k, FF), False, False)
                        for m in range(2):
                            ins = mm(outs[m], xl[:, par, k, :], weights(e, 0, m, k, FF), False, k == KC - 1)
                    ins.then_inc(gu, 1)

                def down(j, par, e, shared=False):
                    pe.wait_ge(hTl_ready, n0 + j + 1)
                    if not isinstance(j, int) or layer or j > 0:
                        if shared or isinstance(j, int) and j == NT:
                            pe.wait_ge(shared_added, layer * NT + j)
                        else:
                            pe.wait_ge(y_ready, layer * ROUTED + j - NT)
                    for c in range(FC):
                        mm(bank[Y][:, 0:D], hTh[:, par, c, :], weights(e, 0, 2, c, D), c == 0, False)
                        mm(bank[Y][:, 0:D], hTh[:, par, c, :], weights(e, 1, 2, c, D), False, False)
                        ins = mm(bank[Y][:, 0:D], hTl[:, par, c, :], weights(e, 0, 2, c, D), False, c == FC - 1)
                    ins.then_inc(y_ps, 1)

                def turn_hidden(j, par):
                    pe.wait_ge(h_ready, n0 + j + 1)
                    for c in range(FC):
                        ins = pe.transpose(bank[HT][:, c * P:(c + 1) * P], hh[:, par, c * P:(c + 1) * P], ident)
                    ins.then_inc(h_t, 1)

                def expert(j):
                    return pe.snap(pe.value_load(etab[0:1, bass.ds(j, 1)], min_val=0, max_val=3 * E))

                rows_in(0, 0, waits=False)
                rows_in(1, 1)
                pe.wait_ge(w_lo, 2)
                pe.wait_ge(w_lo2, 1)
                gate_up(0, 0, 0, waits=False)
                rows_in(2, 0)
                gate_up(1, 1, 0, waits=False)
                rank()
                turn_hidden(0, 0)

                def pair_of_tiles(i, shared, shared_down=False):
                    for par in range(2):
                        j = 2 * i + par
                        rows_in(j + 1, 1 - par, nth=i + par)
                        gate_up(j, par, 0 if shared else expert(j))
                        down(j - 2, par, 0 if shared_down else expert(j - 2), shared_down)
                        turn_hidden(j - 1, 1 - par)

                pair_of_tiles(1, True, True)
                with pe.Fori(2, NT // 2) as i:
                    pair_of_tiles(i, True, True)
                pe.wait_ge(w_lo, 2 * NW)
                pe.wait_ge(w_lo2, NW)
                pe.wait_ge(slot_ready, layer + 1)
                pair_of_tiles(NT // 2, False, True)
                pair_of_tiles(NT // 2 + 1, False)
                with pe.Fori(NT // 2 + 2, TILES // 2) as i:
                    pair_of_tiles(i, False)
                j = TILES - 1
                gate_up(j, 0, expert(j))
                down(j - 2, 0, expert(j - 2))
                turn_hidden(j - 1, 1)
                down(j - 1, 1, expert(j - 1))
                turn_hidden(j, 0)
                down(j, 0, expert(j))

            def attention_b():
                def project(c):
                    for s in range(0, SEQ, 2):
                        turn(1, c * SEQ + s, (tile_b(c * SEQ + s), tile_b(c * SEQ + s + 1)))
                    for s in range(SEQ):
                        n = c * SEQ + s
                        i = nth_turn(1, n)
                        pe.wait_ge(xT_ready, i + 1)
                        if n >= 2:
                            pe.wait_ge(b_q, n - 1)
                        for k in range(KC):
                            ins = mm(bank[2 + n % 2][:, 0:QKVB], xT[:, i % 2, n % 2, k, :], wb[:, k, :],
                                     k == 0, k == KC - 1)
                        ins.then_inc(b_qkv, 1)

                project(0)
                for c in range(T):
                    if c + 1 < T:
                        project(c + 1)
                    for i in range(c * SEQ // 2, (c + 1) * SEQ // 2):
                        pe.wait_ge(b_mul, (2 * c + 1) * NPAIR + pair(2 * i % SEQ + 2))
                        if i >= 1:
                            pe.wait_ge(b_oT, i)
                        for j in range(2):
                            s = 2 * i % SEQ + j
                            for k in range(KC):
                                for t in range(s + 1):
                                    ins = mm(bank[4][:, j * D + k * P:j * D + (k + 1) * P],
                                             prod[:, pair(s, t), k * P:(k + 1) * P], ident, t == 0, t == s)
                        ins.then_inc(b_ot, 1)
                        pe.wait_ge(b_oT, i + 1)
                        if i >= 2:
                            pe.wait_ge(b_x, 2 * (i - 1))
                        for j in range(2):
                            for k in range(KC):
                                ins = mm(y_slot(2 * i + j), oT[:, j, k, :], pb[:, k, :], k == 0, k == KC - 1)
                        ins.then_inc(b_y, 1)
                    if c:
                        turns_and_logits(1, range((c - 1) * SEQ, c * SEQ))

            moe(0)
            attention_b()
            moe(1)


def kernel(**inputs):
    import concourse.bacc as bacc
    from concourse.bass_utils import run_bass_kernel_spmd

    a = {k.replace("L0_", ""): np.asarray(v) for k, v in inputs.items()}
    swap = np.arange(D) ^ 1

    def chunks(m):
        return np.ascontiguousarray(m.reshape(m.shape[0] // P, P, m.shape[1]).transpose(1, 0, 2))

    wq, wk, wv = (a["attn_a_w_qkv"][:, i * D:(i + 1) * D] for i in range(3))
    bq, bk, bv = (a["attn_a_b_qkv"][i * D:(i + 1) * D] for i in range(3))
    wa = chunks(np.concatenate([wk, wk[:, swap], wq, wq[:, swap], wv, a["attn_a_w_gate"], a["attn_a_w_lm_qkv"],
                                a["attn_a_w_lm_out"], a["attn_a_w_l2t_q"], a["attn_a_w_l2t_out"],
                                a["attn_a_w_lm_kv"], a["attn_a_w_out"]], axis=1))
    blm, bkv = a["attn_a_b_lm_qkv"], a["attn_a_b_lm_kv"]
    cols = [bk, bk[swap], bq, bq[swap], blm[0:D], blm[D:2 * D], a["attn_a_b_lm_out"], a["attn_a_b_l2t_q"],
            a["attn_a_b_l2t_out"], bkv[0:D]]
    ba = np.ascontiguousarray(np.concatenate(cols).reshape(B_TOTAL, P).T)
    ra = np.concatenate([bv, a["attn_a_b_gate"], blm[2 * D:], bkv[D:], a["attn_a_b_out"]])
    ra = np.ascontiguousarray(np.broadcast_to(ra, (P, R_TOTAL)))
    pool_q = a["attn_a_pool_q"].reshape(M, H, DH)
    pq = np.zeros((P, KC, HC, M), np.float32)
    for h in range(H):
        pq[DH * (h % HC):DH * (h % HC) + DH, h // HC, h % HC, :] = pool_q[:, h, :].T
    pq = pq.reshape(P, KC, HC * M)

    wb = chunks(a["attn_b_weight_qkv"].T)
    pb = chunks(a["attn_b_weight_proj"].T)
    wg = chunks(a["ffn_wg"].T)
    we = np.stack([np.stack([chunks(g.T).reshape(P, -1), chunks(u.T).reshape(P, -1), chunks(d.T).reshape(P, -1)])
                   for g, u, d in zip(*([a["ffn_sh_" + n]] + list(a["ffn_ex_" + n]) for n in ("gate", "up", "down")))])

    host = {"x": a["attn_a_x"], "const": CONST, "table": TABLE, "wa": wa, "pq": pq, "ba": ba, "ra": ra, "wb": wb, "pb": pb,
            "wg": wg, "we": we}
    nc = bacc.Bacc("TRN2", target_bir_lowering=False, num_devices=1)
    host = {n: np.ascontiguousarray(h) for n, h in host.items()}
    args = [nc.dram_tensor("in_" + n, h.shape, mybir.dt.from_np(h.dtype), kind="ExternalInput").ap()
            for n, h in host.items()]
    out = nc.dram_tensor("out", (B, L, D), F32, kind="ExternalOutput").ap()
    build(nc, *args, out)
    result = run_bass_kernel_spmd(nc, [{"in_" + n: h for n, h in host.items()}], core_ids=[0])
    return result.results[0]["out"]
```

```python
from contextlib import ExitStack

import numpy as np

import concourse.bass as bass
from concourse import mybir

F32 = mybir.dt.float32
BF16 = mybir.dt.bfloat16
I32 = mybir.dt.int32
U32 = mybir.dt.uint32
ALU = mybir.AluOpType
ACT = mybir.ActivationFunctionType
AX = mybir.AxisListType

P = 128
B, L, D = 4, 512, 256
T = L // P
NT = B * T
KC = D // P
LN_EPS = 1e-5

H, DH = 32, 8
S = 64
NB = L // S
M = 4
NL = NB * M
HC = P // DH
HQ = 4
C8 = H // HQ
SCALE = DH ** -0.5
NEG = -1e30
SUM_EPS = 1e-9
PARTS = 3 * HQ * DH
ROWS = PARTS + 2 * HQ

SEQ, BATCH = B, L
NH, NKV, HD = 16, 4, 16
GROUP = (NH // NKV + 2) * HD
QKVB = NKV * GROUP
SCALE_B = float(np.float32(1.0 / np.sqrt(HD)))

E, TOPK, FF = 8, 2, 512
NW = E + 1
FC = FF // P
ROUTED = (NT * P * TOPK - E) // P + E
TILES = NT + ROUTED
SLOTS = ROUTED * P
WCOL = KC * FF


def constants():
    p = np.arange(P)
    f = np.float32
    inv = (f(1.0) / f(10000.0) ** (np.arange(0, DH, 2, dtype=f) / f(DH))).astype(f)
    angle = np.arange(L, dtype=f)[None, :] * inv[(p % DH) // 2][:, None]
    sign = np.where(p % 2 == 0, f(-1), f(1))[:, None]
    tab = {"ident": np.eye(P), "cos": np.cos(angle), "sin": np.sin(angle) * sign}
    r = np.arange(PARTS)
    part, feat = r // (HQ * DH), r % (HQ * DH)
    for name, hi_parts in (("selk", (0, 1)), ("selq", (0, 2))):
        sel = np.zeros((P, 4, 2, PARTS))
        for a in range(4):
            is_hi = np.isin(part, hi_parts)
            sel[HQ * DH * a + feat, a, np.where(is_hi, 0, 1), r] = 1.0
        tab[name] = sel.reshape(P, -1)
    tab["headmask"] = np.where(p[:, None] < PARTS, (p[:, None] % (HQ * DH)) // DH == np.arange(HQ),
                               (p[:, None] - PARTS) // 2 == np.arange(HQ)) * 1.0
    k = np.arange(S)
    tab["causal"] = np.where(k[None, :] > (p % S)[:, None], NEG, 0.0)
    tab["causalT"] = np.where((p % S)[:, None] > k[None, :], NEG, 0.0)
    tab["bd16"] = (p[:, None] // DH == np.arange(HC)) * 1.0
    lm = np.arange(NL)
    la = np.zeros((P, NL))
    la[:NL] = np.where((lm // M)[:, None] < (lm // M)[None, :], NEG, 0.0)
    tab["lamask"] = la
    selg = np.zeros((P, C8, HQ, NL))
    for h in range(H):
        selg[h, h // HQ, h % HQ] = 1.0
        selg[H + h, h // HQ, h % HQ] = 1.0
    below = np.where(np.arange(NB)[:, None] > (lm // M)[None, :], 0.0, NEG)
    selg[2 * H:2 * H + NB] = below[:, None, None, :]
    tab["selg"] = selg.reshape(P, -1)
    oh = np.zeros((P, L))
    oh[2 * H:2 * H + NB] = np.arange(L)[None, :] // S == np.arange(NB)[:, None]
    oh[0:NB] = oh[2 * H:2 * H + NB]
    tab["onehot"] = oh
    gm = np.zeros((P, NL))
    gm[0:NB] = below
    tab["gmask"] = gm
    tab["valid"] = (p[:, None] >= S) * 1.0
    tab["tri"] = (p[:, None] < p[None, :]) * 1.0
    tab["ones"] = np.ones((P, P))
    tab["iota8"] = np.broadcast_to(np.arange(E), (P, E))
    e = np.arange(E)
    tab["tri8"] = np.broadcast_to((e[None, :] < e[:, None]).reshape(1, E * E) * 1.0, (P, E * E))
    tab["tilestart"] = np.broadcast_to(np.arange(ROUTED) * float(P), (P, ROUTED))
    home = SLOTS + 2.0 * (np.arange(NT)[None, :] * P + p[:, None])
    tab["home"] = np.concatenate([home, home + 1], 1)
    tab["slot"] = np.arange(ROUTED)[None, :] * P + p[:, None]

    def pack(names):
        at, off = {}, 0
        for name in names:
            at[name] = (off, tab[name].shape[1])
            off += tab[name].shape[1]
        return np.ascontiguousarray(np.concatenate([tab[n] for n in names], 1, dtype=np.float64).astype(f)), at

    return pack([n for n in tab if n not in CAST]), pack(CAST)


CAST = ("selk", "selq", "causal", "causalT", "selg", "onehot", "gmask")
(CONST, CONST_AT), (TABLE, TABLE_AT) = constants()

W_COLS = {"k": (0, 256), "ks": (256, 256), "q": (512, 256), "qs": (768, 256), "v": (1024, 256),
          "gate": (1280, 32), "lm": (1312, 768), "lm_out": (2080, 256), "l2t_q": (2336, 256),
          "l2t_out": (2592, 256), "lm_kv": (2848, 512), "out": (3360, 256)}
W_TOTAL = 3616
B_COLS = {"k": 0, "ks": 2, "q": 4, "qs": 6, "lq": 8, "lk": 10, "lm_out": 12, "l2t_q": 14, "l2t_out": 16, "gk": 18}
B_TOTAL = 20
R_COLS = {"v": (0, 256), "gate": (256, 32), "lv": (288, 256), "gv": (544, 256), "out": (800, 256)}
R_TOTAL = 1056


def build(nc, x_d, const_d, table_d, wa_d, pq_d, ba_d, ra_d, wb_d, pb_d, wg_d, we_d, out_d):
    with ExitStack() as ctx:
        x = ctx.enter_context(nc.sbuf_tensor("x", [P, NT, D], F32))
        st6 = ctx.enter_context(nc.sbuf_tensor("st6", [P, 2 * NT, 6], F32))
        cst = ctx.enter_context(nc.sbuf_tensor("cst", [P, CONST.shape[1]], F32))
        mean = ctx.enter_context(nc.sbuf_tensor("mean", [P, NT], F32))
        rstd = ctx.enter_context(nc.sbuf_tensor("rstd", [P, NT], F32))
        rows_s = nc.dram_tensor("rows_s", (NT * P, D), F32, kind="Internal").ap()
        slots_x = nc.dram_tensor("slots_x", (2 * SLOTS, D + 1), F32, kind="Internal").ap()
        slots_y = nc.dram_tensor("slots_y", (SLOTS + 2 * NT * P, D), F32, kind="Internal").ap()
        banks = [ctx.enter_context(nc.psum_tensor(f"bank{i}", [P, 512], F32)) for i in range(8)]
        attention_a(nc, x, st6, cst, mean, rstd, banks, x_d, const_d, table_d, wa_d, pq_d, ba_d, ra_d, slots_x)
        experts_and_attention_b(nc, x, st6, cst, banks, wb_d, pb_d, wg_d, we_d, rows_s, slots_x, slots_y, out_d)


def const(cst, name, rows=slice(0, P)):
    off, n = CONST_AT[name]
    return cst[rows, off:off + n]


def table(stage, name, rows=slice(0, P)):
    off, n = TABLE_AT[name]
    return stage[rows, off:off + n]


def attention_a(nc, x, st6, cst, mean, rstd, bank, x_d, const_d, table_d, wa_d, pq_d, ba_d, ra_d, slots_x):
    with ExitStack() as ctx:
        def sb(name, shape, dt=F32):
            return ctx.enter_context(nc.sbuf_tensor(name, shape, dt))

        def sem(name):
            return ctx.enter_context(nc.semaphore(name))

        w = sb("wa", [P, KC, W_TOTAL])
        pq = sb("pq", [P, KC, HC * M])
        ba = sb("ba", [P, B_TOTAL])
        rb = sb("ra", [P, R_TOTAL])
        identb = sb("identb", [P, P], BF16)
        selk = sb("selk", [P, 4, 2, PARTS], BF16)
        selq = sb("selq", [P, 4, 2, PARTS], BF16)
        causal = sb("causal", [P, 8, S], BF16)
        causal_t = sb("causal_t", [P, 8, S], BF16)
        selg = sb("selg", [P, C8, P], BF16)
        onehot = sb("onehot", [NB, L], BF16)
        gmask = sb("gmask", [NB, HC, NL], BF16)
        zero = sb("zero", [P, D + 1])
        mv = sb("mv", [P, NT, 2])
        newton = sb("newton", [P, 2, NT])

        xn = sb("xn", [P, T, D])
        xnT = sb("xnT", [P, KC, L])
        rope_ab = sb("rope_ab", [P, 4, L])
        rope_a, rope_b = rope_ab[:, 0:2, :], rope_ab[:, 2:4, :]
        kqT = sb("kqT", [P, 4, L])
        hi = sb("hi", [P, 4, L], BF16)
        lo = sb("lo", [P, 4, L], BF16)
        ks = sb("ks", [P, C8, L], BF16)
        qs = sb("qs", [P, C8, L], BF16)
        kd = sb("kd", [P, 2, C8, HQ, P], BF16)
        qd = sb("qd", [P, C8, HQ, P], BF16)
        v = sb("v", [P, T, D])
        vd = sb("vd", [P, T, H, 32])
        gate = sb("gate", [P, 3, T * H])
        nm = sb("nm", [P, 2, H])
        nmh = sb("nmh", [P, 2, H, 2], BF16)
        pt = sb("pt", [P, 2, 8, S])
        r_sb = sb("r_sb", [P, C8, S])
        rec = sb("rec", [S, 2, 16])
        ol = sb("ol", [P, T, D])
        a_s = sb("a_s", [P, L])
        a_stat = sb("a_stat", [P, 4, NB])
        a_pt = sb("a_pt", [P, T, 2, P])
        a_m = sb("a_m", [P, NL, HC])
        lmT = sb("lmT", [P, 8, KC, NL])
        lmf, lq, lk, lo_T, lmf2, l2q, roT, lmf3 = range(8)
        gkT = sb("gkT", [P, KC, NL])
        lv = sb("lv", [NL, D])
        gv = sb("gv", [NL, D])
        lkbd = sb("lkbd", [P, KC, HC, NL])
        lvd = sb("lvd", [P, C8, 32])
        le = sb("le", [NL, H, NL])
        lstat = sb("lstat", [NL, 3, H])
        lpt = sb("lpt", [P, C8, NL])
        l2qbd = lkbd[:, :, :, :].rearrange("p c h k -> p c (h k)").rearrange("p c (n j) -> p c n j", n=NB)
        gkp = sb("gkp", [P, 2, KC, NL], BF16)
        gkd = sb("gkd", [PARTS, C8, HQ, NL], BF16)
        gvd = sb("gvd", [P, C8, 64])
        gnm = sb("gnm", [P, T, H])
        mm_ = sb("mm_", [P, L], BF16)
        pg = pt
        rg = rope_ab
        grec = sb("grec", [P, 2, H])
        og = xn
        oT = sb("oT", [P, 2, KC, P])

        stage = kd[:, :, :, :, :].rearrange("p a b c d -> p (a b c d)").bitcast(F32)
        d_c, d_t, d_w2 = sem("d_c"), sem("d_t"), sem("d_w2")
        W_FIRST = W_COLS["v"][0]
        d_w, d_x, x_in = sem("d_w"), [sem(f"d_x{i}") for i in range(B)], sem("x_in")
        c_ones, c_cast, c_stats, c_var, c_std = sem("c_ones"), sem("c_cast"), sem("c_stats"), sem("c_var"), sem("c_std")
        c_rstd, batch_open = sem("c_rstd"), sem("batch_open")
        (xn_ready, xn_t, xnT_ready, proj, rope_mul, rope, hi_ready, lo_ready, v_ps, v_ready, vd_ready, gate_ps,
         gate_z, gate_e, gate_ready, stack_ps, stack_k, stack_q, stack_q2, xb) = [sem(n) for n in (
             "xn_ready xn_t xnT_ready proj rope_mul rope hi_ready lo_ready v_ps v_ready vd_ready gate_ps "
             "gate_z gate_e gate_ready stack_ps stack_k stack_q stack_q2 xb").split()]
        (kd_ready, s_ps, smax, nmh_ready, nm_t, nm_row, qd_ready, st_ps, exps, pv, r_ready, r_t, rec_ready,
         ol_ready) = [sem(n) for n in (
             "kd_ready s_ps smax nmh_ready nm_t nm_row qd_ready st_ps exps pv r_ready r_t rec_ready "
             "ol_ready").split()]
        (at_s, at_sub, at_e, at_p, at_t, at_pt, at_o, at_red, lm_ps, lkbd_ready, lvd_ready, la_s, la_sub, la_e,
         la_p, la_t, la_pt, la_o, lo_ready_, lin_ps, lin_ready, gk_parts, gk_stack, gkd_ready, gvd_ready) = [sem(n) for n in (
             "at_s at_sub at_e at_p at_t at_pt at_o at_red lm_ps lkbd_ready lvd_ready la_s la_sub la_e "
             "la_p la_t la_pt la_o lo_T_ready lin_ps lin_ready gk_parts gk_stack gkd_ready gvd_ready").split()]
        (sg, gmax, gm_t, mm_hi, mm_lo, sgt, gexp, gpv, rg_ready, rg_t, og_ready, o_ready, o_t, oT_ready, y_ps,
         x_new) = [sem(n) for n in (
             "sg gmax gm_t mm_hi mm_lo sgt gexp gpv rg_ready rg_t og_ready o_ready o_t oT_ready y_ps "
             "x_new").split()]
        kd_last, qd_last = sem("kd_last"), sem("qd_last")
        dve_step = sem("dve_step")

        ident = const(cst, "ident")
        bank5b = bank[5][:, :].bitcast(BF16)
        block = ctx.enter_context(nc.Block())

        def wcol(name, k, lo_=0, n=None):
            off, full = W_COLS[name]
            return w[:, k, off + lo_:off + lo_ + (full if n is None else n)]

        def bcol(name, c):
            return ba[:, B_COLS[name] + c:B_COLS[name] + c + 1]

        def row(name, rows=slice(0, P)):
            off, n = R_COLS[name]
            return rb[rows, off:off + n]

        @block.sync
        def _(sp):
            xv = x_d.rearrange("b (t p) d -> b p t d", p=P)
            sp.dma_start(x[:, 0:T, :], xv[0]).then_inc(d_x[0], 16)
            sp.dma_start(cst[:, :], const_d).then_inc(d_c, 16)
            sp.dma_start(w[:, :, 0:W_FIRST], wa_d[:, :, 0:W_FIRST]).then_inc(d_w, 16)
            sp.dma_start(ba[:, :], ba_d).then_inc(d_w, 16)
            sp.dma_start(rb[:, :], ra_d).then_inc(d_w, 16)
            sp.dma_start(pq[:, :, :], pq_d).then_inc(d_w, 16)
            sp.dma_start(stage[:, 0:TABLE.shape[1]], table_d).then_inc(d_t, 16)
            for b in range(1, B):
                sp.dma_start(x[:, b * T:(b + 1) * T, :], xv[b]).then_inc(d_x[b], 16)
            sp.dma_start(w[:, :, W_FIRST:W_TOTAL], wa_d[:, :, W_FIRST:W_TOTAL]).then_inc(d_w2, 16)
            sp.wait_ge(x_in, 1)
            sp.dma_start(slots_x.rearrange("(j p) d -> p j d", p=P),
                         zero[:, :].unsqueeze(1).broadcast_to([P, 2 * ROUTED, D + 1])).then_inc(x_in, 16)
            sp.wait_ge(x_in, 17)

        @block.gpsimd
        def _(pool):
            pool.memset(zero[:, :], 0.0).then_inc(x_in, 1)
            n = 0
            for buf in (vd[:, :, :, :], a_pt[:, :, :, :], lvd[:, :, :], gvd[:, :, :]):
                pool.memset(buf, 0.0).then_inc(c_ones, 1)
                n += 1
            pool.wait_ge(d_w, 64)
            def projections(b):
                for t in range(T):
                    pool.wait_ge(xn_ready, b * T + t + 1)
                    pool.tensor_tensor(x[:, b * T + t, :], x[:, b * T + t, :], row("out"), ALU.add).then_inc(xb, 1)
                for r in range(4):
                    pool.wait_ge(rope_mul, b * 8 + 2 * r + 2)
                    pool.tensor_tensor(kqT[:, r, :], rope_a[:, r % 2, :], rope_b[:, r % 2, :],
                                       ALU.add).then_inc(rope, 1)
                    pool.wait_ge(hi_ready, b * 4 + r + 1)
                    pool.tensor_tensor(lo[:, r, :], kqT[:, r, :], hi[:, r, :], ALU.subtract).then_inc(lo_ready, 1)

            def local_share(b):
                pool.wait_ge(gate_ready, b + 1)
                for t in range(T):
                    pool.wait_ge(ol_ready, b * 16 + 4 * t + 4)
                    olv = ol[:, t, :].rearrange("p (h d) -> p h d", d=DH)
                    g = gate[:, 0, t * H:(t + 1) * H].unsqueeze(2).broadcast_to([P, H, DH])
                    pool.tensor_tensor(olv, olv, g, ALU.mult).then_inc(o_ready, 1)

            projections(0)
            with pool.Fori(0, B - 1) as b:
                local_share(b)
                projections(b + 1)
            local_share(B - 1)

        @block.scalar
        def _(act):
            def roots(n, cols):
                act.wait_ge(c_var, n + 1)
                act.activation(newton[:, 0, cols], newton[:, 0, cols], ACT.Sqrt).then_inc(c_std, 1)

            def casts():
                act.wait_ge(d_c, 16)
                act.wait_ge(d_t, 16)
                act.activation(identb[:, :], ident, ACT.Copy).then_inc(c_cast, 1)
                for dst, name in ((selk, "selk"), (selq, "selq")):
                    act.activation(dst[:, :, :, :].rearrange("p a b c -> p (a b c)"), table(stage, name),
                                   ACT.Copy).then_inc(c_cast, 1)
                for dst, name in ((causal, "causal"), (causal_t, "causalT")):
                    act.activation(dst[:, :, :], table(stage, name).unsqueeze(1).broadcast_to([P, 8, S]),
                                   ACT.Copy).then_inc(c_cast, 1)
                act.activation(selg[:, :, :].rearrange("p a b -> p (a b)"), table(stage, "selg"), ACT.Copy).then_inc(c_cast, 1)
                act.activation(onehot[:, :], table(stage, "onehot", slice(0, NB)), ACT.Copy).then_inc(c_cast, 1)
                act.activation(gmask[:, :, :], table(stage, "gmask", slice(0, NB)).unsqueeze(1).broadcast_to([NB, HC, NL]),
                               ACT.Copy).then_inc(c_cast, 1)
                act.activation(mm_[2 * H:2 * H + NB, :], table(stage, "onehot", slice(2 * H, 2 * H + NB)),
                               ACT.Copy).then_inc(c_cast, 1)

            def rows_turned(b):
                for p in range(2):
                    act.wait_ge(xn_t, b * T + 2 * p + 2)
                    act.activation(xnT[:, :, 2 * p * P:(2 * p + 2) * P].rearrange("p k (t c) -> p t k c", t=2),
                                   bank[p][:, :].rearrange("p (t k c) -> p t k c", t=2, k=KC),
                                   ACT.Copy).then_inc(xnT_ready, 1)

            def high_part(b, r):
                act.wait_ge(rope, b * 4 + r + 1)
                act.activation(hi[:, r, :], kqT[:, r, :], ACT.Copy).then_inc(hi_ready, 1)

            def values(b, t):
                act.wait_ge(v_ready, b * T + t + 1)
                vv = v[:, t, :].rearrange("p (h d) -> p h d", d=DH)
                for blk in range(2):
                    rows = slice(S * blk, S * blk + S)
                    act.activation(vd[rows, t, :, 16 * blk:16 * blk + DH], vv[rows], ACT.Copy).then_inc(vd_ready, 1)

            roots(0, slice(0, T))
            rows_turned(0)
            casts()
            for r in range(4):
                high_part(0, r)
            for t in range(T):
                values(0, t)

            def stacked_k(b, s):
                act.wait_ge(stack_ps, b * 16 + s + 1)
                act.activation(ks[0:PARTS, s, :], bank[s % 4][0:PARTS, :], ACT.Copy).then_inc(stack_k, 1)

            for s in range(8):
                stacked_k(0, s)
            roots(1, slice(T, NT))

            def batch(b, last):
                for s in range(8, 16, 2):
                    act.wait_ge(stack_ps, b * 16 + s + 1)
                    act.activation(qs[0:PARTS, s - 8, :], bank[s % 4][0:PARTS, :], ACT.Copy).then_inc(stack_q, 1)
                act.wait_ge(gate_z, b + 1)
                act.activation(gate[:, 1, :], gate[:, 0, :], ACT.Exp, scale=-1.0).then_inc(gate_e, 1)

                def attend_exp(a):
                    act.wait_ge(at_sub, b * 2 + a + 1)
                    act.activation(a_s[:, :], a_s[:, :], ACT.Exp, scale=SCALE).then_inc(at_e, 1)

                def attend_turned(a):
                    act.wait_ge(at_t, b * 2 + a + 1)
                    for blk in range(2):
                        rows = slice(S * blk, S * blk + S)
                        act.activation(a_pt[rows, :, blk, :],
                                       bank[7][rows, :].rearrange("p (t c) -> p t c", t=T),
                                       ACT.Copy).then_inc(at_pt, 1)

                def la_exp():
                    act.wait_ge(la_sub, b * 2 + 2)
                    act.activation(le[:, :, :], le[:, :, :], ACT.Exp, scale=SCALE).then_inc(la_e, 1)

                def la_turned():
                    act.wait_ge(la_t, b + 1)
                    act.activation(lpt[:, :, :].rearrange("p c q -> p (c q)"), bank[7][:, 0:C8 * NL],
                                   ACT.Copy).then_inc(la_pt, 1)

                def la_out():
                    act.wait_ge(la_o, b + 1)
                    act.activation(lmT[:, lo_T, :, :].rearrange("p c q -> p (c q)"), bank[7][:, 0:KC * NL],
                                   ACT.Copy).then_inc(lo_ready_, 1)

                def exp_unit(t, g):
                    u = 4 * t + g
                    act.wait_ge(st_ps, b * 16 + u + 1)
                    if u >= 2:
                        act.wait_ge(pv, b * 16 + u - 1)
                    act.activation(pt[:, g % 2, :, :].rearrange("p h q -> p (h q)"), bank[2 + g % 2][:, :],
                                   ACT.Exp, scale=SCALE).then_inc(exps, 1)

                def weighted_out(t):
                    act.wait_ge(pv, b * 16 + 4 * t + 4)
                    if t >= 1:
                        act.wait_ge(r_t, b * 8 + 2 * t)
                    act.activation(r_sb[:, :, :].rearrange("p c q -> p (c q)"), bank[4][:, :],
                                   ACT.Copy).then_inc(r_ready, 1)

                hm = const(cst, "headmask")

                def expand_k(t):
                    if t >= 2:
                        act.wait_ge(s_ps, b * 16 + 4 * (t - 1))
                    act.activation(kd[0:PARTS, t % 2, :, HQ - 1, :], ks[0:PARTS, :, t * P:(t + 1) * P], ACT.Copy,
                                   scale=hm[0:PARTS, HQ - 1:HQ]).then_inc(kd_last, 1)

                def expand_q(t):
                    if t == 0:
                        act.wait_ge(stack_q2, b * 4 + 4)
                    if t >= 1:
                        act.wait_ge(st_ps, b * 16 + 4 * t)
                    act.wait_ge(nm_row, b * T + t + 1)
                    act.activation(qd[0:ROWS, :, HQ - 1, :], qs[0:ROWS, :, t * P:(t + 1) * P], ACT.Copy,
                                   scale=hm[0:ROWS, HQ - 1:HQ]).then_inc(qd_last, 1)

                landmarks = {1: lambda: attend_turned(0), 6: la_exp, 8: la_turned, 9: la_out,
                             12: lambda: attend_exp(1), 14: lambda: attend_turned(1)}
                expand_k(0)
                expand_k(1)
                attend_exp(0)
                for t in range(T):
                    act.wait_ge(nm_t, b * T + t + 1)
                    act.activation(qs[PARTS:ROWS, :, t * P:(t + 1) * P],
                                   bank5b[0:2 * HQ, :].rearrange("p (c q) -> p c q", c=C8),
                                   ACT.Copy).then_inc(nm_row, 1)
                    expand_q(t)
                    if t >= 1:
                        weighted_out(t - 1)
                    for g in range(4):
                        exp_unit(t, g)
                        if g == 3 and t + 2 < T:
                            expand_k(t + 2)
                        if 4 * t + g in landmarks:
                            landmarks[4 * t + g]()
                weighted_out(T - 1)
                if not last:
                    rows_turned(b + 1)
                    for r in range(3):
                        high_part(b + 1, r)
                act.wait_ge(gm_t, b + 1)
                act.activation(mm_[0:H, :], bank[4][0:H, :], ACT.Copy).then_inc(mm_hi, 1)
                for c in range(C8):
                    act.wait_ge(sgt, b * C8 + c + 1)
                    if c >= 2:
                        act.wait_ge(gpv, b * C8 + c - 1)
                    act.activation(pg[:, c % 2, :, :].rearrange("p h q -> p (h q)"), bank[c % 4][:, :],
                                   ACT.Exp, scale=SCALE).then_inc(gexp, 1)
                    if c == 1 and not last:
                        high_part(b + 1, 3)
                for j in range(4):
                    act.wait_ge(gpv, b * C8 + 2 * j + 2)
                    act.activation(rg[:, j, :], bank[4 + j][:, :], ACT.Copy).then_inc(rg_ready, 1)
                for t in range(T):
                    act.wait_ge(o_t, b * T + t + 1)
                    if t >= 2:
                        act.wait_ge(y_ps, b * T + t - 1)
                    act.activation(oT[:, t % 2, :, :].rearrange("p k c -> p (k c)"), bank[4 + t % 2][:, 0:KC * P],
                                   ACT.Copy).then_inc(oT_ready, 1)
                    if not last:
                        stacked_k(b + 1, 2 * t)
                        stacked_k(b + 1, 2 * t + 1)
                if not last:
                    for t in range(T):
                        values(b + 1, t)

            with act.Fori(0, B - 1) as b:
                batch(b, False)
            batch(B - 1, True)

        @block.vector
        def _(dve):
            def link(ins, b, per, n):
                ins.then_inc(dve_step, 1)
                dve.wait_ge(dve_step, b * per + n)

            def statistics(n, batches):
                cols = slice(batches[0] * T, (batches[-1] + 1) * T)
                before = 2 * batches[0] * T
                tiles = len(batches) * T
                for i in batches:
                    dve.wait_ge(d_x[i], 16)
                    for t in range(i * T, (i + 1) * T):
                        dve.bn_stats(st6[:, t, :], x[:, t, :]).then_inc(c_stats, 1)
                for t in range(tiles):
                    dve.wait_ge(c_stats, before + tiles)
                    dve.bn_aggr(mv[:, cols.start + t, :], st6[:, cols.start + t, :]).then_inc(c_stats, 1)
                dve.wait_ge(c_stats, before + 2 * tiles)
                dve.tensor_copy(mean[:, cols], mv[:, cols, 0]).then_inc(c_rstd, 1)
                dve.tensor_scalar(newton[:, 0, cols], mv[:, cols, 1], LN_EPS, None, ALU.add).then_inc(c_var, 1)
                dve.wait_ge(c_std, n + 1)
                dve.reciprocal(rstd[:, cols], newton[:, 0, cols]).then_inc(c_rstd, 1)
                dve.wait_ge(c_rstd, 2 * n + 2)

            def rows(b):
                for t in range(T):
                    dve.tensor_scalar(xn[:, t, :], x[:, b * T + t, :],
                                      mean[:, bass.ds(b * T + t, 1)],
                                      rstd[:, bass.ds(b * T + t, 1)], ALU.subtract, ALU.mult).then_inc(xn_ready, 1)

            def rope_products(b, j):
                r = j // 2
                if r >= 2:
                    dve.wait_ge(rope, b * 4 + r - 1)
                dve.wait_ge(proj, b * 8 + j + 1)
                name, c = ("k", "k", "q", "q")[r], r % 2
                buf, name, tab = ((rope_a, name, "cos"), (rope_b, name + "s", "sin"))[j % 2]
                dve.scalar_tensor_tensor(buf[:, r % 2, :], bank[5 + j % 2][:, :], bcol(name, c), const(cst, tab),
                                         ALU.add, ALU.mult).then_inc(rope_mul, 1)

            def values(b, t):
                dve.wait_ge(v_ps, b * T + t + 1)
                dve.tensor_tensor(v[:, t, :], bank[6 + t % 2][:, 0:D], row("v"), ALU.add).then_inc(v_ready, 1)

            statistics(0, [0])
            rows(0)
            dve.wait_ge(c_ones, 4)
            dve.memset(vd[0:S, :, :, 8:9], 1.0).then_inc(c_ones, 1)
            dve.memset(vd[S:P, :, :, 24:25], 1.0).then_inc(c_ones, 1)
            for i in range(HQ):
                dve.memset(gvd[32 * i:32 * i + 32, :, 32 + i:33 + i], 1.0).then_inc(c_ones, 1)
            dve.memset(ks[PARTS:P, :, :], 1.0).then_inc(c_ones, 1)
            dve.wait_ge(d_c, 16)
            dve.wait_ge(d_w, 64)
            for j in range(8):
                rope_products(0, j)
            for t in range(T):
                values(0, t)
            statistics(1, [1, 2, 3])
            dve.wait_ge(c_ones, 11)
            dve.wait_ge(c_cast, 9)
            dve.memset(newton[:, 1, 0:1], 0.0).then_inc(batch_open, 1)

            def batch(b, last):
                count = [0]
                PER = DVE_LINKS_A

                def step(ins):
                    count[0] += 1
                    link(ins, b, PER, count[0])

                def gate_input():
                    dve.wait_ge(gate_ps, b + 1)
                    dve.tensor_tensor(gate[:, 0, :].rearrange("p (t h) -> p t h", t=T),
                                      bank[5][:, 0:T * H].rearrange("p (t h) -> p t h", t=T),
                                      row("gate").unsqueeze(1).broadcast_to([P, T, H]), ALU.add).then_inc(gate_z, 1)

                def gate_output():
                    dve.wait_ge(gate_e, b + 1)
                    step(dve.tensor_scalar(gate[:, 0, :], gate[:, 1, :], 1.0, None, ALU.add))
                    step(dve.reciprocal(gate[:, 2, :], gate[:, 0, :]))
                    dve.tensor_scalar(gate[:, 0, :], gate[:, 2, :], -1.0, 1.0, ALU.mult, ALU.add)\
                       .then_inc(gate_ready, 1)

                bd = const(cst, "bd16")
                hm = const(cst, "headmask")

                sv = bank[7][:, :].rearrange("p (n s) -> p n s", n=NB)
                av = a_s[:, :].rearrange("p (n s) -> p n s", n=NB)

                def attend_max(a):
                    dve.wait_ge(at_s, b * 2 + a + 1)
                    step(dve.tensor_reduce(a_stat[:, 0, :], sv, AX.X, ALU.max))
                    dve.tensor_tensor(av, sv, a_stat[:, 0, :].unsqueeze(2).broadcast_to([P, NB, S]),
                                      ALU.subtract).then_inc(at_sub, 1)

                def attend_norm(a):
                    dve.wait_ge(at_e, b * 2 + a + 1)
                    step(dve.tensor_reduce(a_stat[:, 1, :], av, AX.X, ALU.add))
                    step(dve.reciprocal(a_stat[:, 2, :], a_stat[:, 1, :]))
                    dve.tensor_tensor(av, av, a_stat[:, 2, :].unsqueeze(2).broadcast_to([P, NB, S]),
                                      ALU.mult).then_inc(at_p, 1)

                def attend_out(a, dst, c):
                    dve.wait_ge(at_o, b * 4 + a * 2 + c + 1)
                    step(dve.tensor_tensor(
                        a_m[:, :, :].rearrange("p (n m) h -> p n h m", n=NB),
                        bank[7][:, :].rearrange("p (n h m) -> p n h m", n=NB, h=HC),
                        bd.unsqueeze(1).unsqueeze(3).broadcast_to([P, NB, HC, M]), ALU.mult))
                    dve.tensor_reduce(lmT[:, dst, c, :], a_m[:, :, :], AX.X, ALU.add).then_inc(at_red, 1)

                def spread(dst, src, signal):
                    for i in range(HQ):
                        dve.tensor_copy(dst[32 * i:32 * i + 32, :, DH * i:DH * i + DH],
                                        src[:, :].rearrange("k (c i d) -> k c i d", i=HQ, d=DH)[:, :, i, :])\
                           .then_inc(signal, 1)

                def block_diagonal(dst, src, signal):
                    for c in range(KC):
                        dve.tensor_tensor(dst[:, c, :, :], src[c].unsqueeze(1).broadcast_to([P, HC, NL]),
                                          bd.unsqueeze(2).broadcast_to([P, HC, NL]), ALU.mult).then_inc(signal, 1)

                def landmarks_qkv():
                    dve.wait_ge(lm_ps, b * 2 + 1)
                    for c in range(KC):
                        dve.tensor_scalar(lmT[:, lq, c, :], bank[7][:, c * NL:(c + 1) * NL], bcol("lq", c), None,
                                          ALU.add).then_inc(lkbd_ready, 1)
                    for c in range(KC):
                        dve.tensor_scalar(lmT[:, lk, c, :], bank[7][:, (2 + c) * NL:(3 + c) * NL], bcol("lk", c), None,
                                          ALU.add).then_inc(lkbd_ready, 1)
                    step(dve.tensor_tensor(lv[:, :], bank[7][0:NL, P:P + D], row("lv", slice(0, NL)), ALU.add))
                    block_diagonal(lkbd, [lmT[:, lk, c, :] for c in range(KC)], lkbd_ready)
                    spread(lvd, lv, lvd_ready)

                def la_max(c):
                    dve.wait_ge(la_s, b * 2 + c + 1)
                    lsv = bank[7][0:NL, :].rearrange("q (h k) -> q h k", h=HC)
                    step(dve.tensor_reduce(lstat[:, 0, HC * c:HC * c + HC], lsv, AX.X, ALU.max))
                    dve.tensor_tensor(le[:, HC * c:HC * c + HC, :], lsv,
                                      lstat[:, 0, HC * c:HC * c + HC].unsqueeze(2).broadcast_to([NL, HC, NL]),
                                      ALU.subtract).then_inc(la_sub, 1)

                def la_norm():
                    dve.wait_ge(la_e, b + 1)
                    step(dve.tensor_reduce(lstat[:, 1, :], le[:, :, :], AX.X, ALU.add))
                    step(dve.reciprocal(lstat[:, 2, :], lstat[:, 1, :]))
                    dve.tensor_tensor(le[:, :, :], le[:, :, :],
                                      lstat[:, 2, :].unsqueeze(2).broadcast_to([NL, H, NL]), ALU.mult).then_inc(la_p, 1)

                def linear(n, name, dst, add):
                    dve.wait_ge(lin_ps, b * 3 + n + 1)
                    for c in range(KC):
                        src = bank[7][:, c * NL:(c + 1) * NL]
                        if add is None:
                            ins = dve.tensor_scalar(lmT[:, dst, c, :], src, bcol(name, c), None, ALU.add)
                        else:
                            ins = dve.scalar_tensor_tensor(lmT[:, dst, c, :], src, bcol(name, c), lmT[:, add, c, :],
                                                           ALU.add, ALU.add)
                        ins.then_inc(lin_ready, 1)

                def queries_to_blocks():
                    dve.wait_ge(lin_ready, b * 8 + 4)
                    for c in range(KC):
                        dve.tensor_tensor(l2qbd[:, c, :, :].rearrange("p n (h m) -> p n h m", h=HC),
                                          lmT[:, l2q, c, :].rearrange("p (n m) -> p n m", n=NB).unsqueeze(2)
                                          .broadcast_to([P, NB, HC, M]),
                                          bd.unsqueeze(1).unsqueeze(3).broadcast_to([P, NB, HC, M]),
                                          ALU.mult).then_inc(lin_ready, 1)

                def landmarks_kv():
                    dve.wait_ge(lm_ps, b * 2 + 2)
                    for c in range(KC):
                        ins = dve.tensor_scalar(gkT[:, c, :], bank[7][:, c * NL:(c + 1) * NL], bcol("gk", c), None,
                                                ALU.add)
                        step(ins)
                    step(dve.tensor_tensor(gv[:, :], bank[7][0:NL, P:P + D], row("gv", slice(0, NL)), ALU.add))
                    step(dve.tensor_copy(gkp[:, 0, :, :], gkT[:, :, :]))
                    dve.tensor_tensor(gkp[:, 1, :, :], gkT[:, :, :], gkp[:, 0, :, :], ALU.subtract)\
                       .then_inc(gk_parts, 1)
                    spread(gvd, gv, gvd_ready)
                    if not last:
                        rope_products(b + 1, 0)
                    dve.wait_ge(gk_stack, b + 1)
                    dve.tensor_tensor(gkd[:, :, :, :], bank[7][0:PARTS, 0:C8 * NL].rearrange("p (c k) -> p c k", c=C8)
                                      .unsqueeze(2).broadcast_to([PARTS, C8, HQ, NL]),
                                      hm[0:PARTS, :].unsqueeze(1).unsqueeze(3).broadcast_to([PARTS, C8, HQ, NL]),
                                      ALU.mult).then_inc(gkd_ready, 1)

                def expand_k(t):
                    if t == 0:
                        dve.wait_ge(stack_k, b * 8 + 8)
                    if t >= 2:
                        dve.wait_ge(s_ps, b * 16 + 4 * (t - 1))
                    for i in range(HQ - 1):
                        dve.tensor_scalar(kd[0:PARTS, t % 2, :, i, :], ks[0:PARTS, :, t * P:(t + 1) * P],
                                          hm[0:PARTS, i:i + 1], None, ALU.mult).then_inc(kd_ready, 1)

                def maximum(t, g):
                    dve.wait_ge(s_ps, b * 16 + 4 * t + g + 1)
                    dve.tensor_reduce(nm[:, t % 2, 8 * g:8 * g + 8],
                                      bank[g % 2][:, :].rearrange("p (h k) -> p h k", h=8), AX.X, ALU.max,
                                      negate=True).then_inc(smax, 1)
                    if g == 3:
                        dve.wait_ge(smax, b * 16 + 4 * t + 4)
                        step(dve.tensor_copy(nmh[:, t % 2, :, 0], nm[:, t % 2, :]))
                        dve.tensor_tensor(nmh[:, t % 2, :, 1], nm[:, t % 2, :], nmh[:, t % 2, :, 0],
                                          ALU.subtract).then_inc(nmh_ready, 1)

                def expand_q(t):
                    dve.wait_ge(nm_row, b * T + t + 1)
                    if t == 0:
                        dve.wait_ge(stack_q, b * 4 + 4)
                        dve.wait_ge(stack_q2, b * 4 + 4)
                    if t >= 1:
                        dve.wait_ge(st_ps, b * 16 + 4 * t)
                    for i in range(HQ - 1):
                        dve.tensor_scalar(qd[0:ROWS, :, i, :], qs[0:ROWS, :, t * P:(t + 1) * P],
                                          hm[0:ROWS, i:i + 1], None, ALU.mult).then_inc(qd_ready, 1)

                def normalise(t, hf):
                    dve.wait_ge(r_t, b * 8 + 2 * t + hf + 1)
                    rv = bank[6][0:S, :].rearrange("q (h c) -> q h c", c=32)
                    for blk in range(2):
                        dve.reciprocal(rec[:, blk, :], rv[:, :, 16 * blk + DH]).then_inc(rec_ready, 1)
                    for blk in range(2):
                        dve.wait_ge(rec_ready, b * 16 + 4 * t + 2 * hf + blk + 1)
                        dve.tensor_tensor(
                            ol[S * blk:S * blk + S, t, hf * P:(hf + 1) * P].rearrange("q (h d) -> q h d", d=DH),
                            rv[:, :, 16 * blk:16 * blk + DH],
                            rec[:, blk, :].unsqueeze(2).broadcast_to([S, 16, DH]), ALU.mult).then_inc(ol_ready, 1)

                def queries():
                    linear(1, "l2t_q", l2q, None)
                    queries_to_blocks()

                landmarks = {0: lambda: attend_norm(0), 2: lambda: attend_out(0, lmf, 0),
                             3: lambda: attend_out(0, lmf, 1), 4: landmarks_qkv, 5: lambda: la_max(0),
                             6: lambda: la_max(1), 7: la_norm, 10: lambda: linear(0, "lm_out", lmf2, lmf), 11: queries,
                             12: lambda: attend_max(1), 13: lambda: attend_norm(1),
                             15: lambda: attend_out(1, roT, 0)}
                if not last:
                    landmarks[14] = lambda: rows(b + 1)

                expand_k(0)
                for s in range(9, 16, 2):
                    dve.wait_ge(stack_ps, b * 16 + s + 1)
                    dve.tensor_copy(qs[0:PARTS, s - 8, :], bank[s % 4][0:PARTS, :]).then_inc(stack_q2, 1)
                gate_input()
                expand_k(1)
                attend_max(0)
                for g in range(4):
                    maximum(0, g)
                gate_output()
                for t in range(T):
                    if t + 1 < T:
                        maximum(t + 1, 0)
                        maximum(t + 1, 1)
                    expand_q(t)
                    for g in range(4):
                        if t >= 1 and g < 2:
                            normalise(t - 1, g)
                        if 1 <= g < 3 and t + 1 < T:
                            maximum(t + 1, g + 1)
                        if g == 3 and t + 2 < T:
                            expand_k(t + 2)
                        if 4 * t + g in landmarks:
                            landmarks[4 * t + g]()
                normalise(T - 1, 0)
                attend_out(1, roT, 1)
                normalise(T - 1, 1)
                linear(2, "l2t_out", lmf3, lmf2)

                landmarks_kv()
                if not last:
                    rope_products(b + 1, 1)
                for t in range(T):
                    for c in range(KC):
                        dve.wait_ge(sg, b * 8 + 2 * t + c + 1)
                        dve.tensor_reduce(gnm[:, t, HC * c:HC * c + HC],
                                          bank[2 * (t % 2) + c][:, :].rearrange("p (h k) -> p h k", h=HC), AX.X,
                                          ALU.max, negate=True).then_inc(gmax, 1)
                    if not last:
                        rope_products(b + 1, 2 + t)
                dve.wait_ge(gmax, b * 9 + 2)
                dve.tensor_scalar(gnm[:, 0, :], gnm[:, 0, :], const(cst, "valid"), None, ALU.mult).then_inc(gmax, 1)
                dve.wait_ge(mm_hi, b + 1)
                dve.tensor_tensor(mm_[H:2 * H, :], bank[4][0:H, :], mm_[0:H, :], ALU.subtract).then_inc(mm_lo, 1)
                if not last:
                    rope_products(b + 1, 6)
                    rope_products(b + 1, 7)
                for t in range(T):
                    dve.wait_ge(rg_t, b * T + t + 1)
                    gvw = bank[t][:, :].rearrange("p (c j) -> p c j", c=C8)
                    step(dve.tensor_scalar(grec[:, 0, :].rearrange("p (c i) -> p c i", c=C8), gvw[:, :, 32:36],
                                           SUM_EPS, None, ALU.max))
                    step(dve.reciprocal(grec[:, 1, :], grec[:, 0, :]))
                    step(dve.tensor_tensor(grec[:, 1, :], grec[:, 1, :], gate[:, 2, t * H:(t + 1) * H], ALU.mult))
                    dve.tensor_tensor(og[:, t, :].rearrange("p (c i d) -> p c i d", c=C8, i=HQ),
                                      gvw[:, :, 0:32].rearrange("p c (i d) -> p c i d", i=HQ),
                                      grec[:, 1, :].rearrange("p (c i) -> p c i", c=C8).unsqueeze(3)
                                      .broadcast_to([P, C8, HQ, DH]), ALU.mult).then_inc(og_ready, 1)
                for t in range(T):
                    if not last and t < 2:
                        values(b + 1, 2 * t)
                        values(b + 1, 2 * t + 1)
                    dve.wait_ge(y_ps, b * T + t + 1)
                    dve.wait_ge(xb, b * T + t + 1)
                    dve.tensor_tensor(x[:, b * T + t, :], bank[4 + t % 2][:, D:2 * D], x[:, b * T + t, :],
                                      ALU.add).then_inc(x_new, 1)
                dve.wait_ge(x_new, b * T + T)
                dve.memset(newton[:, 1, 0:1], 0.0).then_inc(batch_open, 1)
                for t in range(T):
                    dve.bn_stats(st6[:, b * T + t, :], x[:, b * T + t, :]).then_inc(c_stats, 1)
                assert count[0] == PER, count[0]

            with dve.Fori(0, B - 1) as b:
                batch(b, False)
            batch(B - 1, True)

        @block.tensor
        def _(pe):
            def mm(out, lhs, rhs, start=True, stop=True):
                return pe.matmul(out, lhs, rhs, start=start, stop=stop, skip_group_check=True)

            pe.wait_ge(d_c, 16)

            def rows_turned(b):
                for t in range(T):
                    pe.wait_ge(xn_ready, b * T + t + 1)
                    for k in range(KC):
                        ins = pe.transpose(bank[t // 2][:, (t % 2) * 256 + k * P:(t % 2) * 256 + (k + 1) * P],
                                           xn[:, t, k * P:(k + 1) * P], ident)
                    ins.then_inc(xn_t, 1)

            def projection(b, j):
                if j == 0:
                    pe.wait_ge(xnT_ready, b * 2 + 2)
                if j >= 2:
                    pe.wait_ge(rope_mul, b * 8 + j - 1)
                name, c = ("k", "ks", "k", "ks", "q", "qs", "q", "qs")[j], j // 2 % 2
                for k in range(KC):
                    ins = mm(bank[5 + j % 2][:, :], wcol(name, k, c * P, P), xnT[:, k, :], k == 0, k == KC - 1)
                ins.then_inc(proj, 1)

            def values(b, t):
                if t >= 2:
                    pe.wait_ge(v_ready, b * T + t - 1)
                for k in range(KC):
                    ins = mm(bank[6 + t % 2][:, 0:D], xnT[:, k, t * P:(t + 1) * P], wcol("v", k),
                             k == 0, k == KC - 1)
                ins.then_inc(v_ps, 1)

            rows_turned(0)
            pe.wait_ge(d_w, 64)
            for j in range(8):
                projection(0, j)
            pe.wait_ge(rope_mul, 8)
            pe.wait_ge(d_w2, 16)
            for t in range(T):
                values(0, t)

            def stack(b, s):
                r = s // 4
                pe.wait_ge(lo_ready, b * 4 + r + 1)
                if 4 <= s < 12:
                    pe.wait_ge(stack_k, b * 8 + s - 3)
                elif s >= 12 and s % 2 == 0:
                    pe.wait_ge(stack_q, b * 4 + (s - 12) // 2 + 1)
                elif s >= 12:
                    pe.wait_ge(stack_q2, b * 4 + (s - 12) // 2 + 1)
                sel = selk if s < 8 else selq
                mm(bank[s % 4][0:PARTS, :], sel[:, s % 4, 0, :], hi[:, r, :], True, False)
                mm(bank[s % 4][0:PARTS, :], sel[:, s % 4, 1, :], lo[:, r, :], False, True).then_inc(stack_ps, 1)

            pe.wait_ge(c_cast, 9)
            for s in range(8):
                stack(0, s)

            def batch(b, last):
                for s in range(8, 16):
                    stack(b, s)
                pe.wait_ge(batch_open, b + 1)
                for t in range(T):
                    for k in range(KC):
                        ins = mm(bank[5][:, t * H:(t + 1) * H], xnT[:, k, t * P:(t + 1) * P], wcol("gate", k),
                                 k == 0, k == KC - 1)
                ins.then_inc(gate_ps, 1)

                def attend_scores(a):
                    if a == 0:
                        pe.wait_ge(rope, b * 4 + 4)
                        pe.wait_ge(v_ready, b * T + T)
                        for c in range(KC):
                            ins = mm(bank[7][64 * c:64 * c + 64, :], pq[:, c, :], kqT[:, c, :])
                    else:
                        pe.wait_ge(lin_ready, b * 8 + 6)
                        for n in range(NB):
                            for c in range(KC):
                                ins = mm(bank[7][64 * c:64 * c + 64, n * S:(n + 1) * S], l2qbd[:, c, n, :],
                                         kqT[:, c, n * S:(n + 1) * S])
                    ins.then_inc(at_s, 1)

                def attend_turn(a):
                    pe.wait_ge(at_p, b * 2 + a + 1)
                    for t in range(T):
                        ins = pe.transpose(bank[7][:, t * P:(t + 1) * P], a_s[:, t * P:(t + 1) * P], ident)
                    ins.then_inc(at_t, 1)

                def attend_out(a, c):
                    pe.wait_ge(at_pt, b * 4 + 2 * a + 2)
                    if c:
                        pe.wait_ge(at_red, b * 4 + 2 * a + 1)
                    for t in range(T):
                        ins = mm(bank[7][:, t * P:(t + 1) * P], v[:, t, c * P:(c + 1) * P],
                                 a_pt[:, t, :, 64 * c:64 * c + 64])
                    ins.then_inc(at_o, 1)

                def project(name, src, lo_, n, chunks):
                    for c in range(chunks):
                        for k in range(KC):
                            ins = mm(bank[7][:, c * NL:(c + 1) * NL], wcol(name, k, lo_ + c * P, P), lmT[:, src, k, :],
                                     k == 0, k == KC - 1)
                    return ins

                def rows(name, src, lo_):
                    for k in range(KC):
                        ins = mm(bank[7][0:NL, P:P + D], lmT[:, src, k, :], wcol(name, k, lo_, D), k == 0, k == KC - 1)
                    return ins

                def landmarks_qkv():
                    pe.wait_ge(at_red, b * 4 + 2)
                    project("lm", lmf, 0, P, 4)
                    rows("lm", lmf, 2 * D).then_inc(lm_ps, 1)

                def la_scores(c):
                    if c == 0:
                        pe.wait_ge(lkbd_ready, b * 6 + 6)
                        pe.wait_ge(lvd_ready, b * 4 + 4)
                    else:
                        pe.wait_ge(la_sub, b * 2 + 1)
                    mm(bank[7][0:NL, :], lmT[:, lq, c, :], lkbd[:, c, :, :], True, False)
                    mm(bank[7][0:NL, :], ident[0:NL, 0:NL],
                       const(cst, "lamask", slice(0, NL)).unsqueeze(1).broadcast_to([NL, HC, NL]),
                       False, True).then_inc(la_s, 1)

                def la_turn():
                    pe.wait_ge(d_w, 64)
                    pe.wait_ge(la_p, b + 1)
                    for c in range(C8):
                        ins = pe.transpose(bank[7][:, c * NL:(c + 1) * NL],
                                           le[:, HQ * c:HQ * c + HQ, :].rearrange("q h k -> q (h k)"),
                                           ident[0:NL, 0:NL])
                    ins.then_inc(la_t, 1)

                def la_weighted():
                    pe.wait_ge(la_pt, b + 1)
                    for c in range(C8):
                        i = c % 4
                        ins = mm(bank[7][32 * i:32 * i + 32, (c // 4) * NL:(c // 4 + 1) * NL], lvd[:, c, :],
                                 lpt[:, c, :])
                    ins.then_inc(la_o, 1)

                def la_project():
                    pe.wait_ge(lo_ready_, b + 1)
                    project("lm_out", lo_T, 0, P, KC).then_inc(lin_ps, 1)

                def queries():
                    pe.wait_ge(lin_ready, b * 8 + 2)
                    project("l2t_q", lmf2, 0, P, KC).then_inc(lin_ps, 1)

                def token_project():
                    pe.wait_ge(at_red, b * 4 + 4)
                    project("l2t_out", roT, 0, P, KC).then_inc(lin_ps, 1)

                def scores(t, g):
                    u = 4 * t + g
                    if u == 0:
                        pe.wait_ge(stack_q, b * 4 + 4)
                        pe.wait_ge(stack_q2, b * 4 + 4)
                    if g == 0:
                        pe.wait_ge(kd_ready, b * 12 + 3 * t + 3)
                        pe.wait_ge(kd_last, b * T + t + 1)
                    if u >= 2:
                        pe.wait_ge(smax, b * 16 + u - 1)
                    mm(bank[g % 2][:, :], identb[:, :], causal[:, :, :].rearrange("p h k -> p (h k)"), True, False)
                    for c in (2 * g, 2 * g + 1):
                        for blk in range(2):
                            ins = mm(bank[g % 2][S * blk:S * blk + S, (c % 2) * 256:(c % 2) * 256 + 256],
                                     qs[0:PARTS, c, t * P + S * blk:t * P + S * blk + S],
                                     kd[0:PARTS, t % 2, c, :, S * blk:S * blk + S], False, c % 2 == 1)
                    ins.then_inc(s_ps, 1)

                def maxima_rows(t):
                    pe.wait_ge(nmh_ready, b * T + t + 1)
                    if t == 0:
                        pe.wait_ge(gate_z, b + 1)
                    if t >= 1:
                        pe.wait_ge(nm_row, b * T + t)
                    for c in range(C8):
                        ins = pe.transpose(bank5b[0:2 * HQ, c * P:(c + 1) * P],
                                           nmh[:, t % 2, HQ * c:HQ * c + HQ, :].rearrange("p h j -> p (h j)"),
                                           identb[:, :])
                    ins.then_inc(nm_t, 1)

                def scores_t(t, g):
                    u = 4 * t + g
                    if g == 0:
                        pe.wait_ge(qd_ready, b * 12 + 3 * t + 3)
                        pe.wait_ge(qd_last, b * T + t + 1)
                    if u >= 2:
                        pe.wait_ge(exps, b * 16 + u - 1)
                    mm(bank[2 + g % 2][:, :], identb[:, :], causal_t[:, :, :].rearrange("p h k -> p (h k)"), True, False)
                    for c in (2 * g, 2 * g + 1):
                        for blk in range(2):
                            ins = mm(bank[2 + g % 2][S * blk:S * blk + S, (c % 2) * 256:(c % 2) * 256 + 256],
                                     ks[0:ROWS, c, t * P + S * blk:t * P + S * blk + S],
                                     qd[0:ROWS, c, :, S * blk:S * blk + S], False, c % 2 == 1)
                    ins.then_inc(st_ps, 1)

                def weighted(t, g):
                    u = 4 * t + g
                    if g == 0:
                        pe.wait_ge(vd_ready, b * 8 + 2 * t + 2)
                        if t >= 1:
                            pe.wait_ge(r_ready, b * T + t)
                    pe.wait_ge(exps, b * 16 + u + 1)
                    for j in range(8):
                        h = 8 * g + j
                        c, i = h // HQ, h % HQ
                        ins = mm(bank[4][32 * i:32 * i + 32, c * S:(c + 1) * S], vd[:, t, h, :], pt[:, g % 2, j, :])
                    ins.then_inc(pv, 1)

                def turn(t, hf):
                    pe.wait_ge(d_w, 64)
                    if hf == 0:
                        pe.wait_ge(r_ready, b * T + t + 1)
                    if 2 * t + hf >= 1:
                        pe.wait_ge(ol_ready, b * 16 + 2 * (2 * t + hf))
                    for j in range(4):
                        ins = pe.transpose(bank[6][0:S, j * P:(j + 1) * P], r_sb[:, 4 * hf + j, :], ident)
                    ins.then_inc(r_t, 1)

                attend_scores(0)
                landmarks = {1: lambda: attend_turn(0), 2: lambda: attend_out(0, 0), 3: lambda: attend_out(0, 1),
                             4: landmarks_qkv, 5: lambda: la_scores(0), 6: lambda: la_scores(1), 8: la_turn,
                             9: la_weighted, 10: la_project, 11: queries, 12: lambda: attend_scores(1),
                             14: lambda: attend_turn(1), 15: lambda: attend_out(1, 0)}
                late = (5, 6, 10, 11)
                for g in range(4):
                    scores(0, g)
                for t in range(T):
                    maxima_rows(t)
                    if t + 1 < T:
                        scores(t + 1, 0)
                        scores(t + 1, 1)
                    if t >= 1:
                        weighted(t - 1, 3)
                    for g in range(4):
                        if t >= 1 and g < 2:
                            turn(t - 1, g)
                        if 4 * t + g in landmarks and 4 * t + g not in late:
                            landmarks[4 * t + g]()
                        scores_t(t, g)
                        if 4 * t + g in late:
                            landmarks[4 * t + g]()
                        if 1 <= g + 1 < 3 and t + 1 < T:
                            scores(t + 1, g + 2)
                        if g >= 1:
                            weighted(t, g - 1)
                weighted(T - 1, 3)
                attend_out(1, 1)
                turn(T - 1, 0)
                if not last:
                    pe.wait_ge(smax, b * 16 + 16)
                    rows_turned(b + 1)
                turn(T - 1, 1)
                token_project()

                pe.wait_ge(lin_ready, b * 8 + 8)
                project("lm_kv", lmf3, 0, P, KC)
                rows("lm_kv", lmf3, D).then_inc(lm_ps, 1)
                if not last:
                    pe.wait_ge(nm_row, b * T + T)
                    projection(b + 1, 0)
                pe.wait_ge(d_w, 64)
                pe.wait_ge(gk_parts, b + 1)
                for c in range(C8):
                    out = bank[7][0:PARTS, c * NL:(c + 1) * NL]
                    mm(out, selk[:, c % 4, 0, :], gkp[:, 0, c // 4, :], True, False)
                    ins = mm(out, selk[:, c % 4, 1, :], gkp[:, 1, c // 4, :], False, True)
                ins.then_inc(gk_stack, 1)
                if not last:
                    pe.wait_ge(ol_ready, b * 16 + 16)
                    projection(b + 1, 1)
                pe.wait_ge(gkd_ready, b + 1)
                pe.wait_ge(smax, b * 16 + 16)
                for t in range(T):
                    for c in range(KC):
                        if t >= 2:
                            pe.wait_ge(gmax, b * 9 + 2 * (t - 2) + c + 1)
                        out = bank[2 * (t % 2) + c][:, :]
                        mm(out, onehot[:, t * P:(t + 1) * P], gmask[:, :, :].rearrange("n h k -> n (h k)"), True, False)
                        for j in range(4):
                            ins = mm(out[:, j * P:(j + 1) * P], qs[0:PARTS, 4 * c + j, t * P:(t + 1) * P],
                                     gkd[:, 4 * c + j, :, :].rearrange("p h k -> p (h k)"), False, j == 3)
                        ins.then_inc(sg, 1)
                    if not last:
                        projection(b + 1, 2 + t)
                pe.wait_ge(gmax, b * 9 + 9)
                pe.wait_ge(r_ready, b * T + T)
                for t in range(T):
                    ins = pe.transpose(bank[4][0:H, t * P:(t + 1) * P], gnm[:, t, :], ident)
                ins.then_inc(gm_t, 1)

                def global_scores(c):
                    if c >= 4:
                        pe.wait_ge(gexp, b * C8 + c - 3)
                    mm(bank[c % 4][:, :], selg[0:2 * H + NB, c, :], mm_[0:2 * H + NB, :], True, False)
                    mm(bank[c % 4][:, :], gkd[:, c, :, :].rearrange("p h k -> p (h k)"), qs[0:PARTS, c, :],
                       False, True).then_inc(sgt, 1)

                def global_weighted(c):
                    if c == 2:
                        if last:
                            pe.wait_ge(ol_ready, b * 16 + 16)
                            pe.wait_ge(nm_row, b * T + T)
                        else:
                            pe.wait_ge(rope_mul, (b + 1) * 8 + 8)
                    pe.wait_ge(gexp, b * C8 + c + 1)
                    mm(bank[4 + c // 2][64 * (c % 2):64 * (c % 2) + 64, :], gvd[:, c, :],
                       pg[:, c % 2, :, :].rearrange("p h q -> p (h q)")).then_inc(gpv, 1)

                if not last:
                    projection(b + 1, 6)
                    projection(b + 1, 7)
                pe.wait_ge(mm_lo, b + 1)
                pe.wait_ge(gvd_ready, b * 4 + 4)
                global_scores(0)
                for c in range(1, C8):
                    global_scores(c)
                    global_weighted(c - 1)
                global_weighted(C8 - 1)
                pe.wait_ge(rg_ready, b * 4 + 4)
                for t in range(T):
                    for j in range(4):
                        ins = pe.transpose(bank[t][:, j * P:(j + 1) * P], rg[:, j, t * P:(t + 1) * P], ident)
                    ins.then_inc(rg_t, 1)
                if not last:
                    values(b + 1, 0)
                    values(b + 1, 1)
                for t in range(T):
                    pe.wait_ge(o_ready, b * T + t + 1)
                    pe.wait_ge(og_ready, b * T + t + 1)
                    if t >= 2:
                        pe.wait_ge(x_new, b * T + t - 1)
                    for k in range(KC):
                        out = bank[4 + t % 2][:, k * P:(k + 1) * P]
                        mm(out, ol[:, t, k * P:(k + 1) * P], ident, True, False)
                        ins = mm(out, og[:, t, k * P:(k + 1) * P], ident, False, True)
                    ins.then_inc(o_t, 1)
                    if not last:
                        if t < 2:
                            values(b + 1, 2 + t)
                        if t == 0:
                            pe.wait_ge(og_ready, b * T + T)
                        stack(b + 1, 2 * t)
                        stack(b + 1, 2 * t + 1)
                    pe.wait_ge(oT_ready, b * T + t + 1)
                    for k in range(KC):
                        ins = mm(bank[4 + t % 2][:, D:2 * D], oT[:, t % 2, k, :], wcol("out", k), k == 0, k == KC - 1)
                    ins.then_inc(y_ps, 1)

            with pe.Fori(0, B - 1) as b:
                batch(b, False)
            batch(B - 1, True)


DVE_LINKS_A = 37


def experts_and_attention_b(nc, x, st6, cst, bank, wb_d, pb_d, wg_d, we_d, rows_s, slots_x, slots_y, out_d):
    with ExitStack() as ctx:
        def sb(name, shape, dt=F32):
            return ctx.enter_context(nc.sbuf_tensor(name, shape, dt))

        def sem(name):
            return ctx.enter_context(nc.semaphore(name))

        wh = sb("wh", [P, 3 * NW, WCOL], BF16)
        wl = sb("wl", [P, 3 * NW, WCOL], BF16)
        stage = sb("stage", [P, 3, WCOL])
        wb = sb("wb", [P, KC, QKVB])
        pb = sb("pb", [P, KC, D])
        wg = sb("wg", [P, KC, E])
        mv = sb("mvb", [P, 2 * NT, 2])
        var = sb("var", [P, 2 * NT])
        mean = sb("meanb", [P, 2 * NT])
        rstd = sb("rstdb", [P, 2 * NT])
        xn = sb("xnb", [P, NT, D + 1])
        xT = sb("xTb", [P, 2, 2, KC, P])
        oT = sb("oTb", [P, 2, 2, KC, P])
        prob = sb("prob", [P, NT, E])
        key = sb("key", [P, NT, E])
        eq = sb("eq", [P, NT, E])
        pick = sb("pick", [P, 2, NT, E])
        pickb = sb("pickb", [P, NT, E], BF16)
        trib = sb("trib", [P, P], BF16)
        onesb = sb("onesb", [P, P], BF16)
        best = sb("best", [P, 8, NT])
        seg = sb("seg", [P, 4, E])
        wide = sb("wide", [P, ROUTED * E])
        slot_f = sb("slot_f", [P, 2, NT])
        slot_i = sb("slot_i", [P, 2, NT], I32)
        etab = sb("etab", [P, TILES + 1], I32)
        etab_f = sb("etab_f", [P, ROUTED])
        weight = sb("weight", [P, 2, NT])
        xs = sb("xs", [P, 2, D + 1])
        place = sb("place", [P, 2], I32)
        slot_tab = sb("slot_tab", [P, ROUTED], I32)
        place_i = sb("place_i", [P, ROUTED], I32)
        xh = sb("xh", [P, 2, KC, P], BF16)
        xl = sb("xl", [P, 2, KC, P], BF16)
        NPAIR = SEQ * (SEQ + 1) // 2
        work = sb("work", [P, NPAIR * D])
        sg = work[:, 0:2 * FF].rearrange("p (a n) -> p a n", a=2)
        hh = work[:, 2 * FF:4 * FF].rearrange("p (a n) -> p a n", a=2)
        ysb = work[:, 4 * FF:4 * FF + 2 * D].rearrange("p (a n) -> p a n", a=2)
        hTh = sb("hTh", [P, 2, FC, P], BF16)
        hTl = sb("hTl", [P, 2, FC, P], BF16)
        RING = 4
        gat = sb("gat", [P, RING, 2 * D])

        d_stage = [sem(f"d_stage{m}") for m in range(3)]
        y_out = [sem("y_out_even"), sem("y_out_odd")]
        g_in = [sem(f"g_in{r}") for r in range(RING)]
        PER = ((TILES + 1) // 2, TILES // 2)
        STORED = ((ROUTED + 1) // 2, ROUTED // 2)
        w_lo2 = sem("w_lo2")
        d_b, shared_added, w_hi, w_lo, casts = sem("d_b"), sem("shared_added"), sem("w_hi"), sem("w_lo"), sem("casts")
        (bstat, bvar, bstd, brs, xn_t, xT_ready, logits, r_sub, r_exp, r_step, pick_ready, ranks, slot_ready,
         xn_out, scattered) = [sem(n) for n in (
             "bstat bvar bstd brs bxn_t bxT_ready logits r_sub r_exp r_step pick_ready ranks slot_ready "
             "xn_out scattered").split()]
        (xs_t, xh_ready, xl_ready, gu, sg_ready, h_ready, h_t, hTh_ready, hTl_ready, y_ps, y_ready,
         combined) = [sem(n) for n in (
             "xs_t xh_ready xl_ready gu sg_ready h_ready h_t hTh_ready hTl_ready by_ps by_ready "
             "combined").split()]
        b_mul2, b_prob = sem("b_mul2"), sem("b_prob")
        placed, place_ready = sem("placed"), sem("place_ready")
        second = sem("second")
        xn_ready = [sem(f"bxn_ready{i}") for i in range(3)]
        xs_in = [sem("xs_in_even"), sem("xs_in_odd")]
        (b_qkv, b_q, b_mul, b_sub, b_exp, b_ot, b_oT, b_y, b_x) = [sem(n) for n in (
            "b_qkv b_q b_mul b_sub b_exp b_ot b_oT b_y b_x").split()]
        done = sem("done")

        ident = const(cst, "ident")
        X, G, U, HT, Y, RT = 0, (1, 2), (3, 4), 7, 6, 5
        qkv = stage[:, :, :].rearrange("p a b -> p (a b)").rearrange("p (c s n) -> p c s n", c=2, s=SEQ)
        prod = work[:, :].rearrange("p (a n) -> p a n", a=NPAIR)
        sc = sb("scb", [P, NPAIR, NH])
        sstat = sb("sstat", [P, 3, SEQ, NH])
        block = ctx.enter_context(nc.Block())

        def pair(s, t=0):
            return s * (s + 1) // 2 + t

        def head(a):
            return a.rearrange("p (g n) -> p g n", g=NKV)

        def product_qk(engine, c, s, t):
            q = head(qkv[:, c % 2, s, :])[:, :, 0:64].rearrange("p g (r d) -> p g r d", d=HD)
            k = head(qkv[:, c % 2, t, :])[:, :, 64:80].unsqueeze(2).broadcast_to([P, NKV, 4, HD])
            return engine.tensor_tensor(prod[:, pair(s, t), :].rearrange("p (g r d) -> p g r d", g=NKV, r=4),
                                        q, k, ALU.mult)

        def product_pv(engine, c, s, t):
            vv = head(qkv[:, c % 2, t, :])[:, :, 80:96].unsqueeze(2).broadcast_to([P, NKV, 4, HD])
            pp = sc[:, pair(s, t), :].rearrange("p (g r) -> p g r", g=NKV).unsqueeze(3)\
                .broadcast_to([P, NKV, 4, HD])
            return engine.tensor_tensor(prod[:, pair(s, t), :].rearrange("p (g r d) -> p g r d", g=NKV, r=4),
                                        vv, pp, ALU.mult)

        OB = (4, 2)

        def y_slot(n):
            return bank[6 + n // 2 % 2][:, (n % 2) * D:(n % 2 + 1) * D]

        def tile_b(n):
            return (n % SEQ) * T + n // SEQ

        TURNS = [(0, 0), (0, 1), (0, 2), (0, 3), (1, 0), (1, 1), (1, 2), (2, 0), (1, 3), (2, 1), (2, 2), (2, 3)]

        def nth_turn(which, n):
            return (TURNS.index((which, n // SEQ)) * SEQ + n % SEQ) // 2

        def tile_moe(layer, n):
            return n if layer == 0 else tile_b(n)

        @block.sync
        def _(sp):
            sp.dma_start(wg[:, :, :], wg_d).then_inc(d_b, 16)
            sp.dma_start(wb[:, :, :], wb_d).then_inc(d_b, 16)
            sp.dma_start(pb[:, :, :], pb_d).then_inc(d_b, 16)
            for m in range(3):
                sp.dma_start(stage[:, m, :], we_d[0, m]).then_inc(d_stage[m], 16)
            shared_rows = rows_s.rearrange("(j p) d -> j p d", p=P)
            rows_y = slots_y[SLOTS:SLOTS + 2 * NT * P, :].rearrange("(t p k) d -> t p (k d)", p=P, k=2)
            we_v = we_d.rearrange("e m p n -> (e m) p n")
            assert E == NT // 2
            for layer in range(2):
                first = layer == 0
                for n in range(NT):
                    t = tile_moe(layer, n)
                    sp.wait_ge(xn_ready[2 * layer], n + 1)
                    sp.dma_start(shared_rows[t], xn[:, t, 0:D]).then_inc(xn_out, 16)
                sp.wait_ge(xn_out, (layer + 1) * 16 * NT)

                for par in range(2):
                    if layer:
                        sp.wait_ge(xs_t, layer * TILES)
                    sp.dma_start(xs[:, par, 0:D], shared_rows[par]).then_inc(xs_in[par], 16)

                def weights_of(e):
                    for m in range(3):
                        sp.wait_ge(w_hi, 3 * e - 2 + m)
                        if m == 0:
                            sp.wait_ge(w_lo, e)
                        else:
                            sp.wait_ge(w_lo2, 2 * e - 2 + m)
                        sp.dma_start(stage[:, m, :], we_v[3 * e + m]).then_inc(d_stage[m], 16)

                if first:
                    weights_of(1)
                    with sp.Fori(2, NW) as e:
                        weights_of(e)
                for par in range(2):
                    sp.wait_ge(y_out[par], (layer + 1) * 16 * STORED[par])
                for n in range(NT):
                    if n >= RING:
                        sp.wait_ge(combined, layer * NT + n - RING + 1)
                    elif layer:
                        sp.wait_ge(combined, NT)
                    sp.dma_start(gat[:, n % RING, :], rows_y[tile_b(n) if layer == 0 else n]).then_inc(g_in[n % RING], 16)
            out_v = out_d.rearrange("b (t p) d -> b p t d", p=P)
            for b in range(B):
                sp.wait_ge(combined, NT + (b + 1) * T)
                sp.dma_start(out_v[b], x[:, b * T:(b + 1) * T, :]).then_inc(done, 16)
            sp.wait_ge(done, 16 * B)

        @block.gpsimd
        def _(pool):
            def low_parts(e):
                pool.wait_ge(w_hi, 3 * e + 1)
                pool.tensor_tensor(wl[:, 3 * e, :], stage[:, 0, :], wh[:, 3 * e, :], ALU.subtract).then_inc(w_lo, 1)

            low_parts(0)
            low_parts(1)
            for layer in range(2):
                for e in range(2, NW):
                    if layer == 0:
                        low_parts(e)
                    if e == 2:
                        pool.wait_ge(slot_ready, layer + 1)
                        pool.wait_ge(xn_ready[2 * layer], NT)
                    for i in range(6 * (e - 2), min(6 * (e - 1), 2 * NT)):
                        k, t = i // NT, i % NT
                        if i == NT:
                            pool.wait_ge(scattered, layer * 32 * NT + 16 * NT)
                            pool.tensor_tensor(xn[:, :, D], const(cst, "home")[:, NT:2 * NT], slot_f[:, 1, :],
                                               ALU.subtract).then_inc(second, 1)
                            pool.wait_ge(second, layer + 1)
                        pool.indirect_dma_start(slots_x,
                                                bass.IndirectOffsetOnAxis(ap=slot_i[:, k, t:t + 1], axis=0),
                                                xn[:, t, :], None).then_inc(scattered, 16)

                def place_of(j):
                    pool.wait_ge(placed, layer * ROUTED + j + 1)
                    pool.tensor_tensor(place_i[:, j:j + 1], place[:, j % 2:j % 2 + 1],
                                       slot_tab[:, j:j + 1], ALU.add).then_inc(place_ready, 1)

                def store(j):
                    pool.wait_ge(y_ready, layer * ROUTED + j + 1)
                    pool.wait_ge(place_ready, layer * ROUTED + j + 1)
                    pool.indirect_dma_start(slots_y, bass.IndirectOffsetOnAxis(ap=place_i[:, j:j + 1], axis=0),
                                            ysb[:, j % 2, :], None).then_inc(y_out[j % 2], 16)

                if layer:
                    for par in range(2):
                        pool.wait_ge(y_out[par], 16 * STORED[par])
                place_of(0)
                place_of(1)
                for j in range(ROUTED):
                    if j + 2 < ROUTED:
                        place_of(j + 2)
                    store(j)

                if layer == 0:
                    for c in range(T):
                        pool.wait_ge(b_q, (c + 1) * SEQ)
                        if c:
                            pool.wait_ge(b_ot, c * SEQ // 2)
                        for t in range(SEQ):
                            product_qk(pool, c, SEQ - 1, t).then_inc(b_mul2, 1)
                        pool.wait_ge(b_prob, c * SEQ + 1)
                        for t in range(SEQ):
                            product_pv(pool, c, SEQ - 1, t).then_inc(b_mul2, 1)

        @block.scalar
        def _(act):
            act.activation(trib[:, :], const(cst, "tri"), ACT.Copy).then_inc(casts, 1)
            act.activation(onesb[:, :], const(cst, "ones"), ACT.Copy).then_inc(casts, 1)

            def std(n, cols=slice(0, NT)):
                act.wait_ge(bvar, n + 1)
                act.activation(var[:, cols], var[:, cols], ACT.Sqrt).then_inc(bstd, 1)

            def turned(which, n):
                i = nth_turn(which, n)
                act.wait_ge(xn_t, i + 1)
                act.activation(xT[:, i % 2, :, :, :].rearrange("p t k c -> p (t k c)"), bank[i % 2][:, :], ACT.Copy)\
                   .then_inc(xT_ready, 1)

            shared_rows = rows_s.rearrange("(j p) d -> j p d", p=P)
            rows_x = slots_x.rearrange("(j p) d -> j p d", p=P)

            def moe(layer):
                if layer == 0:
                    std(0)
                for n in range(0 if layer == 0 else NT - SEQ, NT, 2):
                    turned(2 * layer, n)
                n0 = layer * TILES

                def x_high(j, par, routed=False, placing=False):
                    act.wait_ge(xs_t, n0 + j + 1)
                    act.activation(xh[:, par, :, :].rearrange("p k c -> p (k c)"), bank[X][:, 0:D],
                                   ACT.Copy).then_inc(xh_ready, 1)
                    if isinstance(j, int) and j >= NT or placing:
                        if not isinstance(j, int) or j >= NT + 2 or layer:
                            act.wait_ge(place_ready, layer * ROUTED + j - NT - 1)
                        act.activation(place[:, par:par + 1], xs[:, par, D:D + 1], ACT.Copy).then_inc(placed, 1)
                        act.wait_ge(placed, layer * ROUTED + j - NT + 1)
                    if isinstance(j, int) and j + 2 == NT:
                        act.wait_ge(scattered, (layer + 1) * 32 * NT)
                    if not isinstance(j, int) or j + 2 < TILES:
                        if routed:
                            act.dma_start(xs[:, par, :], rows_x[layer * ROUTED + j + 2 - NT]).then_inc(xs_in[par], 16)
                        else:
                            act.dma_start(xs[:, par, 0:D], shared_rows[j + 2]).then_inc(xs_in[par], 16)

                def gates(j, par):
                    act.wait_ge(gu, n0 + j + 1)
                    act.activation(sg[:, par, :], bank[G[par]][:, :], ACT.Silu).then_inc(sg_ready, 1)

                def h_high(j, par):
                    act.wait_ge(h_t, n0 + j + 1)
                    act.activation(hTh[:, par, :, :].rearrange("p c t -> p (c t)"), bank[HT][:, :],
                                   ACT.Copy).then_inc(hTh_ready, 1)

                def rows_out(j, par, nth):
                    act.wait_ge(y_ps, n0 + j + 1)
                    if not isinstance(nth, int) or layer * STORED[par] + nth:
                        act.wait_ge(y_out[par], 16 * (layer * STORED[par] + nth))
                    act.activation(ysb[:, par, :], bank[Y][:, 0:D], ACT.Copy).then_inc(y_ready, 1)

                x_high(0, 0)
                x_high(1, 1)
                act.wait_ge(r_sub, layer + 1)
                act.activation(prob[:, :, :], prob[:, :, :], ACT.Exp).then_inc(r_exp, 1)
                gates(0, 0)
                x_high(2, 0)
                gates(1, 1)
                h_high(0, 0)

                def pair_of_tiles(i, out, routed=True):
                    for par in range(2):
                        j = 2 * i + par
                        x_high(j + 1, 1 - par, isinstance(i, int) and j + 3 >= NT or routed, placing=out)
                        if out:
                            rows_out(j - 2, par, i - 1 - NT // 2)
                        gates(j, par)
                        h_high(j - 1, 1 - par)

                with act.Fori(1, NT // 2 - 2) as i:
                    pair_of_tiles(i, False, routed=False)
                pair_of_tiles(NT // 2 - 2, False, routed=False)
                for i in (NT // 2 - 1, NT // 2):
                    pair_of_tiles(i, False)
                pair_of_tiles(NT // 2 + 1, True)
                with act.Fori(NT // 2 + 2, TILES // 2 - 1) as i:
                    pair_of_tiles(i, True)
                pair_of_tiles(TILES // 2 - 1, True)
                j, last = TILES - 1, ROUTED // 2
                rows_out(j - 2, 0, last - 1)
                gates(j, 0)
                h_high(j - 1, 1)
                rows_out(j - 1, 1, last - 1)
                h_high(j, 0)
                rows_out(j, 0, last)

            def attention_b():
                LN1, LN2 = (1, 2, 3, 5), (4, 6, 7, 8)

                def qkv_rows(c, rows=range(SEQ)):
                    if 0 in rows:
                        for s in range(0, SEQ, 2):
                            turned(1, c * SEQ + s)
                    for s in rows:
                        n = c * SEQ + s
                        act.wait_ge(b_qkv, n + 1)
                        if s == 0 and c >= 2:
                            act.wait_ge(b_mul, 2 * (c - 1) * pair(SEQ - 1))
                            act.wait_ge(b_mul2, 2 * (c - 1) * SEQ)
                        act.activation(qkv[:, c % 2, s, :], bank[2 + n % 2][:, 0:QKVB], ACT.Copy).then_inc(b_q, 1)

                std(LN1[0], slice(0, SEQ))
                qkv_rows(0)
                for c in range(T):
                    if c + 1 < T:
                        std(LN1[c + 1], slice((c + 1) * SEQ, (c + 2) * SEQ))
                        qkv_rows(c + 1, (0, 1))
                    act.wait_ge(b_sub, SEQ * (c + 1))
                    act.activation(sc[:, :, :], sc[:, :, :], ACT.Exp, scale=SCALE_B).then_inc(b_exp, 1)
                    if c + 1 < T:
                        qkv_rows(c + 1, (2, 3))
                    if c:
                        std(LN2[c - 1], slice(NT + (c - 1) * SEQ, NT + c * SEQ))
                    for i in range(c * SEQ // 2, (c + 1) * SEQ // 2):
                        act.wait_ge(b_ot, i + 1)
                        if i >= 2:
                            act.wait_ge(b_y, i - 1)
                        act.activation(oT[:, i % 2, :, :, :].rearrange("p t k c -> p (t k c)"), bank[OB[i % 2]][:, :],
                                       ACT.Copy).then_inc(b_oT, 1)
                    if c:
                        for s in range(0, SEQ, 2):
                            turned(2, (c - 1) * SEQ + s)
                std(LN2[T - 1], slice(NT + (T - 1) * SEQ, NT + T * SEQ))

            moe(0)
            attention_b()
            moe(1)

        @block.vector
        def _(dve):
            steps = [0]

            def signal(ins):
                steps[0] += 1
                ins.then_inc(r_step, 1)

            def step(ins):
                signal(ins)
                dve.wait_ge(r_step, steps[0])

            stats = [0, 0, 0]

            def row_statistics(col, tile):
                stats[0] += 1
                dve.bn_stats(st6[:, col, :], x[:, tile, :]).then_inc(bstat, 1)

            def variances(cols):
                dve.wait_ge(bstat, stats[0])
                for col in cols:
                    stats[0] += 1
                    dve.bn_aggr(mv[:, col, :], st6[:, col, :]).then_inc(bstat, 1)
                dve.wait_ge(bstat, stats[0])
                sl = slice(cols[0], cols[-1] + 1)
                dve.tensor_copy(mean[:, sl], mv[:, sl, 0]).then_inc(brs, 1)
                stats[2] += 1
                dve.tensor_scalar(var[:, sl], mv[:, sl, 1], LN_EPS, None, ALU.add).then_inc(bvar, 1)

            def normalised(cols, tiles, which):
                sl = slice(cols[0], cols[-1] + 1)
                stats[1] += 1
                dve.wait_ge(bstd, stats[1])
                dve.reciprocal(rstd[:, sl], var[:, sl]).then_inc(brs, 1)
                stats[2] += 1
                dve.wait_ge(brs, stats[2])
                for col, tile in zip(cols, tiles):
                    dve.tensor_scalar(xn[:, tile, 0:D], x[:, tile, :], mean[:, col:col + 1], rstd[:, col:col + 1],
                                      ALU.subtract, ALU.mult).then_inc(xn_ready[which], 1)

            lg = bank[RT][:, 0:NT * E].rearrange("p (t e) -> p t e", e=E)
            rk = bank[RT][:, P:P + (NT + 1) * E].rearrange("p (t e) -> p t e", e=E)
            cnt, tiles, base, end = (seg[:, i, :] for i in range(4))
            starts = const(cst, "tilestart")

            def over(a):
                return a.unsqueeze(2).broadcast_to([P, NT, E])

            def router_probabilities(layer):
                dve.wait_ge(logits, layer + 1)
                step(dve.tensor_reduce(best[:, 0, :], lg, AX.X, ALU.max))
                dve.tensor_tensor(prob[:, :, :], lg, over(best[:, 0, :]), ALU.subtract).then_inc(r_sub, 1)
                dve.wait_ge(r_exp, layer + 1)
                step(dve.tensor_reduce(best[:, 1, :], prob[:, :, :], AX.X, ALU.add))
                step(dve.reciprocal(best[:, 2, :], best[:, 1, :]))
                step(dve.tensor_tensor(prob[:, :, :], prob[:, :, :], over(best[:, 2, :]), ALU.mult))
                router_pick(0)
                step(dve.scalar_tensor_tensor(prob[:, :, :], pick[:, 0, :, :], -2.0, prob[:, :, :], ALU.mult, ALU.add))

            def router_pick(k):
                iota = const(cst, "iota8").unsqueeze(1).broadcast_to([P, NT, E])
                step(dve.tensor_reduce(best[:, 3 + k, :], prob[:, :, :], AX.X, ALU.max))
                step(dve.tensor_tensor(eq[:, :, :], prob[:, :, :], over(best[:, 3 + k, :]), ALU.is_equal))
                step(dve.scalar_tensor_tensor(key[:, :, :], eq[:, :, :], float(-E), iota, ALU.mult, ALU.add))
                step(dve.tensor_reduce(best[:, 5, :], key[:, :, :], AX.X, ALU.min))
                step(dve.tensor_tensor(pick[:, k, :, :], key[:, :, :], over(best[:, 5, :]), ALU.is_equal))

            def router_weights(layer):
                router_pick(1)
                dve.tensor_tensor(pickb[:, :, :], pick[:, 0, :, :], pick[:, 1, :, :], ALU.add).then_inc(pick_ready, 1)
                step(dve.tensor_tensor(best[:, 6, :], best[:, 3, :], best[:, 4, :], ALU.add))
                step(dve.reciprocal(best[:, 7, :], best[:, 6, :]))
                for k in range(2):
                    step(dve.tensor_tensor(weight[:, k, :], best[:, 3 + k, :], best[:, 7, :], ALU.mult))

            def router_bases(layer):
                dve.wait_ge(ranks, layer + 1)
                step(dve.tensor_copy(cnt, rk[:, NT, :]))
                wv = wide[:, 0:E * NT].rearrange("p (e j) -> p e j", e=E)
                step(dve.tensor_tensor(wv, cnt.unsqueeze(2).broadcast_to([P, E, NT]),
                                       starts[:, 0:NT].unsqueeze(1).broadcast_to([P, E, NT]), ALU.is_gt))
                step(dve.tensor_reduce(tiles, wv, AX.X, ALU.add))
                bv = wide[:, 0:E * E].rearrange("p (e f) -> p e f", e=E)
                step(dve.tensor_tensor(bv, tiles.unsqueeze(1).broadcast_to([P, E, E]),
                                       const(cst, "tri8").rearrange("p (e f) -> p e f", e=E), ALU.mult))
                step(dve.tensor_reduce(base, bv, AX.X, ALU.add))
                step(dve.tensor_tensor(end, base, tiles, ALU.add))
                step(dve.tensor_scalar(base, base, float(P), None, ALU.mult))
                step(dve.tensor_scalar(end, end, float(P), None, ALU.mult))
                step(dve.tensor_tensor(eq[:, :, :], rk[:, 0:NT, :], base.unsqueeze(1).broadcast_to([P, NT, E]),
                                       ALU.add))

            def router_slots(layer):
                for k in range(2):
                    step(dve.tensor_tensor(key[:, :, :], eq[:, :, :], pick[:, k, :, :], ALU.mult))
                    step(dve.tensor_reduce(slot_f[:, k, :], key[:, :, :], AX.X, ALU.add))
                step(dve.tensor_tensor(xn[:, :, D], const(cst, "home")[:, 0:NT], slot_f[:, 0, :], ALU.subtract))
                tv = wide[:, :].rearrange("p (j e) -> p j e", e=E)
                step(dve.tensor_tensor(tv, starts.unsqueeze(2).broadcast_to([P, ROUTED, E]),
                                       end.unsqueeze(1).broadcast_to([P, ROUTED, E]), ALU.is_ge))
                step(dve.tensor_reduce(etab_f[:, :], tv, AX.X, ALU.add))
                step(dve.tensor_scalar(etab_f[:, :], etab_f[:, :], float(E - 1), 1.0, ALU.min, ALU.add))
                step(dve.tensor_scalar(etab[:, NT:TILES], etab_f[:, :], 3.0, None, ALU.mult))
                dve.tensor_scalar(slot_i[:, :, :], slot_f[:, :, :], float(layer * SLOTS), None, ALU.add)\
                   .then_inc(slot_ready, 1)

            def high_parts(e):
                for m in range(3):
                    dve.wait_ge(d_stage[m], 16 * e + 16)
                    dve.tensor_copy(wh[:, bass.ds(3 * e + m, 1), :], stage[:, m:m + 1, :]).then_inc(w_hi, 1)

            def low_parts(e):
                dve.wait_ge(w_hi, 3 * e + 3)
                for m in (1, 2):
                    dve.tensor_tensor(wl[:, bass.ds(3 * e + m, 1), :], stage[:, m:m + 1, :],
                                      wh[:, bass.ds(3 * e + m, 1), :], ALU.subtract).then_inc(w_lo2, 1)

            def moe(layer):
                if layer == 0:
                    variances(range(NT))
                    normalised(range(NT), range(NT), 0)
                    step(dve.memset(etab[:, 0:NT], 0))
                    step(dve.tensor_copy(slot_tab[:, :], const(cst, "slot")))
                    for e in range(2):
                        high_parts(e)
                        low_parts(e)
                n0 = layer * TILES

                def x_low(j, par):
                    dve.wait_ge(xh_ready, n0 + j + 1)
                    dve.tensor_tensor(xl[:, par, :, :].rearrange("p k c -> p (k c)"), bank[X][:, 0:D],
                                      xh[:, par, :, :].rearrange("p k c -> p (k c)"), ALU.subtract)\
                       .then_inc(xl_ready, 1)

                def hidden(j, par):
                    dve.wait_ge(sg_ready, n0 + j + 1)
                    dve.tensor_tensor(hh[:, par, :], bank[U[par]][:, :], sg[:, par, :], ALU.mult).then_inc(h_ready, 1)

                def h_low(j, par):
                    dve.wait_ge(hTh_ready, n0 + j + 1)
                    dve.tensor_tensor(hTl[:, par, :, :].rearrange("p c t -> p (c t)"), bank[HT][:, :],
                                      hTh[:, par, :, :].rearrange("p c t -> p (c t)"), ALU.subtract)\
                       .then_inc(hTl_ready, 1)

                def add_shared(j):
                    dve.wait_ge(y_ps, n0 + j + 1)
                    if isinstance(j, int):
                        tile, out = x[:, j, :], bank[Y][:, 0:D]
                    else:
                        tile, out = x[:, bass.ds(j, 1), :], bank[Y][:, 0:D].unsqueeze(1)
                    dve.tensor_tensor(tile, out, tile, ALU.add).then_inc(shared_added, 1)

                x_low(0, 0)
                x_low(1, 1)
                router_probabilities(layer)
                hidden(0, 0)
                x_low(2, 0)
                router_weights(layer)
                hidden(1, 1)
                h_low(0, 0)

                def pair_of_tiles(i, splits, shared, routing=False):
                    for par in range(2):
                        j = 2 * i + par
                        if splits:
                            (high_parts, low_parts)[par](i + 1)
                        x_low(j + 1, 1 - par)
                        hidden(j, par)
                        if shared:
                            add_shared(j - 2)
                        h_low(j - 1, 1 - par)
                        if routing:
                            (router_bases, router_slots)[par](layer)

                pair_of_tiles(1, layer == 0, True, routing=True)
                with dve.Fori(2, NT // 2) as i:
                    pair_of_tiles(i, layer == 0, True)
                pair_of_tiles(NT // 2, False, True)
                with dve.Fori(NT // 2 + 1, TILES // 2) as i:
                    pair_of_tiles(i, False, False)
                j = TILES - 1
                hidden(j, 0)
                h_low(j - 1, 1)
                h_low(j, 0)

            def combine(layer, n, t):
                dve.wait_ge(g_in[n % RING], 16 * (layer * (NT // RING) + n // RING + 1))
                for k in range(2):
                    ins = dve.scalar_tensor_tensor(x[:, t, :], gat[:, n % RING, k * D:(k + 1) * D], weight[:, k, t:t + 1],
                                                   x[:, t, :], ALU.mult, ALU.add)
                    if k == 0:
                        step(ins)
                ins.then_inc(combined, 1)

            def attention_b():
                def columns(c, half):
                    return range(half * NT + c * SEQ, half * NT + (c + 1) * SEQ)

                def chunk_tiles(c):
                    return [tile_b(c * SEQ + s) for s in range(SEQ)]

                def combine_chunk(c):
                    for s in range(SEQ):
                        combine(0, c * SEQ + s, tile_b(c * SEQ + s))
                    for s in range(SEQ):
                        dve.wait_ge(combined, c * SEQ + s + 1)
                        row_statistics(c * SEQ + s, tile_b(c * SEQ + s))
                    variances(columns(c, 0))

                def products_qk(c):
                    dve.wait_ge(b_q, (c + 1) * SEQ)
                    if c:
                        dve.wait_ge(b_ot, c * SEQ // 2)
                    for s in range(SEQ - 1):
                        for t in range(s + 1):
                            product_qk(dve, c, s, t).then_inc(b_mul, 1)

                def softmax(c):
                    dve.wait_ge(b_mul, (2 * c + 1) * pair(SEQ - 1))
                    dve.wait_ge(b_mul2, (2 * c + 1) * SEQ)
                    step(dve.tensor_reduce(sc[:, :, :].rearrange("p a h -> p (a h)"),
                                           prod[:, :, :].rearrange("p a (h d) -> p (a h) d", d=HD), AX.X, ALU.add))

                    def own(s):
                        return sc[:, pair(s):pair(s) + s + 1, :]

                    for s in range(SEQ):
                        ins = dve.tensor_reduce(sstat[:, 0, s, :], own(s).rearrange("p a h -> p h a"), AX.X, ALU.max)
                        signal(ins)
                    dve.wait_ge(r_step, steps[0])
                    for s in range(SEQ):
                        dve.tensor_tensor(own(s), own(s), sstat[:, 0, s, :].unsqueeze(1).broadcast_to([P, s + 1, NH]),
                                          ALU.subtract).then_inc(b_sub, 1)
                    dve.wait_ge(b_exp, c + 1)
                    for s in range(SEQ):
                        ins = dve.tensor_reduce(sstat[:, 1, s, :], own(s).rearrange("p a h -> p h a"), AX.X, ALU.add)
                        signal(ins)
                    dve.wait_ge(r_step, steps[0])
                    step(dve.reciprocal(sstat[:, 2, :, :], sstat[:, 1, :, :]))
                    for s in reversed(range(SEQ)):
                        ins = dve.tensor_tensor(own(s), own(s), sstat[:, 2, s, :].unsqueeze(1)
                                                .broadcast_to([P, s + 1, NH]), ALU.mult)
                        ins.then_inc(b_prob, 1)
                    dve.wait_ge(b_prob, (c + 1) * SEQ)

                def products_pv(c):
                    for s in range(SEQ - 1):
                        for t in range(s + 1):
                            product_pv(dve, c, s, t).then_inc(b_mul, 1)

                def output_onto_x(c):
                    for s in range(SEQ):
                        n = c * SEQ + s
                        dve.wait_ge(b_y, n // 2 + 1)
                        dve.tensor_tensor(x[:, s * T + c, :], y_slot(n), x[:, s * T + c, :], ALU.add)\
                           .then_inc(b_x, 1)
                    for s in range(SEQ):
                        dve.wait_ge(b_x, c * SEQ + s + 1)
                        row_statistics(NT + c * SEQ + s, s * T + c)
                    variances(columns(c, 1))

                combine_chunk(0)
                normalised(columns(0, 0), chunk_tiles(0), 1)
                for c in range(T):
                    if c + 1 < T:
                        combine_chunk(c + 1)
                    products_qk(c)
                    if c + 1 < T:
                        normalised(columns(c + 1, 0), chunk_tiles(c + 1), 1)
                    softmax(c)
                    if c:
                        output_onto_x(c - 1)
                    products_pv(c)
                    if c:
                        normalised(columns(c - 1, 1), chunk_tiles(c - 1), 2)
                output_onto_x(T - 1)
                normalised(columns(T - 1, 1), chunk_tiles(T - 1), 2)

            moe(0)
            attention_b()
            moe(1)
            for t in range(NT):
                combine(1, t, t)

        @block.tensor
        def _(pe):
            def mm(out, lhs, rhs, start=True, stop=True):
                return pe.matmul(out, lhs, rhs, start=start, stop=stop, skip_group_check=True)

            def turn(which, n, tiles):
                i = nth_turn(which, n)
                pe.wait_ge(xn_ready[which], n + 2)
                if i >= 2:
                    pe.wait_ge(xT_ready, i - 1)
                for j, tile in enumerate(tiles):
                    for k in range(KC):
                        ins = pe.transpose(bank[i % 2][:, j * D + k * P:j * D + (k + 1) * P],
                                           xn[:, tile, k * P:(k + 1) * P], ident)
                ins.then_inc(xn_t, 1)

            def turns_and_logits(layer, ns):
                def tiles(n):
                    return tile_moe(layer, n), tile_moe(layer, n + 1)

                ns = list(ns)
                turn(2 * layer, ns[0], tiles(ns[0]))
                for n in ns:
                    if n % 2 == 0 and n + 2 <= ns[-1]:
                        turn(2 * layer, n + 2, tiles(n + 2))
                    i = nth_turn(2 * layer, n)
                    pe.wait_ge(xT_ready, i + 1)
                    t = tile_moe(layer, n)
                    for k in range(KC):
                        ins = mm(bank[RT][:, t * E:(t + 1) * E], xT[:, i % 2, n % 2, k, :], wg[:, k, :],
                                 k == 0, k == KC - 1)
                return ins

            pe.wait_ge(d_b, 48)
            pe.wait_ge(casts, 2)

            def moe(layer):
                turns_and_logits(layer, range(NT) if layer == 0 else range(NT - SEQ, NT)).then_inc(logits, 1)

                def rank():
                    pe.wait_ge(pick_ready, layer + 1)
                    mm(bank[RT][:, P:P + NT * E], trib[:, :], pickb[:, :, :].rearrange("p t e -> p (t e)"), True, False)
                    for s in range(1, NT + 1):
                        n = (NT + 1 - s) * E
                        ins = mm(bank[RT][:, P + s * E:P + s * E + n], onesb[:, :],
                                 pickb[:, :, :].rearrange("p t e -> p (t e)")[:, 0:n], False, s == NT)
                    ins.then_inc(ranks, 1)

                n0 = layer * TILES

                def rows_in(j, par, waits=True, nth=None):
                    if waits:
                        pe.wait_ge(xl_ready, n0 + j)
                    pe.wait_ge(xs_in[par], 16 * (layer * PER[par] + (nth if nth is not None else j // 2) + 1))
                    for k in range(KC):
                        ins = pe.transpose(bank[X][:, k * P:(k + 1) * P], xs[:, par, k * P:(k + 1) * P], ident)
                    ins.then_inc(xs_t, 1)

                def weights(e, part, m, k, cols):
                    buf = (wh, wl)[part]
                    if isinstance(e, int):
                        return buf[:, e + m, k * cols:(k + 1) * cols]
                    return buf[:, bass.ds(e + m, 1), k * cols:(k + 1) * cols]

                def gate_up(j, par, e, waits=True):
                    pe.wait_ge(xl_ready, n0 + j + 1)
                    if waits:
                        pe.wait_ge(h_ready, n0 + j - 1)
                    outs = (bank[G[par]][:, :], bank[U[par]][:, :])
                    for k in range(KC):
                        for m in range(2):
                            mm(outs[m], xh[:, par, k, :], weights(e, 0, m, k, FF), k == 0, False)
                            mm(outs[m], xh[:, par, k, :], weights(e, 1, m, k, FF), False, False)
                        for m in range(2):
                            ins = mm(outs[m], xl[:, par, k, :], weights(e, 0, m, k, FF), False, k == KC - 1)
                    ins.then_inc(gu, 1)

                def down(j, par, e, shared=False):
                    pe.wait_ge(hTl_ready, n0 + j + 1)
                    if not isinstance(j, int) or layer or j > 0:
                        if shared or isinstance(j, int) and j == NT:
                            pe.wait_ge(shared_added, layer * NT + j)
                        else:
                            pe.wait_ge(y_ready, layer * ROUTED + j - NT)
                    for c in range(FC):
                        mm(bank[Y][:, 0:D], hTh[:, par, c, :], weights(e, 0, 2, c, D), c == 0, False)
                        mm(bank[Y][:, 0:D], hTh[:, par, c, :], weights(e, 1, 2, c, D), False, False)
                        ins = mm(bank[Y][:, 0:D], hTl[:, par, c, :], weights(e, 0, 2, c, D), False, c == FC - 1)
                    ins.then_inc(y_ps, 1)

                def turn_hidden(j, par):
                    pe.wait_ge(h_ready, n0 + j + 1)
                    for c in range(FC):
                        ins = pe.transpose(bank[HT][:, c * P:(c + 1) * P], hh[:, par, c * P:(c + 1) * P], ident)
                    ins.then_inc(h_t, 1)

                def expert(j):
                    return pe.snap(pe.value_load(etab[0:1, bass.ds(j, 1)], min_val=0, max_val=3 * E))

                rows_in(0, 0, waits=False)
                rows_in(1, 1)
                pe.wait_ge(w_lo, 1)
                pe.wait_ge(w_lo2, 2)
                gate_up(0, 0, 0, waits=False)
                rows_in(2, 0)
                gate_up(1, 1, 0, waits=False)
                rank()
                turn_hidden(0, 0)

                def pair_of_tiles(i, shared, shared_down=False):
                    for par in range(2):
                        j = 2 * i + par
                        rows_in(j + 1, 1 - par, nth=i + par)
                        gate_up(j, par, 0 if shared else expert(j))
                        down(j - 2, par, 0 if shared_down else expert(j - 2), shared_down)
                        turn_hidden(j - 1, 1 - par)

                pair_of_tiles(1, True, True)
                with pe.Fori(2, NT // 2) as i:
                    pair_of_tiles(i, True, True)
                pe.wait_ge(w_lo, NW)
                pe.wait_ge(w_lo2, 2 * NW)
                pe.wait_ge(slot_ready, layer + 1)
                pair_of_tiles(NT // 2, False, True)
                pair_of_tiles(NT // 2 + 1, False)
                with pe.Fori(NT // 2 + 2, TILES // 2) as i:
                    pair_of_tiles(i, False)
                j = TILES - 1
                gate_up(j, 0, expert(j))
                down(j - 2, 0, expert(j - 2))
                turn_hidden(j - 1, 1)
                down(j - 1, 1, expert(j - 1))
                turn_hidden(j, 0)
                down(j, 0, expert(j))

            def attention_b():
                def project(c):
                    for s in range(0, SEQ, 2):
                        turn(1, c * SEQ + s, (tile_b(c * SEQ + s), tile_b(c * SEQ + s + 1)))
                    for s in range(SEQ):
                        n = c * SEQ + s
                        i = nth_turn(1, n)
                        pe.wait_ge(xT_ready, i + 1)
                        if n >= 2:
                            pe.wait_ge(b_q, n - 1)
                        if n % SEQ == 0 and c >= 2:
                            pe.wait_ge(b_oT, (c - 1) * SEQ // 2)
                        for k in range(KC):
                            ins = mm(bank[2 + n % 2][:, 0:QKVB], xT[:, i % 2, n % 2, k, :], wb[:, k, :],
                                     k == 0, k == KC - 1)
                        ins.then_inc(b_qkv, 1)

                project(0)
                for c in range(T):
                    if c + 1 < T:
                        project(c + 1)
                    pairs = range(c * SEQ // 2, (c + 1) * SEQ // 2)
                    for i in pairs:
                        pe.wait_ge(b_mul, (2 * c + 1) * pair(SEQ - 1) + pair(min(2 * i % SEQ + 2, SEQ - 1)))
                        if 2 * i % SEQ + 2 == SEQ:
                            pe.wait_ge(b_mul2, (2 * c + 2) * SEQ)
                        if i >= 2:
                            pe.wait_ge(b_oT, i - 1)
                        if i % 2:
                            pe.wait_ge(b_q, min((c + 2) * SEQ, NT))
                        for j in range(2):
                            s = 2 * i % SEQ + j
                            for k in range(KC):
                                for t in range(s + 1):
                                    ins = mm(bank[OB[i % 2]][:, j * D + k * P:j * D + (k + 1) * P],
                                             prod[:, pair(s, t), k * P:(k + 1) * P], ident, t == 0, t == s)
                        ins.then_inc(b_ot, 1)
                    for i in pairs:
                        pe.wait_ge(b_oT, i + 1)
                        if i >= 2:
                            pe.wait_ge(b_x, 2 * (i - 1))
                        for j in range(2):
                            for k in range(KC):
                                ins = mm(y_slot(2 * i + j), oT[:, i % 2, j, k, :], pb[:, k, :], k == 0, k == KC - 1)
                        ins.then_inc(b_y, 1)
                    if c:
                        turns_and_logits(1, range((c - 1) * SEQ, c * SEQ))

            moe(0)
            attention_b()
            moe(1)


def kernel(**inputs):
    import concourse.bacc as bacc
    from concourse.bass_utils import run_bass_kernel_spmd

    a = {k.replace("L0_", ""): np.asarray(v) for k, v in inputs.items()}
    swap = np.arange(D) ^ 1

    def chunks(m):
        return np.ascontiguousarray(m.reshape(m.shape[0] // P, P, m.shape[1]).transpose(1, 0, 2))

    wq, wk, wv = (a["attn_a_w_qkv"][:, i * D:(i + 1) * D] for i in range(3))
    bq, bk, bv = (a["attn_a_b_qkv"][i * D:(i + 1) * D] for i in range(3))
    wa = chunks(np.concatenate([wk, wk[:, swap], wq, wq[:, swap], wv, a["attn_a_w_gate"], a["attn_a_w_lm_qkv"],
                                a["attn_a_w_lm_out"], a["attn_a_w_l2t_q"], a["attn_a_w_l2t_out"],
                                a["attn_a_w_lm_kv"], a["attn_a_w_out"]], axis=1))
    blm, bkv = a["attn_a_b_lm_qkv"], a["attn_a_b_lm_kv"]
    cols = [bk, bk[swap], bq, bq[swap], blm[0:D], blm[D:2 * D], a["attn_a_b_lm_out"], a["attn_a_b_l2t_q"],
            a["attn_a_b_l2t_out"], bkv[0:D]]
    ba = np.ascontiguousarray(np.concatenate(cols).reshape(B_TOTAL, P).T)
    ra = np.concatenate([bv, a["attn_a_b_gate"], blm[2 * D:], bkv[D:], a["attn_a_b_out"]])
    ra = np.ascontiguousarray(np.broadcast_to(ra, (P, R_TOTAL)))
    pool_q = a["attn_a_pool_q"].reshape(M, H, DH)
    pq = np.zeros((P, KC, HC, M), np.float32)
    for h in range(H):
        pq[DH * (h % HC):DH * (h % HC) + DH, h // HC, h % HC, :] = pool_q[:, h, :].T
    pq = pq.reshape(P, KC, HC * M)

    wb = chunks(a["attn_b_weight_qkv"].T)
    pb = chunks(a["attn_b_weight_proj"].T)
    wg = chunks(a["ffn_wg"].T)
    we = np.stack([np.stack([chunks(g.T).reshape(P, -1), chunks(u.T).reshape(P, -1), chunks(d.T).reshape(P, -1)])
                   for g, u, d in zip(*([a["ffn_sh_" + n]] + list(a["ffn_ex_" + n]) for n in ("gate", "up", "down")))])

    host = {"x": a["attn_a_x"], "const": CONST, "table": TABLE, "wa": wa, "pq": pq, "ba": ba, "ra": ra, "wb": wb, "pb": pb,
            "wg": wg, "we": we}
    nc = bacc.Bacc("TRN2", target_bir_lowering=False, num_devices=1)
    host = {n: np.ascontiguousarray(h) for n, h in host.items()}
    args = [nc.dram_tensor("in_" + n, h.shape, mybir.dt.from_np(h.dtype), kind="ExternalInput").ap()
            for n, h in host.items()]
    out = nc.dram_tensor("out", (B, L, D), F32, kind="ExternalOutput").ap()
    build(nc, *args, out)
    result = run_bass_kernel_spmd(nc, [{"in_" + n: h for n, h in host.items()}], core_ids=[0])
    return result.results[0]["out"]
```
